# Optimizing a Trainium2 kernel written in Bass

```python
import numpy as np
import jax
import jax.numpy as jnp

def _softmax(x, axis=-1):
    return jax.nn.softmax(x, axis=axis)

def _gelu(x):
    return jax.nn.gelu(x, approximate=True)

def _silu(x):
    return jax.nn.silu(x)

def _sigmoid(x):
    return jax.nn.sigmoid(x)

def _layernorm(x, axis=-1, eps=1e-05):
    m = jnp.mean(x, axis=axis, keepdims=True)
    v = jnp.var(x, axis=axis, keepdims=True)
    return (x - m) / jnp.sqrt(v + eps)

def _scatter_add(tgt, idx, src, axis=0):
    return tgt.at[idx].add(src)

def _segment_sum(src, seg, n):
    return jax.ops.segment_sum(src, seg, n)
kernel_name = 'mk_gnn_resnorm_d2_gnn_r8_24be26'

def setup_inputs(seed: int=0):
    np.random.seed(seed)
    _w = jnp.asarray

    def _rec_inputs():
        import jax
        import jax.numpy as jnp
        _gk = jax.random.key(seed)
        x = -0.000202 + 1 * jax.random.normal(jax.random.fold_in(_gk, 1), (12500, 64), jnp.float32)
        _s = jax.random.randint(jax.random.fold_in(_gk, 2), (100000,), 0, 12500, jnp.int32)
        _d = jax.random.randint(jax.random.fold_in(_gk, 3), (100000,), 0, 12500, jnp.int32)
        _loop = jnp.arange(12500, dtype=jnp.int32)
        src = jnp.concatenate([_s, _d, _loop])
        dst = jnp.concatenate([_d, _s, _loop])
        _o = jnp.argsort(dst, stable=True)
        src = src[_o]
        dst = dst[_o]
        edge_attr_16 = -5.3897e-05 + 0.999841 * jax.random.normal(jax.random.fold_in(_gk, 11), (212500, 16), jnp.float32)
        return (x, src, dst, edge_attr_16)
    x, src, dst, edge_attr_16 = _rec_inputs()

    def _L0_gnn_setup():
        import jax, jax.numpy as jnp
        import numpy as np
        N, E, D, ED, H, O = (12500, 200000, 64, 16, 64, 64)
        key = jax.random.key(seed)
        ks = jax.random.split(key, 8)
        fan_in = 2 * D + ED
        s = 1.0 / np.sqrt(fan_in)
        return {'x': jax.random.normal(ks[0], (N, D), dtype=jnp.float32), 'edge_attr': jax.random.normal(ks[1], (E, ED), dtype=jnp.float32), 'edge_index': jax.random.randint(ks[2], (2, E), 0, N, dtype=jnp.int32), 'W1': jax.random.normal(ks[3], (fan_in, H), dtype=jnp.float32) * s, 'b1': jnp.zeros((H,), dtype=jnp.float32), 'W2': jax.random.normal(ks[4], (2 * H + ED, H), dtype=jnp.float32) * s, 'b2': jnp.zeros((H,), dtype=jnp.float32), 'W3': jax.random.normal(ks[5], (2 * H + ED, O), dtype=jnp.float32) * s, 'b3': jnp.zeros((O,), dtype=jnp.float32)}
    _L0_gnn_all = _L0_gnn_setup()
    _L0_gnn_in = {k: v for k, v in _L0_gnn_all.items() if k in ('W1', 'b1', 'W2', 'b2', 'W3', 'b3')}
    del _L0_gnn_all

    def _L1_gnn_setup():
        import jax, jax.numpy as jnp
        import numpy as np
        N, E, F, FE, L = (6250, 100000, 64, 16, 2)
        AVG_DEG_LOG = float(np.log(17.0))
        EPS_STD = 1e-05
        EPS_BN = 1e-05

        def _pna_layer(x, src, dst, edge_attr, We, be, Wp, bp, Wo, bo, Wl, bl, g, b):
            n = x.shape[0]
            e = edge_attr @ We.T + be
            m = jnp.concatenate([x[dst], x[src], e], axis=-1) @ Wp.T + bp
            ones = jnp.ones((m.shape[0],), x.dtype)
            cnt = jax.ops.segment_sum(ones, dst, n)
            ssum = jax.ops.segment_sum(m, dst, n)
            denom = jnp.maximum(cnt, 1.0)[:, None]
            mean = ssum / denom
            mean_sq = jax.ops.segment_sum(m * m, dst, n) / denom
            std = jnp.sqrt(jnp.maximum(mean_sq - mean * mean, 0.0) + EPS_STD)
            mn = jax.ops.segment_min(m, dst, n)
            mn = jnp.where(jnp.isfinite(mn), mn, 0.0)
            mx = jax.ops.segment_max(m, dst, n)
            mx = jnp.where(jnp.isfinite(mx), mx, 0.0)
            agg = jnp.concatenate([mean, mn, mx, std, ssum], axis=-1)
            deg = jnp.maximum(cnt, 1.0)[:, None]
            amp = jnp.log(deg + 1.0) / AVG_DEG_LOG
            att = AVG_DEG_LOG / jnp.log(deg + 1.0)
            out = jnp.concatenate([agg, agg * amp, agg * att], axis=-1)
            out = jnp.concatenate([x, out], axis=-1) @ Wo.T + bo
            out = out @ Wl.T + bl
            mu = out.mean(axis=0)
            var = out.var(axis=0)
            out = (out - mu) / jnp.sqrt(var + EPS_BN) * g + b
            return jax.nn.relu(out)
        key = jax.random.key(seed)
        ks = jax.random.split(key, 13)
        s = 0.05
        return {'x': jax.random.normal(ks[0], (N, F), jnp.float32), 'edge_index': jax.random.randint(ks[1], (2, E), 0, N, dtype=jnp.int32), 'edge_attr': jax.random.normal(ks[2], (E, FE), jnp.float32), 'W_edge': s * jax.random.normal(ks[3], (L, F, FE), jnp.float32), 'b_edge': s * jax.random.normal(ks[4], (L, F), jnp.float32), 'W_pre': s * jax.random.normal(ks[5], (L, F, 3 * F), jnp.float32), 'b_pre': s * jax.random.normal(ks[6], (L, F), jnp.float32), 'W_post': s * jax.random.normal(ks[7], (L, F, 16 * F), jnp.float32), 'b_post': s * jax.random.normal(ks[8], (L, F), jnp.float32), 'W_lin': s * jax.random.normal(ks[9], (L, F, F), jnp.float32), 'b_lin': s * jax.random.normal(ks[10], (L, F), jnp.float32), 'bn_gamma': jnp.ones((L, F), jnp.float32), 'bn_beta': jnp.zeros((L, F), jnp.float32)}
    _L1_gnn_all = _L1_gnn_setup()
    _L1_gnn_in = {k: v for k, v in _L1_gnn_all.items() if k in ('W_edge', 'b_edge', 'W_pre', 'b_pre', 'W_post', 'b_post', 'W_lin', 'b_lin', 'bn_gamma', 'bn_beta')}
    del _L1_gnn_all
    return {'x': x, 'src': src, 'dst': dst, 'edge_attr_16': edge_attr_16, 'L0_gnn_W1': _L0_gnn_in['W1'], 'L0_gnn_b1': _L0_gnn_in['b1'], 'L0_gnn_W2': _L0_gnn_in['W2'], 'L0_gnn_b2': _L0_gnn_in['b2'], 'L0_gnn_W3': _L0_gnn_in['W3'], 'L0_gnn_b3': _L0_gnn_in['b3'], 'L1_gnn_W_edge': _L1_gnn_in['W_edge'], 'L1_gnn_b_edge': _L1_gnn_in['b_edge'], 'L1_gnn_W_pre': _L1_gnn_in['W_pre'], 'L1_gnn_b_pre': _L1_gnn_in['b_pre'], 'L1_gnn_W_post': _L1_gnn_in['W_post'], 'L1_gnn_b_post': _L1_gnn_in['b_post'], 'L1_gnn_W_lin': _L1_gnn_in['W_lin'], 'L1_gnn_b_lin': _L1_gnn_in['b_lin'], 'L1_gnn_bn_gamma': _L1_gnn_in['bn_gamma'], 'L1_gnn_bn_beta': _L1_gnn_in['bn_beta']}

def reference(x, src, dst, edge_attr_16, L0_gnn_W1, L0_gnn_b1, L0_gnn_W2, L0_gnn_b2, L0_gnn_W3, L0_gnn_b3, L1_gnn_W_edge, L1_gnn_b_edge, L1_gnn_W_pre, L1_gnn_b_pre, L1_gnn_W_post, L1_gnn_b_post, L1_gnn_W_lin, L1_gnn_b_lin, L1_gnn_bn_gamma, L1_gnn_bn_beta):
    import jax
    import jax.numpy as jnp

    def _L0_gnn_ref(x, edge_attr, edge_index, W1, b1, W2, b2, W3, b3):
        import jax, jax.numpy as jnp
        import numpy as np
        N, E, D, ED, H, O = (12500, 200000, 64, 16, 64, 64)
        src = edge_index[0]
        dst = edge_index[1]
        n_nodes = x.shape[0]

        def conv(h, W, b):
            m = jnp.concatenate([h[dst], h[src], edge_attr], axis=1) @ W + b
            return jax.ops.segment_sum(m, dst, num_segments=n_nodes)
        h = jax.nn.relu(conv(x, W1, b1))
        h = jax.nn.relu(conv(h, W2, b2))
        return conv(h, W3, b3)

    def _L1_gnn_ref(x, edge_index, edge_attr, W_edge, b_edge, W_pre, b_pre, W_post, b_post, W_lin, b_lin, bn_gamma, bn_beta):
        import jax, jax.numpy as jnp
        import numpy as np
        N, E, F, FE, L = (6250, 100000, 64, 16, 2)
        AVG_DEG_LOG = float(np.log(17.0))
        EPS_STD = 1e-05
        EPS_BN = 1e-05

        def _pna_layer(x, src, dst, edge_attr, We, be, Wp, bp, Wo, bo, Wl, bl, g, b):
            n = x.shape[0]
            e = edge_attr @ We.T + be
            m = jnp.concatenate([x[dst], x[src], e], axis=-1) @ Wp.T + bp
            ones = jnp.ones((m.shape[0],), x.dtype)
            cnt = jax.ops.segment_sum(ones, dst, n)
            ssum = jax.ops.segment_sum(m, dst, n)
            denom = jnp.maximum(cnt, 1.0)[:, None]
            mean = ssum / denom
            mean_sq = jax.ops.segment_sum(m * m, dst, n) / denom
            std = jnp.sqrt(jnp.maximum(mean_sq - mean * mean, 0.0) + EPS_STD)
            mn = jax.ops.segment_min(m, dst, n)
            mn = jnp.where(jnp.isfinite(mn), mn, 0.0)
            mx = jax.ops.segment_max(m, dst, n)
            mx = jnp.where(jnp.isfinite(mx), mx, 0.0)
            agg = jnp.concatenate([mean, mn, mx, std, ssum], axis=-1)
            deg = jnp.maximum(cnt, 1.0)[:, None]
            amp = jnp.log(deg + 1.0) / AVG_DEG_LOG
            att = AVG_DEG_LOG / jnp.log(deg + 1.0)
            out = jnp.concatenate([agg, agg * amp, agg * att], axis=-1)
            out = jnp.concatenate([x, out], axis=-1) @ Wo.T + bo
            out = out @ Wl.T + bl
            mu = out.mean(axis=0)
            var = out.var(axis=0)
            out = (out - mu) / jnp.sqrt(var + EPS_BN) * g + b
            return jax.nn.relu(out)
        src, dst = (edge_index[0], edge_index[1])
        for l in range(L):
            x = _pna_layer(x, src, dst, edge_attr, W_edge[l], b_edge[l], W_pre[l], b_pre[l], W_post[l], b_post[l], W_lin[l], b_lin[l], bn_gamma[l], bn_beta[l])
        return x
    edge_index = jnp.stack([src, dst])
    x = _layernorm(x + _L0_gnn_ref(x, edge_attr_16, edge_index, L0_gnn_W1, L0_gnn_b1, L0_gnn_W2, L0_gnn_b2, L0_gnn_W3, L0_gnn_b3), axis=-1)
    x = _layernorm(x + _L1_gnn_ref(x, edge_index, edge_attr_16, L1_gnn_W_edge, L1_gnn_b_edge, L1_gnn_W_pre, L1_gnn_b_pre, L1_gnn_W_post, L1_gnn_b_post, L1_gnn_W_lin, L1_gnn_b_lin, L1_gnn_bn_gamma, L1_gnn_bn_beta), axis=-1)
    return x

_drawn_inputs = setup_inputs


def setup_inputs(seed=0):
    import zlib

    import numpy as np

    out = dict(_drawn_inputs(seed))
    spreads = {'L0_gnn_b1': (0.0, 0.1),
     'L0_gnn_b2': (0.0, 0.537),
     'L0_gnn_b3': (0.0, 0.8),
     'L1_gnn_bn_gamma': (1.0, 0.2),
     'L1_gnn_bn_beta': (0.0, 0.1)}
    factors = {'L1_gnn_b_edge': 4.025, 'L1_gnn_b_post': 8.0, 'L1_gnn_b_lin': 8.0}
    for name, (base, spread) in spreads.items():
        noise = np.random.default_rng([zlib.crc32(name.encode()), seed]).standard_normal(out[name].shape)
        drawn = base * np.exp(spread * noise) if base else spread * noise
        out[name] = jnp.asarray(drawn.astype(out[name].dtype))
    for name, factor in factors.items():
        out[name] = (out[name] * factor).astype(out[name].dtype)
    return out
```

```python
from contextlib import ExitStack

import numpy as np
import concourse.bass as bass
from concourse import mybir

F32 = mybir.dt.float32
I32 = mybir.dt.int32
I16 = mybir.dt.int16
BF16 = mybir.dt.bfloat16
ALU = mybir.AluOpType
ACT = mybir.ActivationFunctionType
AX_X = mybir.AxisListType.X

N, E, D, FE = 12500, 212500, 64, 16
P = 128
G = 8
H = 2
J = G // H
GE = G * P
SLOTS = 4
NG = -(-E // (GE * SLOTS)) * SLOTS
EP = NG * GE
CH = 512
NCH = -(-N // CH)
NP = NCH * CH
assert N + P <= NP
B = CH // P
KC = D + FE + 1
RESET = -float(2.0 ** 127)
EPS_LN = 1e-5
EPS_STD = 1e-5
EPS_BN = 1e-5
AVG_LOG = float(np.log(17.0))
LAYERS = 2


def gate(eng):
    eng.nop(nofuse=True)


class Chip:

    def __init__(self, nc):
        self.nc = nc
        self.n = 0

    def scope(self, ctx):
        nc = self.nc
        self.n += 1
        tag = f"_{self.n}"
        sb = lambda name, shape, dt=F32: ctx.enter_context(nc.sbuf_tensor(name + tag, shape, dt))
        ps = lambda name, shape, dt=F32: ctx.enter_context(nc.psum_tensor(name + tag, shape, dt))
        sems = []

        def sem(name):
            sems.append(nc.alloc_semaphore(name + tag))
            return sems[-1]

        def close():
            if sems:
                nc.clear_and_free_semaphores(sems)
                nc.all_engine_barrier()

        ctx.callback(close)
        return sb, ps, sem


def prepare(chip, dst_pad, flags):
    nc = chip.nc
    with ExitStack() as ctx:
        sb, ps, sem = chip.scope(ctx)
        cur = sb("cur", [P, NG * G], I32)
        nxt = sb("nxt", [P, NG * G], I32)
        change = sb("change", [P, NG * G])
        start = sb("start", [P, NG * G], BF16)
        rows = sb("rows", [1, 2, NG], I32)
        wf = sb("wf", [1, 4, NG + 1])
        s_tile = sem("s_tile")
        s_lin = sem("s_lin")
        s_rows = sem("s_rows")
        s_flags = sem("s_flags")
        s_v = sem("s_v")
        s_zero = sem("s_zero")
        s_pool = sem("s_pool")
        s_free = sem("s_free")
        block = ctx.enter_context(nc.Block())
        tiles = lambda shift: dst_pad[shift:shift + EP].rearrange("(q p j) -> p q j", p=P, j=J)
        line = lambda shift: dst_pad[shift:shift + EP].rearrange("(p c) -> p c", p=P)
        q3 = lambda t: t[:, :].rearrange("p (q j) -> p q j", j=J)

        @block.sync
        def _(sp):
            heads = dst_pad[1:1 + EP].rearrange("(a g e) -> a g e", a=1, e=GE)
            sp.dma_start(rows[:, 0, :], heads[:, :, 0], allow_slow_non_contiguous=True).then_inc(s_rows, 16)
            sp.dma_start(rows[:, 1, :], heads[:, :, GE - 1], allow_slow_non_contiguous=True).then_inc(s_rows, 16)
            sp.dma_start(q3(cur), tiles(1)).then_inc(s_tile, 16)
            sp.dma_start(q3(nxt), tiles(2)).then_inc(s_tile, 16)
            sp.wait_ge(s_free, 1)
            sp.dma_start(cur[:, :], line(1)).then_inc(s_lin, 16)
            sp.dma_start(nxt[:, :], line(0)).then_inc(s_lin, 16)
            sp.wait_ge(s_v, 12)
            sp.dma_start(flags.rearrange("(p c) -> p c", p=P), start[:, :]).then_inc(s_flags, 16)
            sp.wait_ge(s_flags, 16)

        @block.gpsimd
        def _(pool):
            pool.iota(chip.ramp[:, :], [[1, NP]], base=0, channel_multiplier=0,
                      allow_small_or_imprecise_dtypes=True)
            pool.memset(chip.ident[:, :], 0.0).then_inc(s_zero, 1)
            pool.wait_ge(s_zero, 1)
            pool.affine_select(out=chip.ident[:, :], in_=chip.ident[:, :], compare_op=ALU.not_equal,
                               fill=1.0, base=0, pattern=[[-1, P]], channel_multiplier=1).then_inc(s_pool, 1)

        @block.vector
        def _(v):
            v.wait_ge(s_rows, 32)
            v.tensor_tensor(rows[:, 1, :], rows[:, 1, :], rows[:, 0, :], ALU.subtract).then_inc(s_v, 1)
            v.wait_ge(s_v, 1)
            v.tensor_scalar(rows[:, 1, :], rows[:, 1, :], 7, None, ALU.arith_shift_right).then_inc(s_v, 1)
            v.wait_ge(s_v, 2)
            v.memset(wf[:, 0, 0:1], 1.0)
            v.tensor_scalar(wf[:, 0, 1:], rows[:, 1, :], 1.0, None, ALU.add).then_inc(s_v, 1)
            v.memset(wf[:, 1, :], 1.0).then_inc(s_v, 1)
            v.wait_ge(s_v, 4)
            v.tensor_tensor_scan(wf[:, 2, :], wf[:, 1, :], wf[:, 0, :], 0.0, ALU.mult, ALU.add).then_inc(s_v, 1)
            v.wait_ge(s_v, 5)
            v.tensor_tensor(wf[:, 3, :], wf[:, 2, :], wf[:, 0, :], ALU.subtract).then_inc(s_v, 1)
            v.tensor_copy(chip.regs[:, 0, :], wf[:, 0, :])
            v.memset(chip.regs[:, 2, 0:1], N)
            v.tensor_copy(chip.regs[:, 2, 1:], rows[:, 0, :])
            v.wait_ge(s_v, 6)
            v.tensor_copy(chip.regs[:, 1, :], wf[:, 3, :]).then_inc(s_v, 1)
            v.wait_ge(s_tile, 32)
            dst2 = chip.dst[:, 1:, :].rearrange("p g j -> p (g j)")
            last2 = chip.last[:, 1:, :].rearrange("p g j -> p (g j)")
            v.memset(chip.dst[:, 0, :], -1.0)
            v.memset(chip.last[:, 0, :], -1.0)
            v.tensor_copy(dst2, cur[:, :])
            v.tensor_tensor(change[:, :], cur[:, :], nxt[:, :], ALU.not_equal).then_inc(s_v, 1)
            v.wait_ge(s_v, 8)
            v.scalar_tensor_tensor(out=last2, in0=dst2, scalar=1.0, in1=change[:, :],
                                   op0=ALU.add, op1=ALU.mult).then_inc(s_v, 1)
            v.wait_ge(s_v, 9)
            v.tensor_scalar(last2, last2, -1.0, None, ALU.add).then_inc(s_v, 1)
            v.wait_ge(s_v, 10)
            v.memset(rows[:, 1, 0:1], 0).then_inc(s_free, 1)
            v.wait_ge(s_lin, 32)
            v.tensor_tensor(change[:, :], cur[:, :], nxt[:, :], ALU.not_equal).then_inc(s_v, 1)
            v.wait_ge(s_v, 11)
            v.tensor_scalar(start[:, :], change[:, :], RESET, None, ALU.mult).then_inc(s_v, 1)


def edge_views(src_pad, g):
    return src_pad[bass.ds(g * GE, GE)].rearrange("(h p j) -> p h j", h=H, p=P)


def sum_pass(chip, table, src_pad, ea_pad, first):
    nc = chip.nc
    acc = chip.acc
    M = KC if first else D
    with ExitStack() as ctx:
        sb, ps, sem = chip.scope(ctx)
        idx = sb("idx", [P, SLOTS, G], I32)
        data = sb("data", [P, SLOTS, G, KC])
        onehot = sb("onehot", [P, G, P])
        scratch = sb("scratch", [1, SLOTS])
        part = ps("part", [P, CH])
        s_free = [sem(f"s_free{r}") for r in range(SLOTS)]
        s_idx = [sem(f"s_idx{r}") for r in range(SLOTS)]
        s_ea = [sem(f"s_ea{r}") for r in range(SLOTS)]
        s_row = [sem(f"s_row{r}") for r in range(SLOTS)]
        s_hot = sem("s_hot")
        s_part = sem("s_part")
        s_added = sem("s_added")
        block = ctx.enter_context(nc.Block())

        @block.sync
        def _(sp):
            with sp.Fori(0, NG // SLOTS) as k:
                for r in range(SLOTS):
                    g = k * SLOTS + r
                    sp.wait_ge(s_free[r], k + 1)
                    sp.dma_start(idx[:, r, :].rearrange("p (h j) -> p h j", h=H),
                                 edge_views(src_pad, g)).then_inc(s_idx[r], 16)
                    if first:
                        for h in range(H):
                            sp.dma_start(data[:, r, J * h:J * h + J, D:D + FE],
                                         ea_pad[bass.ds(g * GE + h * J * P, J * P), :]
                                         .rearrange("(p j) f -> p j f", p=P)).then_inc(s_ea[r], 16)

        @block.gpsimd
        def _(pool):
            with pool.Fori(0, NG // SLOTS) as k:
                for r in range(SLOTS):
                    pool.wait_ge(s_idx[r], k * 16 + 16)
                    gate(pool)
                    for j in range(G):
                        pool.indirect_dma_start(
                            out=data[:, r, j, 0:D], out_offset=None, in_=table[:, :],
                            in_offset=bass.IndirectOffsetOnAxis(ap=idx[:, r, j:j + 1], axis=0),
                        ).then_inc(s_row[r], 16)

        @block.tensor
        def _(pe):
            with pe.Fori(0, NG // SLOTS) as k:
                for r in range(SLOTS):
                    g = k * SLOTS + r
                    windows = pe.value_load(chip.regs[0:1, 0, bass.ds(g + 1, 1)], min_val=1, max_val=NP // P)
                    before = pe.value_load(chip.regs[0:1, 1, bass.ds(g + 1, 1)], min_val=1, max_val=NG * NP // P)
                    pe.wait_ge(s_row[r], k * 16 * G + 16 * G)
                    if first:
                        pe.wait_ge(s_ea[r], k * 16 * H + 16 * H)
                    gate(pe)
                    with pe.Fori(0, windows) as w:
                        pe.wait_ge(s_hot, before + w)
                        pe.wait_ge(s_added, before + w)
                        gate(pe)
                        for j in range(G):
                            mm = pe.matmul(part[0:M, 0:P], data[:, r, j, 0:M], onehot[:, j, :],
                                           start=(j == 0), stop=(j == G - 1))
                        mm.then_inc(s_part, 1)

        @block.vector
        def _(v):
            v.memset(data[:, :, :, KC - 1:KC], 1.0)
            v.memset(acc[0:M, :], 0.0).then_inc(s_added, 1)
            for r in range(SLOTS):
                v.memset(scratch[:, r:r + 1], 0.0).then_inc(s_free[r], 1)
            with v.Fori(0, NG // SLOTS) as k:
                for r in range(SLOTS):
                    g = k * SLOTS + r
                    windows = v.value_load(chip.regs[0:1, 0, bass.ds(g + 1, 1)], min_val=1, max_val=NP // P)
                    before = v.value_load(chip.regs[0:1, 1, bass.ds(g + 1, 1)], min_val=1, max_val=NG * NP // P)
                    base = v.value_load(chip.regs[0:1, 2, bass.ds(g + 1, 1)], min_val=0, max_val=N)
                    with v.Fori(0, windows) as w:
                        at = v.snap((base + w * P).with_bounds(min_val=0, max_val=NP - P))
                        for j in range(G):
                            ins = v.tensor_scalar(onehot[:, j, :], chip.ramp[:, bass.ds(at, P)],
                                                  chip.dst[:, bass.ds(g + 1, 1), j], None, ALU.is_equal)
                        ins.then_inc(s_hot, 1)
                        v.wait_ge(s_part, before + w)
                        v.wait_ge(s_added, before + w)
                        v.tensor_tensor(acc[0:M, bass.ds(at, P)], acc[0:M, bass.ds(at, P)],
                                        part[0:M, 0:P], ALU.add).then_inc(s_added, 1)
                    v.memset(scratch[:, r:r + 1], 0.0).then_inc(s_free[r], 1)


def by_pairs(eng, body):
    with eng.Fori(0, NCH // 2) as k:
        body(k * 2, k, (0, 1))
    if NCH % 2:
        body(NCH - 1, NCH // 2, (0,))


def rows_of(t, c):
    return t[bass.ds(c * CH, CH), :].rearrange("(b p) f -> p b f", p=P)


def conv_nodes(chip, h_rows, W, bias, out_rows, relu):
    nc = chip.nc
    acc = chip.acc
    with ExitStack() as ctx:
        sb, ps, sem = chip.scope(ctx)
        wa = sb("wa", [D, D])
        wsum = sb("wsum", [KC, D])
        pick = sb("pick", [KC, D])
        picked = sb("picked", [1, D])
        hin = sb("hin", [P, 2, B, D])
        ht = sb("ht", [D, 2, CH])
        hc = sb("hc", [D, 2, CH])
        ot = sb("ot", [D, 2, CH])
        stage = sb("stage", [P, 2, B, D])
        p_h = ps("p_h", [P, 2, CH])
        p_cnt = ps("p_cnt", [P, 2, CH])
        p_out = ps("p_out", [P, 2, CH])
        s_w = sem("s_w")
        s_pick0 = sem("s_pick0")
        s_pick1 = sem("s_pick1")
        s_pick = sem("s_pick")
        s_in = [sem(f"s_in{i}") for i in (0, 1)]
        s_turn = sem("s_turn")
        s_ht = sem("s_ht")
        s_hc = sem("s_hc")
        s_sum = sem("s_sum")
        s_ot = sem("s_ot")
        s_back = sem("s_back")
        s_end = sem("s_end")
        s_out = [sem(f"s_out{i}") for i in (0, 1)]
        block = ctx.enter_context(nc.Block())

        @block.sync
        def _(sp):
            sp.dma_start(wa[:, :], W[0:D, :]).then_inc(s_w, 16)
            sp.dma_start(wsum[0:D + FE, :], W[D:, :]).then_inc(s_w, 16)
            sp.dma_start(wsum[KC - 1:KC, :], bias.rearrange("(a f) -> a f", a=1)).then_inc(s_w, 16)
            sp.wait_ge(s_pick0, 2)
            sp.dma_start(pick[KC - 1:KC, :], picked[:, :]).then_inc(s_pick, 16)

            def body(c, k, pars):
                for i in pars:
                    sp.wait_ge(s_end, c + 1)
                    sp.dma_start(hin[:, i], rows_of(h_rows, c + i)).then_inc(s_in[i], 16)
                for i in pars:
                    sp.wait_ge(s_end, c + i + 2)
                    sp.dma_start(rows_of(out_rows, c + i), stage[:, i]).then_inc(s_out[i], 16)

            by_pairs(sp, body)
            for i in (0, 1):
                sp.wait_ge(s_out[i], 16 + 16 * ((NCH + 1 - i) // 2))

        @block.tensor
        def _(pe):
            pe.wait_ge(s_w, 48)
            pe.wait_ge(s_pick, 16)

            def body(c, k, pars):
                for i in pars:
                    pe.wait_ge(s_in[i], k * 16 + 16)
                    gate(pe)
                    for b in range(B):
                        pe.transpose(p_h[0:D, i, b * P:(b + 1) * P], hin[:, i, b, :], chip.ident[:, :])
                    pe.matmul(p_cnt[0:D, i, :], pick[:, :], acc[0:KC, bass.ds((c + i) * CH, CH)],
                              start=True, stop=True).then_inc(s_turn, 1)
                for i in pars:
                    pe.wait_ge(s_hc, c + i + 1)
                    gate(pe)
                    pe.matmul(p_out[0:D, i, :], wsum[:, :], acc[0:KC, bass.ds((c + i) * CH, CH)],
                              start=True, stop=False)
                    pe.matmul(p_out[0:D, i, :], wa[:, :], hc[:, i, :], start=False, stop=True).then_inc(s_sum, 1)
                for i in pars:
                    pe.wait_ge(s_ot, c + i + 1)
                    gate(pe)
                    for b in range(B):
                        t = pe.transpose(p_h[:, i, b * D:(b + 1) * D], ot[:, i, b * P:(b + 1) * P],
                                         chip.ident[0:D, 0:D])
                    t.then_inc(s_back, 1)

            by_pairs(pe, body)

        @block.scalar
        def _(act):
            def body(c, k, pars):
                for i in pars:
                    act.wait_ge(s_turn, c + i + 1)
                    nc.scalar.copy(ht[:, i, :], p_h[0:D, i, :]).then_inc(s_ht, 1)
                for i in pars:
                    act.wait_ge(s_sum, c + i + 1)
                    nc.scalar.activation(ot[:, i, :], p_out[0:D, i, :],
                                         ACT.Relu if relu else ACT.Copy).then_inc(s_ot, 1)

            by_pairs(act, body)

        @block.vector
        def _(v):
            v.memset(pick[:, :], 0.0).then_inc(s_pick0, 1)
            v.memset(picked[:, :], 1.0).then_inc(s_pick0, 1)
            v.memset(stage[:, :, :, :], 0.0).then_inc(s_pick1, 1)
            v.wait_ge(s_pick1, 1)
            for i in (0, 1):
                v.memset(stage[0:1, i, 0, 0:1], 0.0).then_inc(s_out[i], 16)
            v.memset(stage[0:1, 0, 1, 0:1], 0.0).then_inc(s_end, 1)

            def body(c, k, pars):
                for i in pars:
                    v.wait_ge(s_ht, c + i + 1)
                    v.tensor_tensor(hc[:, i, :], ht[:, i, :], p_cnt[0:D, i, :], ALU.mult).then_inc(s_hc, 1)
                for i in pars:
                    v.wait_ge(s_back, c + i + 1)
                    v.wait_ge(s_out[i], k * 16 + 16)
                    v.tensor_copy(stage[:, i, :, :],
                                  p_h[:, i, 0:B * D].rearrange("p (b f) -> p b f", b=B)).then_inc(s_end, 1)

            by_pairs(v, body)


def residual_norm(chip, a_rows, b_rows, out_rows):
    nc = chip.nc
    R = NP // P
    PIECES = 4
    W = R // PIECES
    with ExitStack() as ctx:
        sb, ps, sem = chip.scope(ctx)
        a = sb("a", [P, PIECES, W, D])
        b = sb("b", [P, PIECES, W, D])
        sq = sb("sq", [P, W, D])
        mean = sb("mean", [P, PIECES, W])
        var = sb("var", [P, PIECES, W])
        eps = sb("eps", [P, 1])
        s_a = [sem(f"s_a{n}") for n in range(PIECES)]
        s_v = sem("s_v")
        s_sd = sem("s_sd")
        s_var = sem("s_var")
        s_norm = sem("s_norm")
        s_out = sem("s_out")
        block = ctx.enter_context(nc.Block())
        view = lambda t: t.rearrange("(p q w) f -> q p (w f)", p=P, w=W)
        flat = lambda t, n: t[:, n].rearrange("p w f -> p (w f)")

        @block.sync
        def _(sp):
            for n in range(PIECES):
                sp.dma_start(flat(a, n), view(a_rows)[n]).then_inc(s_a[n], 16)
                sp.dma_start(flat(b, n), view(b_rows)[n]).then_inc(s_a[n], 16)
            for n in range(PIECES):
                sp.wait_ge(s_norm, n + 1)
                sp.dma_start(view(out_rows)[n], flat(b, n)).then_inc(s_out, 16)
            sp.wait_ge(s_out, 16 * PIECES)

        @block.scalar
        def _(act):
            for n in range(PIECES):
                act.wait_ge(s_var, n + 1)
                nc.scalar.activation(var[:, n, :], var[:, n, :], ACT.Sqrt, bias=eps[:, 0:1],
                                     scale=1.0 / D).then_inc(s_sd, 1)

        @block.vector
        def _(v):
            steps = [0]

            def then(ins):
                steps[0] += 1
                ins.then_inc(s_v, 1)
                v.wait_ge(s_v, steps[0])

            then(v.memset(eps[:, :], EPS_LN))

            def finish(n):
                v.wait_ge(s_sd, n + 1)
                then(v.reciprocal(var[:, n, :], var[:, n, :]))
                r3 = var[:, n, :].unsqueeze(2).broadcast_to([P, W, D])
                v.tensor_tensor(b[:, n], a[:, n], r3, ALU.mult).then_inc(s_norm, 1)

            for n in range(PIECES):
                v.wait_ge(s_a[n], 32)
                then(v.tensor_tensor(a[:, n], a[:, n], b[:, n], ALU.add))
                then(v.tensor_reduce(mean[:, n, :], a[:, n], AX_X, ALU.add))
                then(v.tensor_scalar(mean[:, n, :], mean[:, n, :], 1.0 / D, None, ALU.mult))
                m3 = mean[:, n, :].unsqueeze(2).broadcast_to([P, W, D])
                then(v.tensor_tensor(a[:, n], a[:, n], m3, ALU.subtract))
                then(v.tensor_tensor(sq[:, :, :], a[:, n], a[:, n], ALU.mult))
                v.tensor_reduce(var[:, n, :], sq[:, :, :], AX_X, ALU.add).then_inc(s_var, 1)
                if n:
                    finish(n - 1)
            finish(PIECES - 1)


class PnaWeights:

    def __init__(self, sb):
        self.edge = sb("w_edge_feat", [FE, D])
        self.node = sb("w_node", [D, 2 * D])
        self.node_bias = sb("w_node_bias", [P, 1])
        self.source = sb("w_source", [D, D])
        self.wide = sb("w_wide", [P, 3, P])
        self.wide_x = sb("w_wide_x", [D, P])
        self.att = sb("w_att", [P, 3, D])
        self.lin = sb("w_lin", [P, D])
        self.post_bias = sb("w_post_bias", [D, 1])
        self.lin_bias = sb("w_lin_bias", [D, 1])
        self.gamma = sb("w_gamma", [D, 1])
        self.beta = sb("w_beta", [D, 1])


def pna_weights(chip, w, layer, We, be, Wp, bp, Wo, bo, Wl, bl, bn_g, bn_b):
    nc = chip.nc
    AGG = 5 * D
    with ExitStack() as ctx:
        sb, ps, sem = chip.scope(ctx)
        wp = sb("wp", [D, 3 * D])
        wo = sb("wo", [D, 16 * D])
        wl = sb("wl", [D, 2 * D])
        we = sb("we", [D, FE])
        be_c = sb("be_c", [D, 1])
        bp_c = sb("bp_c", [P, 1])
        embed = sb("embed", [D, 2 * D])
        p_t = ps("p_t", [P, 2, 8, D])
        p_e = ps("p_e", [P, CH])
        s_w = sem("s_w")
        s_t = sem("s_t")
        s_embed = sem("s_embed")
        s_fold = sem("s_fold")
        s_zero = sem("s_zero")
        block = ctx.enter_context(nc.Block())
        col = lambda t: t[layer].rearrange("(f a) -> f a", a=1)

        @block.sync
        def _(sp):
            blocks = lambda t: t.rearrange("f (b c) -> f b c", c=D)
            moved = [(blocks(wo[:, :])[:, to:16:5, :], blocks(Wo[layer])[:, of:16:5, :])
                     for to, of in ((1, 1), (2, 3), (3, 2), (4, 4), (5, 5))]
            loads = [(wp[:, :], Wp[layer]), (wo[:, 0:D], Wo[layer][:, 0:D]), *moved, (wl[:, 0:D], Wl[layer]),
                     (wl[:, D:], Wl[layer]), (we[:, :], We[layer]), (be_c[:, :], col(be)),
                     (bp_c[0:D, :], col(bp)), (bp_c[D:, :], col(bp)), (w.post_bias[:, :], col(bo)),
                     (w.lin_bias[:, :], col(bl)), (w.gamma[:, :], col(bn_g)), (w.beta[:, :], col(bn_b))]
            for to, of in loads:
                sp.dma_start(to, of).then_inc(s_w, 16)
            sp.wait_ge(s_w, 16 * len(loads))

        cuts = [(wp, 0, D), (wp, D, D), (wp, 2 * D, D), (wo, 0, D), (wl, 0, 2 * D)]
        for k in range(3):
            cuts += [(wo, D + k * AGG, 2 * D), (wo, 3 * D + k * AGG, 2 * D), (wo, 5 * D + k * AGG, D)]
        turned = lambda n, rows: p_t[rows, n // 8, n % 8, :]
        low, high, both = slice(0, D), slice(D, P), slice(0, P)

        @block.tensor
        def _(pe):
            pe.wait_ge(s_w, 16 * 17)
            for n, (t, at, m) in enumerate(cuts):
                last = pe.transpose(turned(n, slice(0, m)), t[:, at:at + m], chip.ident[0:D, 0:D])
            last.then_inc(s_t, 1)
            pe.wait_ge(s_embed, 1)
            pe.matmul(p_e[0:FE, 0:D], we[:, :], embed[:, 0:D], start=True, stop=True)
            pe.matmul(p_e[:, D:D + 1], embed[:, :], be_c[:, :], start=True, stop=True).then_inc(s_fold, 1)

        @block.scalar
        def _(act):
            act.wait_ge(s_t, 1)
            nc.scalar.copy(embed[:, D:], turned(2, low))
            nc.scalar.copy(embed[:, 0:D], turned(2, low)).then_inc(s_embed, 1)
            nc.scalar.copy(w.node[:, 0:D], turned(0, low))
            nc.scalar.copy(w.node[:, D:], turned(0, low))
            nc.scalar.copy(w.source[:, :], turned(1, low))
            nc.scalar.copy(w.lin[:, :], turned(4, both))
            act.wait_ge(s_zero, 1)
            nc.scalar.copy(w.wide_x[:, 0:D], turned(3, low))
            for k in range(3):
                pair = lambda i: (w.wide[:, i, k * D:k * D + D] if k < 2 else w.att[:, i, :])
                nc.scalar.copy(pair(0), turned(5 + 3 * k, both))
                nc.scalar.mul(pair(1)[low], turned(6 + 3 * k, low), -1.0)
                nc.scalar.copy(pair(1)[high], turned(6 + 3 * k, high))
                nc.scalar.copy(pair(2)[low], turned(7 + 3 * k, low))
            act.wait_ge(s_fold, 1)
            nc.scalar.copy(w.edge[:, :], p_e[0:FE, 0:D])
            nc.scalar.activation(w.node_bias[:, :], p_e[:, D:D + 1], ACT.Identity, bias=bp_c[:, 0:1])

        @block.vector
        def _(v):
            v.memset(w.wide_x[:, D:], 0.0).then_inc(s_zero, 1)


def source_table(chip, w, x_rows, q_rows):
    nc = chip.nc
    with ExitStack() as ctx:
        sb, ps, sem = chip.scope(ctx)
        xin = sb("xin", [P, 2, B, D])
        xt = sb("xt", [D, 2, CH])
        stage = sb("stage", [P, 2, B, D])
        p_x = ps("p_x", [D, 2, CH])
        p_q = ps("p_q", [P, 2, CH])
        s_in = [sem(f"s_in{i}") for i in (0, 1)]
        s_turn = sem("s_turn")
        s_xt = sem("s_xt")
        s_q = sem("s_q")
        s_end = sem("s_end")
        s_out = [sem(f"s_out{i}") for i in (0, 1)]
        block = ctx.enter_context(nc.Block())

        @block.sync
        def _(sp):
            def body(c, k, pars):
                for i in pars:
                    sp.wait_ge(s_end, c + 1)
                    sp.dma_start(xin[:, i], rows_of(x_rows, c + i)).then_inc(s_in[i], 16)
                for i in pars:
                    sp.wait_ge(s_end, c + i + 2)
                    sp.dma_start(rows_of(q_rows, c + i), stage[:, i]).then_inc(s_out[i], 16)

            by_pairs(sp, body)
            for i in (0, 1):
                sp.wait_ge(s_out[i], 16 + 16 * ((NCH + 1 - i) // 2))

        @block.tensor
        def _(pe):
            def body(c, k, pars):
                for i in pars:
                    pe.wait_ge(s_in[i], k * 16 + 16)
                    gate(pe)
                    for b in range(B):
                        t = pe.transpose(p_x[:, i, b * P:(b + 1) * P], xin[:, i, b, :], chip.ident[:, :])
                    t.then_inc(s_turn, 1)
                for i in pars:
                    pe.wait_ge(s_xt, c + i + 1)
                    gate(pe)
                    for b in range(B):
                        m = pe.matmul(p_q[:, i, b * D:(b + 1) * D], xt[:, i, b * P:(b + 1) * P], w.source[:, :],
                                      start=True, stop=True)
                    m.then_inc(s_q, 1)

            by_pairs(pe, body)

        @block.scalar
        def _(act):
            def body(c, k, pars):
                for i in pars:
                    act.wait_ge(s_turn, c + i + 1)
                    nc.scalar.copy(xt[:, i, :], p_x[:, i, :]).then_inc(s_xt, 1)

            by_pairs(act, body)

        @block.vector
        def _(v):
            for i in (0, 1):
                v.memset(stage[0:1, i, 0, 0:1], 0.0).then_inc(s_out[i], 16)
            v.memset(stage[0:1, 0, 1, 0:1], 0.0).then_inc(s_end, 1)

            def body(c, k, pars):
                for i in pars:
                    v.wait_ge(s_q, c + i + 1)
                    v.wait_ge(s_out[i], k * 16 + 16)
                    v.tensor_copy(stage[:, i, :, :],
                                  p_q[:, i, 0:B * D].rearrange("p (b f) -> p b f", b=B)).then_inc(s_end, 1)

            by_pairs(v, body)


def pna_pass(chip, w, q_rows, src_pad, ea_t, flags):
    nc = chip.nc
    acc = chip.acc2
    with ExitStack() as ctx:
        sb, ps, sem = chip.scope(ctx)
        idx = sb("idx", [P, SLOTS, G], I32)
        data = sb("data", [P, SLOTS, G, D])
        feat = sb("feat", [FE, 2, GE])
        flag = sb("flag", [1, 2, GE], BF16)
        ones = sb("ones", [1, P], BF16)
        t3 = sb("t3", [P, 2, G, 3, D])
        reset = sb("reset", [P, H, CH], BF16)
        run = sb("run", [P, 2, GE])
        back = sb("back", [P, G, P])
        hot = sb("hot", [P, 2, G, P])
        scratch = sb("scratch", [1, 4 + SLOTS])
        p_feat = ps("p_feat", [P, CH])
        p_flag = ps("p_flag", [P, CH])
        p_turn = ps("p_turn", [P, H, CH])
        p_back = ps("p_back", [P, H, CH])
        part = ps("part", [P, CH])
        s_free = [sem(f"s_free{r}") for r in range(SLOTS)]
        s_idx = [sem(f"s_idx{r}") for r in range(SLOTS)]
        s_edge = [sem(f"s_edge{i}") for i in (0, 1)]
        s_row = [sem(f"s_row{r}") for r in range(SLOTS)]
        s_ready = sem("s_ready")
        s_feat = sem("s_feat")
        s_t = sem("s_t")
        s_flag = sem("s_flag")
        s_reset = sem("s_reset")
        s_split = sem("s_split")
        s_run = sem("s_run")
        s_back = sem("s_back")
        s_bcopy = sem("s_bcopy")
        s_hot = sem("s_hot")
        s_part = sem("s_part")
        s_added = sem("s_added")
        block = ctx.enter_context(nc.Block())
        HOTS = 3

        @block.sync
        def _(sp):
            with sp.Fori(0, NG // SLOTS) as k:
                for r in range(SLOTS):
                    g = k * SLOTS + r
                    sp.wait_ge(s_free[r], k + 1)
                    sp.dma_start(idx[:, r, :].rearrange("p (h j) -> p h j", h=H),
                                 edge_views(src_pad, g)).then_inc(s_idx[r], 16)
                    sp.wait_ge(s_flag, g * 2 + 2)
                    sp.dma_start(feat[:, r % 2, :], ea_t[:, bass.ds(g * GE, GE)]).then_inc(s_edge[r % 2], 16)
                    sp.dma_start(flag[:, r % 2, :], flags[bass.ds(g * GE, GE)].rearrange("(a e) -> a e", a=1))\
                      .then_inc(s_edge[r % 2], 16)

        @block.gpsimd
        def _(pool):
            with pool.Fori(0, NG // SLOTS) as k:
                for r in range(SLOTS):
                    pool.wait_ge(s_idx[r], k * 16 + 16)
                    gate(pool)
                    for j in range(G):
                        pool.indirect_dma_start(
                            out=data[:, r, j, :], out_offset=None, in_=q_rows[:, :],
                            in_offset=bass.IndirectOffsetOnAxis(ap=idx[:, r, j:j + 1], axis=0),
                        ).then_inc(s_row[r], 16)

        @block.tensor
        def _(pe):
            def windows_of(e, par):
                pe.wait_ge(s_run, e * 2 + 2)
                pe.wait_ge(s_bcopy, e + 1)
                gate(pe)
                for h in range(H):
                    for j in range(J):
                        b = pe.transpose(p_back[:, h, j * P:(j + 1) * P],
                                         run[:, par, h * CH + j:(h + 1) * CH:J], chip.ident[:, :])
                b.then_inc(s_back, 1)
                windows = pe.value_load(chip.regs[0:1, 0, bass.ds(e, 1)], min_val=1, max_val=NP // P)
                before = pe.value_load(chip.regs[0:1, 1, bass.ds(e, 1)], min_val=0, max_val=NG * NP // P)
                with pe.Fori(0, windows) as n:
                    pe.wait_ge(s_hot, (before + n) * HOTS + 1)
                    pe.wait_ge(s_added, before + n + 1)
                    gate(pe)
                    for j in range(G):
                        pe.matmul(part[:, 0:P], t3[:, par, j, 1:3, :].rearrange("p b f -> p (b f)"),
                                  hot[:, 0, j, :], start=(j == 0), stop=(j == G - 1))
                    pe.wait_ge(s_bcopy, e + 2)
                    for h in range(H):
                        pe.wait_ge(s_hot, (before + n) * HOTS + 2 + h)
                        gate(pe)
                        for j in range(J * h, J * h + J):
                            m = pe.matmul(part[:, P:2 * P], back[:, j, :], hot[:, 1, j, :],
                                          start=(j == 0), stop=(j == G - 1))
                    m.then_inc(s_part, 1)

            pe.wait_ge(s_ready, 1)
            with pe.Fori(0, NG // SLOTS) as k:
                for r in range(SLOTS):
                    g = k * SLOTS + r
                    pe.wait_ge(s_edge[r % 2], k * (32 * SLOTS // 2) + 32 * (r // 2) + 32)
                    pe.wait_ge(s_t, g + 1)
                    gate(pe)
                    for j in range(G):
                        at = (j // J) * CH + j % J
                        m = pe.matmul(p_feat[:, j * D:(j + 1) * D], feat[:, r % 2, at:at + CH - J + 1:J],
                                      w.edge[:, :], start=True, stop=True)
                    m.then_inc(s_feat, 1)
                    for h in range(H):
                        pe.wait_ge(s_reset, g * 2 + h + 1)
                        gate(pe)
                        pe.matmul(p_flag[:, :], ones[:, :], flag[:, r % 2, h * CH:(h + 1) * CH],
                                  start=True, stop=True).then_inc(s_flag, 1)
                    windows_of(g, (r + 1) % 2)
                    pe.wait_ge(s_split, g + 1)
                    gate(pe)
                    for j in range(G):
                        at = j % J
                        m = pe.transpose(p_turn[:, j // J, at:at + CH - J + 1:J],
                                         t3[:, r % 2, j, 0:2, :].rearrange("p b f -> p (b f)"), chip.ident[:, :])
                    m.then_inc(s_free[r], 1)
            windows_of(NG, (NG + 1) % 2)

        @block.scalar
        def _(act):
            def copy_back(e):
                act.wait_ge(s_back, e + 1)
                for h in range(H):
                    ins = nc.scalar.copy(back[:, J * h:J * h + J, :].rearrange("p j f -> p (j f)"), p_back[:, h, :])
                ins.then_inc(s_bcopy, 1)

            with act.Fori(0, NG // SLOTS) as k:
                for r in range(SLOTS):
                    g = k * SLOTS + r
                    for h in range(H):
                        act.wait_ge(s_flag, g * 2 + h + 5)
                        if h == 0:
                            act.wait_ge(s_run, g * 2 + 2)
                        nc.scalar.copy(reset[:, h, :], p_flag[:, :]).then_inc(s_reset, 1)
                    act.wait_ge(s_t, g + 2)
                    copy_back(g)
                    t = t3[:, r % 2, :, 1, :]
                    nc.scalar.activation(t3[:, r % 2, :, 2, :], t, ACT.Square)
                    nc.scalar.mul(t3[:, r % 2, :, 0, :], t, -1.0).then_inc(s_split, 1)
            act.wait_ge(s_run, NG * 2 + 2)
            copy_back(NG)

        @block.vector
        def _(v):
            def windows_of(e):
                windows = v.value_load(chip.regs[0:1, 0, bass.ds(e, 1)], min_val=1, max_val=NP // P)
                before = v.value_load(chip.regs[0:1, 1, bass.ds(e, 1)], min_val=0, max_val=NG * NP // P)
                base = v.value_load(chip.regs[0:1, 2, bass.ds(e, 1)], min_val=0, max_val=N)
                with v.Fori(0, windows) as n:
                    at = v.snap((base + n * P).with_bounds(min_val=0, max_val=NP - P))
                    for kind, table in enumerate((chip.dst, chip.last)):
                        for j in range(G):
                            ins = v.tensor_scalar(hot[:, kind, j, :], chip.ramp[:, bass.ds(at, P)],
                                                  table[:, bass.ds(e, 1), j], None, ALU.is_equal)
                            if j == G - 1 or (kind and j == J - 1):
                                ins.then_inc(s_hot, 1)
                    v.wait_ge(s_part, before + n + 1)
                    v.wait_ge(s_added, before + n + 1)
                    v.tensor_tensor(acc[:, :, bass.ds(at, P)], acc[:, :, bass.ds(at, P)],
                                    part[:, 0:2 * P].rearrange("p (a n) -> p a n", a=2), ALU.add)\
                     .then_inc(s_added, 1)

            v.memset(acc[:, :, :], 0.0).then_inc(s_added, 1)
            v.memset(t3[:, 1], 0.0)
            v.memset(ones[:, :], 1.0).then_inc(s_ready, 1)
            v.memset(run[:, 1, :], 0.0).then_inc(s_run, 2)
            v.memset(scratch[:, 0:1], 0.0).then_inc(s_flag, 4)
            v.memset(scratch[:, 1:2], 0.0).then_inc(s_t, 1)
            v.memset(scratch[:, 2:3], 0.0).then_inc(s_reset, 1)
            v.memset(scratch[:, 3:4], 0.0).then_inc(s_bcopy, 1)
            for r in range(SLOTS):
                v.memset(scratch[:, 4 + r:5 + r], 0.0).then_inc(s_free[r], 1)
            with v.Fori(0, NG // SLOTS) as k:
                for r in range(SLOTS):
                    g = k * SLOTS + r
                    v.wait_ge(s_row[r], k * 16 * G + 16 * G)
                    v.wait_ge(s_feat, g + 1)
                    v.tensor_tensor(t3[:, r % 2, :, 1, :], data[:, r, :, :],
                                    p_feat[:, :].rearrange("p (j f) -> p j f", j=G), ALU.add).then_inc(s_t, 1)
                    windows_of(g)
                    v.wait_ge(s_free[r], k + 2)
                    v.wait_ge(s_reset, g * 2 + 3)
                    for h in range(H):
                        v.wait_ge(s_run, g * 2 + 2 + h)
                        before = run[:, (r + 1) % 2, GE - 1:GE] if h == 0 else run[:, r % 2, CH - 1:CH]
                        v.tensor_tensor_scan(run[:, r % 2, h * CH:(h + 1) * CH], reset[:, h, :], p_turn[:, h, :],
                                             before, ALU.add, ALU.max).then_inc(s_run, 1)
            windows_of(NG)


def pna_nodes(chip, w, x_rows, cnt_row):
    nc = chip.nc
    acc = chip.acc2
    low, high = slice(0, D), slice(D, P)
    with ExitStack() as ctx:
        sb, ps, sem = chip.scope(ctx)
        xin = sb("xin", [P, 2, B, D])
        xt = sb("xt", [D, 2, CH])
        cnt = sb("cnt", [P, 2, CH])
        pn = sb("pn", [P, 2, CH])
        rden = sb("rden", [P, 2, CH])
        has = sb("has", [P, 2, CH])
        log = sb("log", [P, 2, CH])
        mom = sb("mom", [P, 2, CH])
        stat_a = sb("stat_a", [P, 2, CH])
        stat_b = sb("stat_b", [P, 2, CH])
        stat_c = sb("stat_c", [D, 2, CH])
        z = sb("z", [P, 2, CH])
        z2 = sb("z2", [D, 2, CH])
        eps = sb("eps", [P, 1])
        one = sb("one", [P, 1])
        p_a = ps("p_a", [P, 2, CH])
        p_b = ps("p_b", [P, 2, CH])
        p_c = ps("p_c", [P, 2, CH])
        s_in = [sem(f"s_in{i}") for i in (0, 1)]
        names = "turn xt pn_p pn deg has den rden mom log ilog sq dv var sd hasp cp stats post z zz lin end eps".split()
        s = {name: sem("s_" + name) for name in names}
        block = ctx.enter_context(nc.Block())

        @block.sync
        def _(sp):
            def body(c, k, pars):
                for i in pars:
                    sp.wait_ge(s["end"], c + 1)
                    sp.dma_start(xin[:, i], rows_of(x_rows, c + i)).then_inc(s_in[i], 16)
                    sp.dma_start(cnt[:, i, :], cnt_row[bass.ds((c + i) * CH, CH)].rearrange("(a n) -> a n", a=1)
                                 .broadcast_to([P, CH])).then_inc(s_in[i], 16)

            by_pairs(sp, body)

        @block.tensor
        def _(pe):
            def body(c, k, pars):
                for i in pars:
                    pe.wait_ge(s_in[i], k * 32 + 32)
                    gate(pe)
                    for b in range(B):
                        t = pe.transpose(p_a[0:D, i, b * P:(b + 1) * P], xin[:, i, b, :], chip.ident[:, :])
                    t.then_inc(s["turn"], 1)
                for i in pars:
                    pe.wait_ge(s["xt"], c + i + 1)
                    gate(pe)
                    pe.matmul(p_b[:, i, :], w.node[:, :], xt[:, i, :], start=True, stop=True).then_inc(s["pn_p"], 1)
                for i in pars:
                    pe.wait_ge(s["stats"], c + i + 1)
                    pe.wait_ge(s["sd"], c + i + 1)
                    gate(pe)
                    for p_out, ws, m in ((p_c, w.wide, P), (p_a, w.att, D)):
                        if m == P:
                            pe.matmul(p_out[:, i, :], w.wide_x[:, :], xt[:, i, :], start=True, stop=False)
                        pe.matmul(p_out[0:m, i, :], ws[:, 0, :], stat_a[:, i, :], start=(m == D), stop=False)
                        pe.matmul(p_out[0:m, i, :], ws[:, 1, :], stat_b[:, i, :], start=False, stop=False)
                        t = pe.matmul(p_out[0:m, i, :], ws[0:D, 2, :], stat_c[:, i, :], start=False, stop=True)
                    t.then_inc(s["post"], 1)
                for i in pars:
                    pe.wait_ge(s["z"], c + i + 1)
                    pe.wait_ge(s["zz"], c + i + 1)
                    gate(pe)
                    pe.matmul(p_b[0:D, i, :], w.lin[:, :], z[:, i, :], start=True, stop=False)
                    pe.matmul(p_b[0:D, i, :], w.lin[0:D, :], z2[:, i, :], start=False, stop=True)\
                      .then_inc(s["lin"], 1)

            by_pairs(pe, body)

        @block.scalar
        def _(act):
            act.wait_ge(s["eps"], 2)

            def body(c, k, pars):
                for i in pars:
                    act.wait_ge(s["turn"], c + i + 1)
                    nc.scalar.copy(xt[:, i, :], p_a[0:D, i, :]).then_inc(s["xt"], 1)
                for i in pars:
                    act.wait_ge(s["deg"], c + i + 1)
                    nc.scalar.activation(log[:, i, :], log[:, i, :], ACT.Ln, bias=one[:, 0:1]).then_inc(s["log"], 1)
                for i in pars:
                    act.wait_ge(s["pn_p"], c + i + 1)
                    nc.scalar.activation(pn[:, i, :], p_b[:, i, :], ACT.Identity,
                                         bias=w.node_bias[:, 0:1]).then_inc(s["pn"], 1)
                for i in pars:
                    act.wait_ge(s["mom"], c + i + 1)
                    nc.scalar.activation(stat_b[high, i, :], mom[low, i, :], ACT.Square).then_inc(s["sq"], 1)
                for i in pars:
                    act.wait_ge(s["var"], c + i + 1)
                    nc.scalar.activation(stat_b[high, i, :], stat_b[high, i, :], ACT.Sqrt,
                                         bias=eps[high, 0:1]).then_inc(s["sd"], 1)
                for i in pars:
                    act.wait_ge(s["post"], c + i + 1)
                    nc.scalar.activation(z[low, i, :], p_c[low, i, :], ACT.Identity,
                                         bias=w.post_bias[:, 0:1]).then_inc(s["z"], 1)
                for i in pars:
                    act.wait_ge(s["lin"], c + i + 1)
                    nc.scalar.activation(acc[low, 0, bass.ds((c + i) * CH, CH)], p_b[low, i, :], ACT.Identity,
                                         bias=w.lin_bias[:, 0:1]).then_inc(s["end"], 1)

            by_pairs(act, body)

        @block.vector
        def _(v):
            v.memset(eps[:, :], EPS_STD).then_inc(s["eps"], 1)
            v.memset(one[:, :], 1.0).then_inc(s["eps"], 1)
            v.memset(z[0:1, 0, 0:1], 0.0).then_inc(s["end"], 1)

            def body(c, k, pars):
                span = lambda i: bass.ds((c + i) * CH, CH)
                for i in pars:
                    v.wait_ge(s_in[i], k * 32 + 32)
                    v.tensor_scalar(log[:, i, :], cnt[:, i, :], 1.0, None, ALU.max).then_inc(s["deg"], 1)
                    v.tensor_scalar(has[:, i, :], cnt[:, i, :], 1.0, None, ALU.min).then_inc(s["has"], 1)
                    v.tensor_scalar(mom[:, i, :], cnt[:, i, :], 1.0, None, ALU.max).then_inc(s["den"], 1)
                for i in pars:
                    v.wait_ge(s["den"], c + i + 1)
                    v.reciprocal(rden[:, i, :], mom[:, i, :]).then_inc(s["rden"], 1)
                for i in pars:
                    v.wait_ge(s["rden"], c + i + 1)
                    v.tensor_tensor(mom[:, i, :], acc[:, 0, span(i)], rden[:, i, :], ALU.mult)\
                     .then_inc(s["mom"], 1)
                for i in pars:
                    v.wait_ge(s["log"], c + i + 1)
                    v.wait_ge(s["mom"], c + i + 1)
                    v.reciprocal(rden[low, i, :], log[low, i, :]).then_inc(s["ilog"], 1)
                for i in pars:
                    v.wait_ge(s["sq"], c + i + 1)
                    v.scalar_tensor_tensor(out=stat_b[high, i, :], in0=stat_b[high, i, :], scalar=-1.0,
                                           in1=mom[high, i, :], op0=ALU.mult, op1=ALU.add).then_inc(s["dv"], 1)
                for i in pars:
                    v.wait_ge(s["dv"], c + i + 1)
                    v.tensor_scalar(stat_b[high, i, :], stat_b[high, i, :], 0.0, None, ALU.max)\
                     .then_inc(s["var"], 1)
                for i in pars:
                    v.wait_ge(s["pn"], c + i + 1)
                    v.wait_ge(s["has"], c + i + 1)
                    v.tensor_tensor(has[:, i, :], has[:, i, :], pn[:, i, :], ALU.mult).then_inc(s["hasp"], 1)
                    v.tensor_tensor(stat_c[:, i, :], cnt[low, i, :], pn[low, i, :], ALU.mult)\
                     .then_inc(s["cp"], 1)
                for i in pars:
                    v.wait_ge(s["hasp"], c + i + 1)
                    v.wait_ge(s["mom"], c + i + 1)
                    v.tensor_tensor(stat_a[low, i, :], has[low, i, :], mom[low, i, :], ALU.add)
                    v.tensor_tensor(stat_a[high, i, :], has[high, i, :], acc[high, 1, span(i)], ALU.add)
                    v.tensor_tensor(stat_b[low, i, :], acc[low, 1, span(i)], has[low, i, :], ALU.subtract)
                    v.wait_ge(s["cp"], c + i + 1)
                    v.tensor_tensor(stat_c[:, i, :], stat_c[:, i, :], acc[low, 0, span(i)], ALU.add)\
                     .then_inc(s["stats"], 1)
                for i in pars:
                    v.wait_ge(s["post"], c + i + 1)
                    v.wait_ge(s["ilog"], c + i + 1)
                    v.scalar_tensor_tensor(out=z[high, i, :], in0=p_c[high, i, :], scalar=1.0 / AVG_LOG,
                                           in1=log[high, i, :], op0=ALU.mult, op1=ALU.mult)
                    v.scalar_tensor_tensor(out=z2[:, i, :], in0=p_a[low, i, :], scalar=AVG_LOG,
                                           in1=rden[low, i, :], op0=ALU.mult, op1=ALU.mult).then_inc(s["zz"], 1)

            by_pairs(v, body)


def batch_norm_stats(chip, w, scale, shift):
    nc = chip.nc
    x = chip.acc2[0:D, 0, 0:N]
    with ExitStack() as ctx:
        sb, ps, sem = chip.scope(ctx)
        c = sb("c", [D, 6])
        s_v = sem("s_v")
        s_mean = sem("s_mean")
        s_sd = sem("s_sd")
        s_sq = sem("s_sq")
        block = ctx.enter_context(nc.Block())

        @block.vector
        def _(v):
            v.memset(c[:, 5:6], EPS_BN)
            v.tensor_reduce(c[:, 0:1], x, AX_X, ALU.add).then_inc(s_v, 1)
            v.wait_ge(s_v, 1)
            v.tensor_scalar(c[:, 1:2], c[:, 0:1], -1.0 / N, None, ALU.mult).then_inc(s_mean, 1)
            v.wait_ge(s_sd, 1)
            v.reciprocal(c[:, 4:5], c[:, 3:4]).then_inc(s_v, 1)
            v.wait_ge(s_v, 2)
            v.tensor_tensor(scale[:, :], c[:, 4:5], w.gamma[:, :], ALU.mult).then_inc(s_v, 1)
            v.wait_ge(s_v, 3)
            v.scalar_tensor_tensor(out=shift[:, :], in0=scale[:, :], scalar=c[:, 1:2], in1=w.beta[:, :],
                                   op0=ALU.mult, op1=ALU.add)

        @block.scalar
        def _(act):
            act.wait_ge(s_mean, 1)
            nc.scalar.activation(chip.acc2[0:D, 1, 0:N], x, ACT.Square, bias=c[:, 1:2],
                                 accum_out=c[:, 2:3]).then_inc(s_sq, 1)
            act.wait_ge(s_sq, 1)
            nc.scalar.activation(c[:, 3:4], c[:, 2:3], ACT.Sqrt, bias=c[:, 5:6], scale=1.0 / N).then_inc(s_sd, 1)


def batch_norm_rows(chip, scale, shift, out_rows):
    nc = chip.nc
    with ExitStack() as ctx:
        sb, ps, sem = chip.scope(ctx)
        xt = sb("xt", [D, 2, CH])
        stage = sb("stage", [P, 2, B, D])
        p_x = ps("p_x", [P, 2, CH])
        s_x = sem("s_x")
        s_turn = sem("s_turn")
        s_end = sem("s_end")
        s_out = [sem(f"s_out{i}") for i in (0, 1)]
        block = ctx.enter_context(nc.Block())

        @block.scalar
        def _(act):
            def body(c, k, pars):
                for i in pars:
                    act.wait_ge(s_end, c + 1)
                    nc.scalar.activation(xt[:, i, :], chip.acc2[0:D, 0, bass.ds((c + i) * CH, CH)], ACT.Relu,
                                         bias=shift[:, 0:1], scale=scale[:, 0:1]).then_inc(s_x, 1)

            by_pairs(act, body)

        @block.tensor
        def _(pe):
            def body(c, k, pars):
                for i in pars:
                    pe.wait_ge(s_x, c + i + 1)
                    gate(pe)
                    for b in range(B):
                        t = pe.transpose(p_x[:, i, b * D:(b + 1) * D], xt[:, i, b * P:(b + 1) * P],
                                         chip.ident[0:D, 0:D])
                    t.then_inc(s_turn, 1)

            by_pairs(pe, body)

        @block.vector
        def _(v):
            for i in (0, 1):
                v.memset(stage[0:1, i, 0, 0:1], 0.0).then_inc(s_out[i], 16)
            v.memset(stage[0:1, 0, 1, 0:1], 0.0).then_inc(s_end, 1)

            def body(c, k, pars):
                for i in pars:
                    v.wait_ge(s_turn, c + i + 1)
                    v.wait_ge(s_out[i], k * 16 + 16)
                    v.tensor_copy(stage[:, i, :, :],
                                  p_x[:, i, 0:B * D].rearrange("p (b f) -> p b f", b=B)).then_inc(s_end, 1)

            by_pairs(v, body)

        @block.sync
        def _(sp):
            def body(c, k, pars):
                for i in pars:
                    sp.wait_ge(s_end, c + i + 2)
                    sp.dma_start(rows_of(out_rows, c + i), stage[:, i]).then_inc(s_out[i], 16)

            by_pairs(sp, body)
            for i in (0, 1):
                sp.wait_ge(s_out[i], 16 + 16 * ((NCH + 1 - i) // 2))


def save_counts(chip, cnt_row):
    nc = chip.nc
    with ExitStack() as ctx:
        sb, ps, sem = chip.scope(ctx)
        s_cnt = sem("s_cnt")
        block = ctx.enter_context(nc.Block())

        @block.sync
        def _(sp):
            sp.dma_start(cnt_row.rearrange("(a n) -> a n", a=1), chip.acc[KC - 1:KC, :]).then_inc(s_cnt, 16)
            sp.wait_ge(s_cnt, 16)


def gnn(nc, x_pad, src_pad, dst_pad, ea_pad, ea_t, W1, b1, W2, b2, W3, b3, We, be, Wp, bp, Wo, bo, Wl, bl,
        bn_g, bn_b, out):
    chip = Chip(nc)
    flags = nc.dram_tensor("flags", [EP], BF16, kind="Internal").ap()
    cnt_row = nc.dram_tensor("cnt_row", [NP], F32, kind="Internal").ap()
    h1 = nc.dram_tensor("h1_rows", [NP, D], F32, kind="Internal").ap()
    h2 = nc.dram_tensor("h2_rows", [NP, D], F32, kind="Internal").ap()
    h3 = nc.dram_tensor("h3_rows", [NP, D], F32, kind="Internal").ap()
    x1 = nc.dram_tensor("x1_rows", [NP, D], F32, kind="Internal").ap()
    x2 = nc.dram_tensor("x2_rows", [NP, D], F32, kind="Internal").ap()
    x3 = nc.dram_tensor("x3_rows", [NP, D], F32, kind="Internal").ap()
    q_rows = nc.dram_tensor("q_rows", [NP, D], F32, kind="Internal").ap()
    with ExitStack() as ctx:
        sb, ps, sem = chip.scope(ctx)
        chip.ramp = sb("ramp", [P, NP], I16)
        chip.ident = sb("ident", [P, P])
        chip.dst = sb("dst", [P, NG + 1, G])
        chip.last = sb("last", [P, NG + 1, G])
        chip.regs = sb("regs", [1, 3, NG + 1], I32)
        prepare(chip, dst_pad, flags)
        with ExitStack() as l0:
            sb, ps, sem = chip.scope(l0)
            chip.acc = sb("acc", [P, NP])
            sum_pass(chip, x_pad, src_pad, ea_pad, True)
            conv_nodes(chip, x_pad, W1, b1, h1, True)
            sum_pass(chip, h1, src_pad, ea_pad, False)
            conv_nodes(chip, h1, W2, b2, h2, True)
            sum_pass(chip, h2, src_pad, ea_pad, False)
            conv_nodes(chip, h2, W3, b3, h3, False)
            save_counts(chip, cnt_row)
        residual_norm(chip, x_pad, h3, x1)
        with ExitStack() as l1:
            sb, ps, sem = chip.scope(l1)
            chip.acc2 = sb("acc2", [P, 2, NP])
            scale = sb("scale", [D, 1])
            shift = sb("shift", [D, 1])
            w = PnaWeights(sb)
            for layer, (x_rows, y_rows) in enumerate(((x1, x2), (x2, x3))):
                pna_weights(chip, w, layer, We, be, Wp, bp, Wo, bo, Wl, bl, bn_g, bn_b)
                source_table(chip, w, x_rows, q_rows)
                pna_pass(chip, w, q_rows, src_pad, ea_t, flags)
                pna_nodes(chip, w, x_rows, cnt_row)
                batch_norm_stats(chip, w, scale, shift)
                batch_norm_rows(chip, scale, shift, y_rows)
        residual_norm(chip, x1, x3, out)


_NAMES = ["L0_gnn_W1", "L0_gnn_b1", "L0_gnn_W2", "L0_gnn_b2", "L0_gnn_W3", "L0_gnn_b3",
          "L1_gnn_W_edge", "L1_gnn_b_edge", "L1_gnn_W_pre", "L1_gnn_b_pre", "L1_gnn_W_post",
          "L1_gnn_b_post", "L1_gnn_W_lin", "L1_gnn_b_lin", "L1_gnn_bn_gamma", "L1_gnn_bn_beta"]


def kernel(**inputs):
    import numpy as _np
    import concourse.bacc as _bacc
    from concourse import mybir as _mybir
    from concourse.bass_utils import run_bass_kernel_spmd as _run

    nc = _bacc.Bacc("TRN2", target_bir_lowering=False, num_devices=1)
    x = _np.asarray(inputs["x"])
    ea = _np.asarray(inputs["edge_attr_16"])
    src = _np.asarray(inputs["src"])
    dst = _np.asarray(inputs["dst"])
    arrays_in = {
        "x_pad": _np.concatenate([x, _np.zeros((NP - N, D), x.dtype)]),
        "src_pad": _np.concatenate([src, _np.zeros((EP - E,), src.dtype)]),
        "dst_pad": _np.concatenate([_np.full((1,), -1, dst.dtype), dst, _np.full((EP - E,), N, dst.dtype),
                                    _np.full((1,), N + 1, dst.dtype)]),
        "ea_pad": _np.concatenate([ea, _np.zeros((EP - E, FE), ea.dtype)]),
    }
    arrays_in["ea_t"] = _np.ascontiguousarray(arrays_in["ea_pad"].T)
    for name in _NAMES:
        arrays_in[name] = _np.ascontiguousarray(inputs[name])
    arrays, args = {}, []
    for name, a in arrays_in.items():
        arrays[f"in_{name}"] = a
        args.append(nc.dram_tensor(f"in_{name}", a.shape, _mybir.dt.from_np(a.dtype), kind="ExternalInput").ap())
    args.append(nc.dram_tensor("out_0", (NP, D), _mybir.dt.float32, kind="ExternalOutput").ap())
    gnn(nc, *args)
    r = _run(nc, [arrays], core_ids=[0])
    return r.results[0]["out_0"][:N]
```

```python
from contextlib import ExitStack

import numpy as np
import concourse.bass as bass
from concourse import mybir

F32 = mybir.dt.float32
I32 = mybir.dt.int32
I16 = mybir.dt.int16
BF16 = mybir.dt.bfloat16
ALU = mybir.AluOpType
ACT = mybir.ActivationFunctionType
AX_X = mybir.AxisListType.X

N, E, D, FE = 12500, 212500, 64, 16
P = 128
G = 8
H = 2
J = G // H
GE = G * P
SLOTS = 4
NG = -(-E // (GE * SLOTS)) * SLOTS
EP = NG * GE
CH = 512
NCH = -(-N // CH)
NP = NCH * CH
assert N + P <= NP
B = CH // P
KC = D + FE + 1
RESET = -float(2.0 ** 127)
EPS_LN = 1e-5
EPS_STD = 1e-5
EPS_BN = 1e-5
AVG_LOG = float(np.log(17.0))
LAYERS = 2


def gate(eng):
    eng.nop(nofuse=True)


class Chip:

    def __init__(self, nc):
        self.nc = nc
        self.n = 0

    def scope(self, ctx):
        nc = self.nc
        self.n += 1
        tag = f"_{self.n}"
        sb = lambda name, shape, dt=F32: ctx.enter_context(nc.sbuf_tensor(name + tag, shape, dt))
        ps = lambda name, shape, dt=F32: ctx.enter_context(nc.psum_tensor(name + tag, shape, dt))
        sems = []

        def sem(name):
            sems.append(nc.alloc_semaphore(name + tag))
            return sems[-1]

        def close():
            if sems:
                nc.clear_and_free_semaphores(sems)
                nc.all_engine_barrier()

        ctx.callback(close)
        return sb, ps, sem


def prepare(chip, dst_pad, flags):
    nc = chip.nc
    with ExitStack() as ctx:
        sb, ps, sem = chip.scope(ctx)
        cur = sb("cur", [P, NG * G], I32)
        nxt = sb("nxt", [P, NG * G], I32)
        change = sb("change", [P, NG * G])
        start = sb("start", [P, NG * G], BF16)
        rows = sb("rows", [1, 2, NG], I32)
        wf = sb("wf", [1, 6, NG + 1])
        ones = sb("ones", [1, P])
        p_first = ps("p_first", [P, CH])
        s_tile = sem("s_tile")
        s_lin = sem("s_lin")
        s_rows = sem("s_rows")
        s_flags = sem("s_flags")
        s_v = sem("s_v")
        s_zero = sem("s_zero")
        s_pool = sem("s_pool")
        s_free = sem("s_free")
        s_row = sem("s_row")
        s_first = sem("s_first")
        block = ctx.enter_context(nc.Block())
        tiles = lambda shift: dst_pad[shift:shift + EP].rearrange("(q p j) -> p q j", p=P, j=J)
        line = lambda shift: dst_pad[shift:shift + EP].rearrange("(p c) -> p c", p=P)
        q3 = lambda t: t[:, :].rearrange("p (q j) -> p q j", j=J)

        @block.sync
        def _(sp):
            heads = dst_pad[1:1 + EP].rearrange("(a g e) -> a g e", a=1, e=GE)
            sp.dma_start(rows[:, 0, :], heads[:, :, 0], allow_slow_non_contiguous=True).then_inc(s_rows, 16)
            sp.dma_start(rows[:, 1, :], heads[:, :, GE - 1], allow_slow_non_contiguous=True).then_inc(s_rows, 16)
            sp.dma_start(q3(cur), tiles(1)).then_inc(s_tile, 16)
            sp.dma_start(q3(nxt), tiles(2)).then_inc(s_tile, 16)
            sp.wait_ge(s_free, 1)
            sp.dma_start(cur[:, :], line(1)).then_inc(s_lin, 16)
            sp.dma_start(nxt[:, :], line(0)).then_inc(s_lin, 16)
            sp.wait_ge(s_v, 13)
            sp.dma_start(flags.rearrange("(p c) -> p c", p=P), start[:, :]).then_inc(s_flags, 16)
            sp.wait_ge(s_flags, 16)

        @block.gpsimd
        def _(pool):
            pool.iota(chip.ramp[:, :], [[1, P]], base=0, channel_multiplier=0,
                      allow_small_or_imprecise_dtypes=True)
            pool.iota(chip.shifts[:, :], [[-P, NP // P]], base=0, channel_multiplier=0,
                      allow_small_or_imprecise_dtypes=True)
            pool.memset(chip.ident[:, :], 0.0).then_inc(s_zero, 1)
            pool.wait_ge(s_zero, 1)
            pool.affine_select(out=chip.ident[:, :], in_=chip.ident[:, :], compare_op=ALU.not_equal,
                               fill=1.0, base=0, pattern=[[-1, P]], channel_multiplier=1).then_inc(s_pool, 1)

        @block.vector
        def _(v):
            v.wait_ge(s_rows, 32)
            v.tensor_tensor(rows[:, 1, :], rows[:, 1, :], rows[:, 0, :], ALU.subtract).then_inc(s_v, 1)
            v.wait_ge(s_v, 1)
            v.tensor_scalar(rows[:, 1, :], rows[:, 1, :], 7, None, ALU.arith_shift_right).then_inc(s_v, 1)
            v.wait_ge(s_v, 2)
            v.memset(wf[:, 0, 0:1], 1.0)
            v.memset(wf[:, 5, 0:1], 0.0)
            v.tensor_copy(wf[:, 5, 1:], rows[:, 1, :])
            v.tensor_scalar(wf[:, 0, 1:], rows[:, 1, :], 1.0, None, ALU.add).then_inc(s_v, 1)
            v.memset(wf[:, 1, :], 1.0).then_inc(s_v, 1)
            v.wait_ge(s_v, 4)
            v.tensor_tensor_scan(wf[:, 2, :], wf[:, 1, :], wf[:, 5, :], 0.0, ALU.mult, ALU.add).then_inc(s_v, 1)
            v.wait_ge(s_v, 5)
            v.tensor_tensor(wf[:, 3, :], wf[:, 2, :], wf[:, 5, :], ALU.subtract).then_inc(s_v, 1)
            v.tensor_copy(chip.regs[:, 0, :], wf[:, 0, :])
            v.memset(chip.regs[:, 2, 0:1], N)
            v.tensor_copy(chip.regs[:, 2, 1:], rows[:, 0, :])
            v.memset(ones[:, :], 1.0)
            v.tensor_copy(wf[:, 4, 1:], rows[:, 0, :]).then_inc(s_row, 1)
            v.wait_ge(s_v, 6)
            v.tensor_copy(chip.regs[:, 1, :], wf[:, 3, :]).then_inc(s_v, 1)
            v.wait_ge(s_tile, 32)
            flat = lambda t: t[:, 1:, :].rearrange("p g j -> p (g j)")
            groups = lambda t: t[:, :].rearrange("p (g j) -> p g j", j=G)
            v.memset(chip.last[:, 0, :], -1.0)
            v.tensor_tensor(change[:, :], cur[:, :], nxt[:, :], ALU.not_equal).then_inc(s_v, 1)
            v.wait_ge(s_first, 1)
            v.tensor_tensor(chip.dst[:, 1:, :], groups(cur),
                            p_first[:, 0:NG].unsqueeze(2).broadcast_to([P, NG, G]), ALU.subtract).then_inc(s_v, 1)
            v.wait_ge(s_v, 9)
            v.scalar_tensor_tensor(out=flat(chip.last), in0=flat(chip.dst), scalar=1.0, in1=change[:, :],
                                   op0=ALU.add, op1=ALU.mult).then_inc(s_v, 1)
            v.wait_ge(s_v, 10)
            v.tensor_scalar(flat(chip.last), flat(chip.last), -1.0, None, ALU.add).then_inc(s_v, 1)
            v.wait_ge(s_v, 11)
            v.memset(rows[:, 1, 0:1], 0).then_inc(s_free, 1)
            v.wait_ge(s_lin, 32)
            v.tensor_tensor(change[:, :], cur[:, :], nxt[:, :], ALU.not_equal).then_inc(s_v, 1)
            v.wait_ge(s_v, 12)
            v.tensor_scalar(start[:, :], change[:, :], RESET, None, ALU.mult).then_inc(s_v, 1)

        @block.tensor
        def _(pe):
            pe.wait_ge(s_row, 1)
            pe.matmul(p_first[:, 0:NG], ones[:, :], wf[:, 4, 1:], start=True, stop=True).then_inc(s_first, 1)


def edge_views(src_pad, g):
    return src_pad[bass.ds(g * GE, GE)].rearrange("(h p j) -> p h j", h=H, p=P)


def build_hot(chip, v, hot, table, entry, beyond=None):
    for j in range(G):
        column = table[:, bass.ds(entry, 1), j]
        if beyond is None:
            ins = v.tensor_scalar(hot[:, j, :], chip.ramp[:, :], column, None, ALU.is_equal)
        else:
            ins = v.tensor_scalar(hot[:, j, :], chip.ramp[:, :], column, chip.shifts[:, bass.ds(beyond, 1)],
                                  ALU.subtract, ALU.is_equal)
    return ins


def load_entry(chip, eng, row, entry, low, high):
    return eng.value_load(chip.regs[0:1, row, bass.ds(entry, 1)], min_val=low, max_val=high)


def further_windows(chip, eng, entry, body):
    windows = load_entry(chip, eng, 0, entry, 1, NP // P)
    with eng.If(windows > 1):
        before = load_entry(chip, eng, 1, entry, 0, NG * NP // P)
        with eng.Fori(1, windows) as n:
            body(n, eng.snap((before + n).with_bounds(min_val=1, max_val=NG * NP // P)))


def sum_pass(chip, table, src_pad, ea_pad, first):
    nc = chip.nc
    acc = chip.acc
    M = KC if first else D
    with ExitStack() as ctx:
        sb, ps, sem = chip.scope(ctx)
        idx = sb("idx", [P, SLOTS, G], I32)
        data = sb("data", [P, SLOTS, G, KC])
        hot = sb("hot", [P, 2, G, P])
        part = ps("part", [P, 2, CH])
        part_x = ps("part_x", [P, CH])
        scratch = sb("scratch", [1, 1])
        s_idx = [sem(f"s_idx{r}") for r in range(SLOTS)]
        s_ea = [sem(f"s_ea{r}") for r in range(SLOTS)]
        s_row = [sem(f"s_row{r}") for r in range(SLOTS)]
        s_ready = sem("s_ready")
        s_hot = sem("s_hot")
        s_part = sem("s_part")
        s_added = sem("s_added")
        s_hot_x = sem("s_hot_x")
        s_part_x = sem("s_part_x")
        s_added_x = sem("s_added_x")
        block = ctx.enter_context(nc.Block())

        @block.sync
        def _(sp):
            with sp.Fori(0, NG // SLOTS) as k:
                for r in range(SLOTS):
                    g = k * SLOTS + r
                    sp.wait_ge(s_added, g + 1)
                    sp.dma_start(idx[:, r, :].rearrange("p (h j) -> p h j", h=H),
                                 edge_views(src_pad, g)).then_inc(s_idx[r], 16)
                    if first:
                        for h in range(H):
                            sp.dma_start(data[:, r, J * h:J * h + J, D:D + FE],
                                         ea_pad[bass.ds(g * GE + h * J * P, J * P), :]
                                         .rearrange("(p j) f -> p j f", p=P)).then_inc(s_ea[r], 16)

        @block.gpsimd
        def _(pool):
            with pool.Fori(0, NG // SLOTS) as k:
                for r in range(SLOTS):
                    pool.wait_ge(s_idx[r], k * 16 + 16)
                    gate(pool)
                    for j in range(G):
                        pool.indirect_dma_start(
                            out=data[:, r, j, 0:D], out_offset=None, in_=table[:, :],
                            in_offset=bass.IndirectOffsetOnAxis(ap=idx[:, r, j:j + 1], axis=0),
                        ).then_inc(s_row[r], 16)

        @block.tensor
        def _(pe):
            def products(out, r):
                for j in range(G):
                    mm = pe.matmul(out[0:M, 0:P], data[:, r, j, 0:M], hot[:, r % 2, j, :],
                                   start=(j == 0), stop=(j == G - 1))
                return mm

            pe.wait_ge(s_ready, 1)
            with pe.Fori(0, NG // SLOTS) as k:
                for r in range(SLOTS):
                    g = k * SLOTS + r
                    pe.wait_ge(s_row[r], k * 16 * G + 16 * G)
                    if first:
                        pe.wait_ge(s_ea[r], k * 16 * H + 16 * H)
                    pe.wait_ge(s_hot, g + 1)
                    pe.wait_ge(s_added, g + SLOTS - 1)
                    gate(pe)
                    products(part[:, r % 2], r).then_inc(s_part, 1)

                    def more(n, x):
                        pe.wait_ge(s_hot_x, x)
                        pe.wait_ge(s_added_x, x)
                        gate(pe)
                        products(part_x, r).then_inc(s_part_x, 1)

                    further_windows(chip, pe, g + 1, more)

        @block.vector
        def _(v):
            def add(base, n, sums):
                at = v.snap((base + n * P).with_bounds(min_val=0, max_val=NP - P))
                return v.tensor_tensor(acc[0:M, bass.ds(at, P)], acc[0:M, bass.ds(at, P)], sums[0:M, 0:P], ALU.add)

            def finish(k, r, g):
                base = load_entry(chip, v, 2, g + 1, 0, N)
                v.wait_ge(s_part, g + 1)
                v.wait_ge(s_added, g + SLOTS)
                add(base, 0, part[:, r % 2]).then_inc(s_added, 1)

                def more(n, x):
                    if_ready = g + SLOTS + 1
                    v.wait_ge(s_added, if_ready)
                    build_hot(chip, v, hot[:, r % 2], chip.dst, g + 1, n).then_inc(s_hot_x, 1)
                    v.wait_ge(s_part_x, x)
                    add(base, n, part_x).then_inc(s_added_x, 1)
                    v.wait_ge(s_added_x, x + 1)

                further_windows(chip, v, g + 1, more)

            v.memset(data[:, :, :, KC - 1:KC], 1.0).then_inc(s_ready, 1)
            v.memset(acc[0:M, :], 0.0).then_inc(s_added, SLOTS)
            v.memset(scratch[:, :], 0.0).then_inc(s_added_x, 1)
            last_k = NG // SLOTS - 1
            build_hot(chip, v, hot[:, 0], chip.dst, 1).then_inc(s_hot, 1)

            def body(k, r, ahead):
                g = k * SLOTS + r
                if ahead:
                    build_hot(chip, v, hot[:, (r + 1) % 2], chip.dst, g + 2).then_inc(s_hot, 1)
                finish(k, r, g)

            with v.Fori(0, last_k) as k:
                for r in range(SLOTS):
                    body(k, r, True)
            for r in range(SLOTS):
                body(last_k, r, r < SLOTS - 1)


def by_pairs(eng, body):
    with eng.Fori(0, NCH // 2) as k:
        body(k * 2, k, (0, 1))
    if NCH % 2:
        body(NCH - 1, NCH // 2, (0,))


def rows_of(t, c):
    return t[bass.ds(c * CH, CH), :].rearrange("(b p) f -> p b f", p=P)


def conv_nodes(chip, h_rows, W, bias, out_rows, relu):
    nc = chip.nc
    acc = chip.acc
    with ExitStack() as ctx:
        sb, ps, sem = chip.scope(ctx)
        wa = sb("wa", [D, D])
        wsum = sb("wsum", [KC, D])
        pick = sb("pick", [KC, D])
        picked = sb("picked", [1, D])
        hin = sb("hin", [P, 2, B, D])
        ht = sb("ht", [D, 2, CH])
        hc = sb("hc", [D, 2, CH])
        ot = sb("ot", [D, 2, CH])
        stage = sb("stage", [P, 2, B, D])
        p_h = ps("p_h", [P, 2, CH])
        p_cnt = ps("p_cnt", [P, 2, CH])
        p_out = ps("p_out", [P, 2, CH])
        s_w = sem("s_w")
        s_pick0 = sem("s_pick0")
        s_pick1 = sem("s_pick1")
        s_pick = sem("s_pick")
        s_in = [sem(f"s_in{i}") for i in (0, 1)]
        s_turn = sem("s_turn")
        s_ht = sem("s_ht")
        s_hc = sem("s_hc")
        s_sum = sem("s_sum")
        s_ot = sem("s_ot")
        s_back = sem("s_back")
        s_end = sem("s_end")
        s_out = [sem(f"s_out{i}") for i in (0, 1)]
        block = ctx.enter_context(nc.Block())

        @block.sync
        def _(sp):
            sp.dma_start(wa[:, :], W[0:D, :]).then_inc(s_w, 16)
            sp.dma_start(wsum[0:D + FE, :], W[D:, :]).then_inc(s_w, 16)
            sp.dma_start(wsum[KC - 1:KC, :], bias.rearrange("(a f) -> a f", a=1)).then_inc(s_w, 16)
            sp.wait_ge(s_pick0, 2)
            sp.dma_start(pick[KC - 1:KC, :], picked[:, :]).then_inc(s_pick, 16)

            def body(c, k, pars):
                for i in pars:
                    sp.wait_ge(s_end, c + 1)
                    sp.dma_start(hin[:, i], rows_of(h_rows, c + i)).then_inc(s_in[i], 16)
                for i in pars:
                    sp.wait_ge(s_end, c + i + 2)
                    sp.dma_start(rows_of(out_rows, c + i), stage[:, i]).then_inc(s_out[i], 16)

            by_pairs(sp, body)
            for i in (0, 1):
                sp.wait_ge(s_out[i], 16 + 16 * ((NCH + 1 - i) // 2))

        @block.tensor
        def _(pe):
            pe.wait_ge(s_w, 48)
            pe.wait_ge(s_pick, 16)

            def body(c, k, pars):
                for i in pars:
                    pe.wait_ge(s_in[i], k * 16 + 16)
                    gate(pe)
                    for b in range(B):
                        pe.transpose(p_h[0:D, i, b * P:(b + 1) * P], hin[:, i, b, :], chip.ident[:, :])
                    pe.matmul(p_cnt[0:D, i, :], pick[:, :], acc[0:KC, bass.ds((c + i) * CH, CH)],
                              start=True, stop=True).then_inc(s_turn, 1)
                for i in pars:
                    pe.wait_ge(s_hc, c + i + 1)
                    gate(pe)
                    pe.matmul(p_out[0:D, i, :], wsum[:, :], acc[0:KC, bass.ds((c + i) * CH, CH)],
                              start=True, stop=False)
                    pe.matmul(p_out[0:D, i, :], wa[:, :], hc[:, i, :], start=False, stop=True).then_inc(s_sum, 1)
                for i in pars:
                    pe.wait_ge(s_ot, c + i + 1)
                    gate(pe)
                    for b in range(B):
                        t = pe.transpose(p_h[:, i, b * D:(b + 1) * D], ot[:, i, b * P:(b + 1) * P],
                                         chip.ident[0:D, 0:D])
                    t.then_inc(s_back, 1)

            by_pairs(pe, body)

        @block.scalar
        def _(act):
            def body(c, k, pars):
                for i in pars:
                    act.wait_ge(s_turn, c + i + 1)
                    nc.scalar.copy(ht[:, i, :], p_h[0:D, i, :]).then_inc(s_ht, 1)
                for i in pars:
                    act.wait_ge(s_sum, c + i + 1)
                    nc.scalar.activation(ot[:, i, :], p_out[0:D, i, :],
                                         ACT.Relu if relu else ACT.Copy).then_inc(s_ot, 1)

            by_pairs(act, body)

        @block.vector
        def _(v):
            v.memset(pick[:, :], 0.0).then_inc(s_pick0, 1)
            v.memset(picked[:, :], 1.0).then_inc(s_pick0, 1)
            v.memset(stage[:, :, :, :], 0.0).then_inc(s_pick1, 1)
            v.wait_ge(s_pick1, 1)
            for i in (0, 1):
                v.memset(stage[0:1, i, 0, 0:1], 0.0).then_inc(s_out[i], 16)
            v.memset(stage[0:1, 0, 1, 0:1], 0.0).then_inc(s_end, 1)

            def body(c, k, pars):
                for i in pars:
                    v.wait_ge(s_ht, c + i + 1)
                    v.tensor_tensor(hc[:, i, :], ht[:, i, :], p_cnt[0:D, i, :], ALU.mult).then_inc(s_hc, 1)
                for i in pars:
                    v.wait_ge(s_back, c + i + 1)
                    v.wait_ge(s_out[i], k * 16 + 16)
                    v.tensor_copy(stage[:, i, :, :],
                                  p_h[:, i, 0:B * D].rearrange("p (b f) -> p b f", b=B)).then_inc(s_end, 1)

            by_pairs(v, body)


def residual_norm(chip, a_rows, b_rows, out_rows):
    nc = chip.nc
    R = NP // P
    PIECES = 4
    W = R // PIECES
    with ExitStack() as ctx:
        sb, ps, sem = chip.scope(ctx)
        a = sb("a", [P, PIECES, W, D])
        b = sb("b", [P, PIECES, W, D])
        sq = sb("sq", [P, W, D])
        mean = sb("mean", [P, PIECES, W])
        var = sb("var", [P, PIECES, W])
        eps = sb("eps", [P, 1])
        s_a = [sem(f"s_a{n}") for n in range(PIECES)]
        s_v = sem("s_v")
        s_sd = sem("s_sd")
        s_var = sem("s_var")
        s_norm = sem("s_norm")
        s_out = sem("s_out")
        block = ctx.enter_context(nc.Block())
        view = lambda t: t.rearrange("(p q w) f -> q p (w f)", p=P, w=W)
        flat = lambda t, n: t[:, n].rearrange("p w f -> p (w f)")

        @block.sync
        def _(sp):
            for n in range(PIECES):
                sp.dma_start(flat(a, n), view(a_rows)[n]).then_inc(s_a[n], 16)
                sp.dma_start(flat(b, n), view(b_rows)[n]).then_inc(s_a[n], 16)
            for n in range(PIECES):
                sp.wait_ge(s_norm, n + 1)
                sp.dma_start(view(out_rows)[n], flat(b, n)).then_inc(s_out, 16)
            sp.wait_ge(s_out, 16 * PIECES)

        @block.scalar
        def _(act):
            for n in range(PIECES):
                act.wait_ge(s_var, n + 1)
                nc.scalar.activation(var[:, n, :], var[:, n, :], ACT.Sqrt, bias=eps[:, 0:1],
                                     scale=1.0 / D).then_inc(s_sd, 1)

        @block.vector
        def _(v):
            steps = [0]

            def then(ins):
                steps[0] += 1
                ins.then_inc(s_v, 1)
                v.wait_ge(s_v, steps[0])

            then(v.memset(eps[:, :], EPS_LN))

            def finish(n):
                v.wait_ge(s_sd, n + 1)
                then(v.reciprocal(var[:, n, :], var[:, n, :]))
                r3 = var[:, n, :].unsqueeze(2).broadcast_to([P, W, D])
                v.tensor_tensor(b[:, n], a[:, n], r3, ALU.mult).then_inc(s_norm, 1)

            for n in range(PIECES):
                v.wait_ge(s_a[n], 32)
                then(v.tensor_tensor(a[:, n], a[:, n], b[:, n], ALU.add))
                then(v.tensor_reduce(mean[:, n, :], a[:, n], AX_X, ALU.add))
                then(v.tensor_scalar(mean[:, n, :], mean[:, n, :], 1.0 / D, None, ALU.mult))
                m3 = mean[:, n, :].unsqueeze(2).broadcast_to([P, W, D])
                then(v.tensor_tensor(a[:, n], a[:, n], m3, ALU.subtract))
                then(v.tensor_tensor(sq[:, :, :], a[:, n], a[:, n], ALU.mult))
                v.tensor_reduce(var[:, n, :], sq[:, :, :], AX_X, ALU.add).then_inc(s_var, 1)
                if n:
                    finish(n - 1)
            finish(PIECES - 1)


class PnaWeights:

    def __init__(self, sb):
        self.edge = sb("w_edge_feat", [FE, D])
        self.node = sb("w_node", [D, 2 * D])
        self.node_bias = sb("w_node_bias", [P, 1])
        self.source = sb("w_source", [D, D])
        self.wide = sb("w_wide", [P, 3, P])
        self.wide_x = sb("w_wide_x", [D, P])
        self.att = sb("w_att", [P, 3, D])
        self.lin = sb("w_lin", [P, D])
        self.post_bias = sb("w_post_bias", [D, 1])
        self.lin_bias = sb("w_lin_bias", [D, 1])
        self.gamma = sb("w_gamma", [D, 1])
        self.beta = sb("w_beta", [D, 1])


def pna_weights(chip, w, layer, We, be, Wp, bp, Wo, bo, Wl, bl, bn_g, bn_b):
    nc = chip.nc
    AGG = 5 * D
    with ExitStack() as ctx:
        sb, ps, sem = chip.scope(ctx)
        wp = sb("wp", [D, 3 * D])
        wo = sb("wo", [D, 16 * D])
        wl = sb("wl", [D, 2 * D])
        we = sb("we", [D, FE])
        be_c = sb("be_c", [D, 1])
        bp_c = sb("bp_c", [P, 1])
        embed = sb("embed", [D, 2 * D])
        p_t = ps("p_t", [P, 2, 8, D])
        p_e = ps("p_e", [P, CH])
        s_w = sem("s_w")
        s_t = sem("s_t")
        s_embed = sem("s_embed")
        s_fold = sem("s_fold")
        s_zero = sem("s_zero")
        block = ctx.enter_context(nc.Block())
        col = lambda t: t[layer].rearrange("(f a) -> f a", a=1)

        @block.sync
        def _(sp):
            blocks = lambda t: t.rearrange("f (b c) -> f b c", c=D)
            moved = [(blocks(wo[:, :])[:, to:16:5, :], blocks(Wo[layer])[:, of:16:5, :])
                     for to, of in ((1, 1), (2, 3), (3, 2), (4, 4), (5, 5))]
            loads = [(wp[:, :], Wp[layer]), (wo[:, 0:D], Wo[layer][:, 0:D]), *moved, (wl[:, 0:D], Wl[layer]),
                     (wl[:, D:], Wl[layer]), (we[:, :], We[layer]), (be_c[:, :], col(be)),
                     (bp_c[0:D, :], col(bp)), (bp_c[D:, :], col(bp)), (w.post_bias[:, :], col(bo)),
                     (w.lin_bias[:, :], col(bl)), (w.gamma[:, :], col(bn_g)), (w.beta[:, :], col(bn_b))]
            for to, of in loads:
                sp.dma_start(to, of).then_inc(s_w, 16)
            sp.wait_ge(s_w, 16 * len(loads))

        cuts = [(wp, 0, D), (wp, D, D), (wp, 2 * D, D), (wo, 0, D), (wl, 0, 2 * D)]
        for k in range(3):
            cuts += [(wo, D + k * AGG, 2 * D), (wo, 3 * D + k * AGG, 2 * D), (wo, 5 * D + k * AGG, D)]
        turned = lambda n, rows: p_t[rows, n // 8, n % 8, :]
        low, high, both = slice(0, D), slice(D, P), slice(0, P)

        @block.tensor
        def _(pe):
            pe.wait_ge(s_w, 16 * 17)
            for n, (t, at, m) in enumerate(cuts):
                last = pe.transpose(turned(n, slice(0, m)), t[:, at:at + m], chip.ident[0:D, 0:D])
            last.then_inc(s_t, 1)
            pe.wait_ge(s_embed, 1)
            pe.matmul(p_e[0:FE, 0:D], we[:, :], embed[:, 0:D], start=True, stop=True)
            pe.matmul(p_e[:, D:D + 1], embed[:, :], be_c[:, :], start=True, stop=True).then_inc(s_fold, 1)

        @block.scalar
        def _(act):
            act.wait_ge(s_t, 1)
            nc.scalar.copy(embed[:, D:], turned(2, low))
            nc.scalar.copy(embed[:, 0:D], turned(2, low)).then_inc(s_embed, 1)
            nc.scalar.copy(w.node[:, 0:D], turned(0, low))
            nc.scalar.copy(w.node[:, D:], turned(0, low))
            nc.scalar.copy(w.source[:, :], turned(1, low))
            nc.scalar.copy(w.lin[:, :], turned(4, both))
            act.wait_ge(s_zero, 1)
            nc.scalar.copy(w.wide_x[:, 0:D], turned(3, low))
            for k in range(3):
                pair = lambda i: (w.wide[:, i, k * D:k * D + D] if k < 2 else w.att[:, i, :])
                nc.scalar.copy(pair(0), turned(5 + 3 * k, both))
                nc.scalar.mul(pair(1)[low], turned(6 + 3 * k, low), -1.0)
                nc.scalar.copy(pair(1)[high], turned(6 + 3 * k, high))
                nc.scalar.copy(pair(2)[low], turned(7 + 3 * k, low))
            act.wait_ge(s_fold, 1)
            nc.scalar.copy(w.edge[:, :], p_e[0:FE, 0:D])
            nc.scalar.activation(w.node_bias[:, :], p_e[:, D:D + 1], ACT.Identity, bias=bp_c[:, 0:1])

        @block.vector
        def _(v):
            v.memset(w.wide_x[:, D:], 0.0).then_inc(s_zero, 1)


def source_table(chip, w, x_rows, q_rows):
    nc = chip.nc
    with ExitStack() as ctx:
        sb, ps, sem = chip.scope(ctx)
        xin = sb("xin", [P, 2, B, D])
        xt = sb("xt", [D, 2, CH])
        stage = sb("stage", [P, 2, B, D])
        p_x = ps("p_x", [D, 2, CH])
        p_q = ps("p_q", [P, 2, CH])
        s_in = [sem(f"s_in{i}") for i in (0, 1)]
        s_turn = sem("s_turn")
        s_xt = sem("s_xt")
        s_q = sem("s_q")
        s_end = sem("s_end")
        s_out = [sem(f"s_out{i}") for i in (0, 1)]
        block = ctx.enter_context(nc.Block())

        @block.sync
        def _(sp):
            def body(c, k, pars):
                for i in pars:
                    sp.wait_ge(s_end, c + 1)
                    sp.dma_start(xin[:, i], rows_of(x_rows, c + i)).then_inc(s_in[i], 16)
                for i in pars:
                    sp.wait_ge(s_end, c + i + 2)
                    sp.dma_start(rows_of(q_rows, c + i), stage[:, i]).then_inc(s_out[i], 16)

            by_pairs(sp, body)
            for i in (0, 1):
                sp.wait_ge(s_out[i], 16 + 16 * ((NCH + 1 - i) // 2))

        @block.tensor
        def _(pe):
            def body(c, k, pars):
                for i in pars:
                    pe.wait_ge(s_in[i], k * 16 + 16)
                    gate(pe)
                    for b in range(B):
                        t = pe.transpose(p_x[:, i, b * P:(b + 1) * P], xin[:, i, b, :], chip.ident[:, :])
                    t.then_inc(s_turn, 1)
                for i in pars:
                    pe.wait_ge(s_xt, c + i + 1)
                    gate(pe)
                    for b in range(B):
                        m = pe.matmul(p_q[:, i, b * D:(b + 1) * D], xt[:, i, b * P:(b + 1) * P], w.source[:, :],
                                      start=True, stop=True)
                    m.then_inc(s_q, 1)

            by_pairs(pe, body)

        @block.scalar
        def _(act):
            def body(c, k, pars):
                for i in pars:
                    act.wait_ge(s_turn, c + i + 1)
                    nc.scalar.copy(xt[:, i, :], p_x[:, i, :]).then_inc(s_xt, 1)

            by_pairs(act, body)

        @block.vector
        def _(v):
            for i in (0, 1):
                v.memset(stage[0:1, i, 0, 0:1], 0.0).then_inc(s_out[i], 16)
            v.memset(stage[0:1, 0, 1, 0:1], 0.0).then_inc(s_end, 1)

            def body(c, k, pars):
                for i in pars:
                    v.wait_ge(s_q, c + i + 1)
                    v.wait_ge(s_out[i], k * 16 + 16)
                    v.tensor_copy(stage[:, i, :, :],
                                  p_q[:, i, 0:B * D].rearrange("p (b f) -> p b f", b=B)).then_inc(s_end, 1)

            by_pairs(v, body)


def pna_pass(chip, w, q_rows, src_pad, ea_t, flags):
    nc = chip.nc
    acc = chip.acc2
    with ExitStack() as ctx:
        sb, ps, sem = chip.scope(ctx)
        idx = sb("idx", [P, SLOTS, G], I32)
        data = sb("data", [P, SLOTS, G, D])
        feat = sb("feat", [FE, 2, GE])
        flag = sb("flag", [1, 2, GE], BF16)
        ones = sb("ones", [1, P], BF16)
        t3 = sb("t3", [P, SLOTS, G, 3, D])
        reset = sb("reset", [P, 2, GE], BF16)
        run = sb("run", [P, 2, GE])
        back = sb("back", [P, G, P])
        hot = sb("hot", [P, 2, 2, G, P])
        scratch = sb("scratch", [1, 8])
        p_feat = ps("p_feat", [P, CH])
        p_flag = ps("p_flag", [P, GE])
        p_turn = ps("p_turn", [P, GE])
        p_back = ps("p_back", [P, GE])
        part = ps("part", [P, 2, 2, P])
        s_idx = [sem(f"s_idx{r}") for r in range(SLOTS)]
        s_edge = [sem(f"s_edge{i}") for i in (0, 1)]
        s_row = [sem(f"s_row{r}") for r in range(SLOTS)]
        s_ready = sem("s_ready")
        s_feat = sem("s_feat")
        s_t = sem("s_t")
        s_flag = sem("s_flag")
        s_reset = sem("s_reset")
        s_split = sem("s_split")
        s_turn = sem("s_turn")
        s_run = sem("s_run")
        s_back = sem("s_back")
        s_bcopy = sem("s_bcopy")
        s_hot = sem("s_hot")
        s_part = sem("s_part")
        s_added = sem("s_added")
        s_hot_x = sem("s_hot_x")
        s_part_x = sem("s_part_x")
        s_added_x = sem("s_added_x")
        block = ctx.enter_context(nc.Block())
        last_k = NG // SLOTS - 1

        def turns(eng, body):
            with eng.Fori(0, last_k) as k:
                for r in range(SLOTS):
                    body(k, r, True)
            for r in range(SLOTS):
                body(last_k, r, r < SLOTS - 1)

        @block.sync
        def _(sp):
            with sp.Fori(0, NG // SLOTS) as k:
                for r in range(SLOTS):
                    g = k * SLOTS + r
                    sp.wait_ge(s_t, g + 1)
                    sp.dma_start(idx[:, r, :].rearrange("p (h j) -> p h j", h=H),
                                 edge_views(src_pad, g)).then_inc(s_idx[r], 16)
                    sp.wait_ge(s_flag, g + 1)
                    sp.dma_start(feat[:, r % 2, :], ea_t[:, bass.ds(g * GE, GE)]).then_inc(s_edge[r % 2], 16)
                    sp.dma_start(flag[:, r % 2, :], flags[bass.ds(g * GE, GE)].rearrange("(a e) -> a e", a=1))\
                      .then_inc(s_edge[r % 2], 16)

        @block.gpsimd
        def _(pool):
            with pool.Fori(0, NG // SLOTS) as k:
                for r in range(SLOTS):
                    pool.wait_ge(s_idx[r], k * 16 + 16)
                    gate(pool)
                    for j in range(G):
                        pool.indirect_dma_start(
                            out=data[:, r, j, :], out_offset=None, in_=q_rows[:, :],
                            in_offset=bass.IndirectOffsetOnAxis(ap=idx[:, r, j:j + 1], axis=0),
                        ).then_inc(s_row[r], 16)

        @block.tensor
        def _(pe):
            def front(k, r):
                g = k * SLOTS + r
                pe.wait_ge(s_edge[r % 2], k * (32 * SLOTS // 2) + 32 * (r // 2) + 32)
                pe.wait_ge(s_t, g + SLOTS)
                gate(pe)
                for j in range(G):
                    at = (j // J) * CH + j % J
                    m = pe.matmul(p_feat[:, j * D:(j + 1) * D], feat[:, r % 2, at:at + CH - J + 1:J],
                                  w.edge[:, :], start=True, stop=True)
                m.then_inc(s_feat, 1)
                pe.wait_ge(s_reset, g + 1)
                gate(pe)
                for h in range(H):
                    m = pe.matmul(p_flag[:, h * CH:(h + 1) * CH], ones[:, :], flag[:, r % 2, h * CH:(h + 1) * CH],
                                  start=True, stop=True)
                m.then_inc(s_flag, 1)

            def turn_back(e, par):
                pe.wait_ge(s_run, e + 1)
                pe.wait_ge(s_bcopy, e + 1)
                gate(pe)
                for j in range(G):
                    at = (j // J) * CH + j % J
                    b = pe.transpose(p_back[:, j * P:(j + 1) * P], run[:, par, at:at + CH - J + 1:J],
                                     chip.ident[:, :])
                b.then_inc(s_back, 1)

            def sums(x, slot, par):
                for j in range(G):
                    pe.matmul(part[:, x, 0, :], t3[:, slot, j, 1:3, :].rearrange("p b f -> p (b f)"),
                              hot[:, par, 0, j, :], start=(j == 0), stop=(j == G - 1))

            def maxima(x, par):
                for j in range(G):
                    m = pe.matmul(part[:, x, 1, :], back[:, j, :], hot[:, par, 1, j, :],
                                  start=(j == 0), stop=(j == G - 1))
                return m

            def sum_stage(e, slot, turn=None):
                par = slot % 2
                turn_back(e, par)
                pe.wait_ge(s_hot, e + 1)
                pe.wait_ge(s_added, e + 1)
                gate(pe)
                sums(0, slot, par)
                if turn:
                    turn()
                pe.wait_ge(s_bcopy, e + 2)
                gate(pe)
                maxima(0, par).then_inc(s_part, 1)

                def more(n, x):
                    pe.wait_ge(s_hot_x, x)
                    pe.wait_ge(s_added_x, x)
                    gate(pe)
                    sums(1, slot, par)
                    maxima(1, par).then_inc(s_part_x, 1)

                further_windows(chip, pe, e, more)

            def body(k, r, has_next):
                i = k * SLOTS + r
                if has_next:
                    front(k + (r + 1) // SLOTS, (r + 1) % SLOTS)

                def turn():
                    pe.wait_ge(s_split, i + 1)
                    gate(pe)
                    for j in range(G):
                        at = (j // J) * CH + j % J
                        m = pe.transpose(p_turn[:, at:at + CH - J + 1:J],
                                         t3[:, r, j, 0:2, :].rearrange("p b f -> p (b f)"), chip.ident[:, :])
                    m.then_inc(s_turn, 1)

                sum_stage(i, (r + SLOTS - 1) % SLOTS, turn)

            pe.wait_ge(s_ready, 1)
            front(0, 0)
            turns(pe, body)
            sum_stage(NG, SLOTS - 1)

        @block.scalar
        def _(act):
            def copy_flags(g, r):
                act.wait_ge(s_flag, g + 3)
                act.wait_ge(s_run, g)
                nc.scalar.copy(reset[:, r % 2, :], p_flag[:, :]).then_inc(s_reset, 1)

            def split(g, r):
                act.wait_ge(s_t, g + 1 + SLOTS)
                t = t3[:, r, :, 1, :]
                nc.scalar.mul(t3[:, r, :, 0, :], t, -1.0)
                nc.scalar.activation(t3[:, r, :, 2, :], t, ACT.Square).then_inc(s_split, 1)

            def copy_back(e):
                act.wait_ge(s_back, e + 1)
                nc.scalar.copy(back[:, :, :].rearrange("p j f -> p (j f)"), p_back[:, :]).then_inc(s_bcopy, 1)

            def body(k, r, has_next):
                i = k * SLOTS + r
                if has_next:
                    copy_flags(i + 1, r + 1)
                copy_back(i)
                if has_next:
                    split(i + 1, (r + 1) % SLOTS)

            act.wait_ge(s_flag, 3)
            nc.scalar.copy(reset[:, 0, :], p_flag[:, :]).then_inc(s_reset, 1)
            split(0, 0)
            turns(act, body)
            copy_back(NG)

        @block.vector
        def _(v):
            def make_t(k, r):
                g = k * SLOTS + r
                v.wait_ge(s_row[r], k * 16 * G + 16 * G)
                v.wait_ge(s_feat, g + 1)
                v.tensor_tensor(t3[:, r, :, 1, :], data[:, r, :, :],
                                p_feat[:, :].rearrange("p (j f) -> p j f", j=G), ALU.add).then_inc(s_t, 1)

            def add(base, n, x):
                at = v.snap((base + n * P).with_bounds(min_val=0, max_val=NP - P))
                return v.tensor_tensor(acc[:, :, bass.ds(at, P)], acc[:, :, bass.ds(at, P)], part[:, x], ALU.add)

            def finish(e, par):
                base = load_entry(chip, v, 2, e, 0, N)
                v.wait_ge(s_part, e + 1)
                v.wait_ge(s_added, e + 1)
                add(base, 0, 0).then_inc(s_added, 1)

                def more(n, x):
                    v.wait_ge(s_added, e + 2)
                    build_hot(chip, v, hot[:, par, 0], chip.dst, e, n)
                    build_hot(chip, v, hot[:, par, 1], chip.last, e, n).then_inc(s_hot_x, 1)
                    v.wait_ge(s_part_x, x)
                    add(base, n, 1).then_inc(s_added_x, 1)
                    v.wait_ge(s_added_x, x + 1)

                further_windows(chip, v, e, more)

            def body(k, r, has_next):
                i = k * SLOTS + r
                if has_next:
                    make_t(k + (r + 1) // SLOTS, (r + 1) % SLOTS)
                build_hot(chip, v, hot[:, r % 2, 0], chip.dst, i + 1)
                build_hot(chip, v, hot[:, r % 2, 1], chip.last, i + 1).then_inc(s_hot, 1)
                v.wait_ge(s_turn, i + 1)
                v.wait_ge(s_reset, i + 2)
                v.wait_ge(s_run, i + 1)
                v.tensor_tensor_scan(run[:, r % 2, :], reset[:, r % 2, :], p_turn[:, :],
                                     run[:, (r + 1) % 2, GE - 1:GE], ALU.add, ALU.max).then_inc(s_run, 1)
                finish(i, (r + 1) % 2)

            v.memset(acc[:, :, :], 0.0).then_inc(s_added, 1)
            v.memset(t3[:, SLOTS - 1], 0.0)
            v.memset(hot[:, 1], 0.0).then_inc(s_hot, 1)
            v.memset(ones[:, :], 1.0).then_inc(s_ready, 1)
            v.memset(run[:, 1, :], 0.0).then_inc(s_run, 1)
            for n, (s, count) in enumerate(((s_flag, 2), (s_reset, 1), (s_bcopy, 1), (s_added_x, 1), (s_t, SLOTS))):
                v.memset(scratch[:, n:n + 1], 0.0).then_inc(s, count)
            make_t(0, 0)
            turns(v, body)
            finish(NG, 1)


def pna_nodes(chip, w, x_rows, cnt_row):
    nc = chip.nc
    acc = chip.acc2
    low, high = slice(0, D), slice(D, P)
    with ExitStack() as ctx:
        sb, ps, sem = chip.scope(ctx)
        xin = sb("xin", [P, 2, B, D])
        xt = sb("xt", [D, 2, CH])
        cnt = sb("cnt", [P, 2, CH])
        pn = sb("pn", [P, 2, CH])
        rden = sb("rden", [P, 2, CH])
        has = sb("has", [P, 2, CH])
        log = sb("log", [P, 2, CH])
        mom = sb("mom", [P, 2, CH])
        stat_a = sb("stat_a", [P, 2, CH])
        stat_b = sb("stat_b", [P, 2, CH])
        stat_c = sb("stat_c", [D, 2, CH])
        z = sb("z", [P, 2, CH])
        z2 = sb("z2", [D, 2, CH])
        eps = sb("eps", [P, 1])
        one = sb("one", [P, 1])
        p_a = ps("p_a", [P, 2, CH])
        p_b = ps("p_b", [P, 2, CH])
        p_c = ps("p_c", [P, 2, CH])
        s_in = [sem(f"s_in{i}") for i in (0, 1)]
        names = "turn xt pn_p pn deg has den rden mom log ilog sq dv var sd hasp cp stats post z zz lin end eps".split()
        s = {name: sem("s_" + name) for name in names}
        block = ctx.enter_context(nc.Block())

        @block.sync
        def _(sp):
            def body(c, k, pars):
                for i in pars:
                    sp.wait_ge(s["end"], c + 1)
                    sp.dma_start(xin[:, i], rows_of(x_rows, c + i)).then_inc(s_in[i], 16)
                    sp.dma_start(cnt[:, i, :], cnt_row[bass.ds((c + i) * CH, CH)].rearrange("(a n) -> a n", a=1)
                                 .broadcast_to([P, CH])).then_inc(s_in[i], 16)

            by_pairs(sp, body)

        @block.tensor
        def _(pe):
            def body(c, k, pars):
                for i in pars:
                    pe.wait_ge(s_in[i], k * 32 + 32)
                    gate(pe)
                    for b in range(B):
                        t = pe.transpose(p_a[0:D, i, b * P:(b + 1) * P], xin[:, i, b, :], chip.ident[:, :])
                    t.then_inc(s["turn"], 1)
                for i in pars:
                    pe.wait_ge(s["xt"], c + i + 1)
                    gate(pe)
                    pe.matmul(p_b[:, i, :], w.node[:, :], xt[:, i, :], start=True, stop=True).then_inc(s["pn_p"], 1)
                for i in pars:
                    pe.wait_ge(s["stats"], c + i + 1)
                    pe.wait_ge(s["sd"], c + i + 1)
                    gate(pe)
                    for p_out, ws, m in ((p_c, w.wide, P), (p_a, w.att, D)):
                        if m == P:
                            pe.matmul(p_out[:, i, :], w.wide_x[:, :], xt[:, i, :], start=True, stop=False)
                        pe.matmul(p_out[0:m, i, :], ws[:, 0, :], stat_a[:, i, :], start=(m == D), stop=False)
                        pe.matmul(p_out[0:m, i, :], ws[:, 1, :], stat_b[:, i, :], start=False, stop=False)
                        t = pe.matmul(p_out[0:m, i, :], ws[0:D, 2, :], stat_c[:, i, :], start=False, stop=True)
                    t.then_inc(s["post"], 1)
                for i in pars:
                    pe.wait_ge(s["z"], c + i + 1)
                    pe.wait_ge(s["zz"], c + i + 1)
                    gate(pe)
                    pe.matmul(p_b[0:D, i, :], w.lin[:, :], z[:, i, :], start=True, stop=False)
                    pe.matmul(p_b[0:D, i, :], w.lin[0:D, :], z2[:, i, :], start=False, stop=True)\
                      .then_inc(s["lin"], 1)

            by_pairs(pe, body)

        @block.scalar
        def _(act):
            act.wait_ge(s["eps"], 2)

            def body(c, k, pars):
                for i in pars:
                    act.wait_ge(s["turn"], c + i + 1)
                    nc.scalar.copy(xt[:, i, :], p_a[0:D, i, :]).then_inc(s["xt"], 1)
                for i in pars:
                    act.wait_ge(s["deg"], c + i + 1)
                    nc.scalar.activation(log[:, i, :], log[:, i, :], ACT.Ln, bias=one[:, 0:1]).then_inc(s["log"], 1)
                for i in pars:
                    act.wait_ge(s["pn_p"], c + i + 1)
                    nc.scalar.activation(pn[:, i, :], p_b[:, i, :], ACT.Identity,
                                         bias=w.node_bias[:, 0:1]).then_inc(s["pn"], 1)
                for i in pars:
                    act.wait_ge(s["mom"], c + i + 1)
                    nc.scalar.activation(stat_b[high, i, :], mom[low, i, :], ACT.Square).then_inc(s["sq"], 1)
                for i in pars:
                    act.wait_ge(s["var"], c + i + 1)
                    nc.scalar.activation(stat_b[high, i, :], stat_b[high, i, :], ACT.Sqrt,
                                         bias=eps[high, 0:1]).then_inc(s["sd"], 1)
                for i in pars:
                    act.wait_ge(s["post"], c + i + 1)
                    nc.scalar.activation(z[low, i, :], p_c[low, i, :], ACT.Identity,
                                         bias=w.post_bias[:, 0:1]).then_inc(s["z"], 1)
                for i in pars:
                    act.wait_ge(s["lin"], c + i + 1)
                    nc.scalar.activation(acc[low, 0, bass.ds((c + i) * CH, CH)], p_b[low, i, :], ACT.Identity,
                                         bias=w.lin_bias[:, 0:1]).then_inc(s["end"], 1)

            by_pairs(act, body)

        @block.vector
        def _(v):
            v.memset(eps[:, :], EPS_STD).then_inc(s["eps"], 1)
            v.memset(one[:, :], 1.0).then_inc(s["eps"], 1)
            v.memset(z[0:1, 0, 0:1], 0.0).then_inc(s["end"], 1)

            def body(c, k, pars):
                span = lambda i: bass.ds((c + i) * CH, CH)
                for i in pars:
                    v.wait_ge(s_in[i], k * 32 + 32)
                    v.tensor_scalar(log[:, i, :], cnt[:, i, :], 1.0, None, ALU.max).then_inc(s["deg"], 1)
                    v.tensor_scalar(has[:, i, :], cnt[:, i, :], 1.0, None, ALU.min).then_inc(s["has"], 1)
                    v.tensor_scalar(mom[:, i, :], cnt[:, i, :], 1.0, None, ALU.max).then_inc(s["den"], 1)
                for i in pars:
                    v.wait_ge(s["den"], c + i + 1)
                    v.reciprocal(rden[:, i, :], mom[:, i, :]).then_inc(s["rden"], 1)
                for i in pars:
                    v.wait_ge(s["rden"], c + i + 1)
                    v.tensor_tensor(mom[:, i, :], acc[:, 0, span(i)], rden[:, i, :], ALU.mult)\
                     .then_inc(s["mom"], 1)
                for i in pars:
                    v.wait_ge(s["log"], c + i + 1)
                    v.wait_ge(s["mom"], c + i + 1)
                    v.reciprocal(rden[low, i, :], log[low, i, :]).then_inc(s["ilog"], 1)
                for i in pars:
                    v.wait_ge(s["sq"], c + i + 1)
                    v.scalar_tensor_tensor(out=stat_b[high, i, :], in0=stat_b[high, i, :], scalar=-1.0,
                                           in1=mom[high, i, :], op0=ALU.mult, op1=ALU.add).then_inc(s["dv"], 1)
                for i in pars:
                    v.wait_ge(s["dv"], c + i + 1)
                    v.tensor_scalar(stat_b[high, i, :], stat_b[high, i, :], 0.0, None, ALU.max)\
                     .then_inc(s["var"], 1)
                for i in pars:
                    v.wait_ge(s["pn"], c + i + 1)
                    v.wait_ge(s["has"], c + i + 1)
                    v.tensor_tensor(has[:, i, :], has[:, i, :], pn[:, i, :], ALU.mult).then_inc(s["hasp"], 1)
                    v.tensor_tensor(stat_c[:, i, :], cnt[low, i, :], pn[low, i, :], ALU.mult)\
                     .then_inc(s["cp"], 1)
                for i in pars:
                    v.wait_ge(s["hasp"], c + i + 1)
                    v.wait_ge(s["mom"], c + i + 1)
                    v.tensor_tensor(stat_a[low, i, :], has[low, i, :], mom[low, i, :], ALU.add)
                    v.tensor_tensor(stat_a[high, i, :], has[high, i, :], acc[high, 1, span(i)], ALU.add)
                    v.tensor_tensor(stat_b[low, i, :], acc[low, 1, span(i)], has[low, i, :], ALU.subtract)
                    v.wait_ge(s["cp"], c + i + 1)
                    v.tensor_tensor(stat_c[:, i, :], stat_c[:, i, :], acc[low, 0, span(i)], ALU.add)\
                     .then_inc(s["stats"], 1)
                for i in pars:
                    v.wait_ge(s["post"], c + i + 1)
                    v.wait_ge(s["ilog"], c + i + 1)
                    v.scalar_tensor_tensor(out=z[high, i, :], in0=p_c[high, i, :], scalar=1.0 / AVG_LOG,
                                           in1=log[high, i, :], op0=ALU.mult, op1=ALU.mult)
                    v.scalar_tensor_tensor(out=z2[:, i, :], in0=p_a[low, i, :], scalar=AVG_LOG,
                                           in1=rden[low, i, :], op0=ALU.mult, op1=ALU.mult).then_inc(s["zz"], 1)

            by_pairs(v, body)


def batch_norm_stats(chip, w, scale, shift):
    nc = chip.nc
    x = chip.acc2[0:D, 0, 0:N]
    with ExitStack() as ctx:
        sb, ps, sem = chip.scope(ctx)
        c = sb("c", [D, 6])
        s_v = sem("s_v")
        s_mean = sem("s_mean")
        s_sd = sem("s_sd")
        s_sq = sem("s_sq")
        block = ctx.enter_context(nc.Block())

        @block.vector
        def _(v):
            v.memset(c[:, 5:6], EPS_BN)
            v.tensor_reduce(c[:, 0:1], x, AX_X, ALU.add).then_inc(s_v, 1)
            v.wait_ge(s_v, 1)
            v.tensor_scalar(c[:, 1:2], c[:, 0:1], -1.0 / N, None, ALU.mult).then_inc(s_mean, 1)
            v.wait_ge(s_sd, 1)
            v.reciprocal(c[:, 4:5], c[:, 3:4]).then_inc(s_v, 1)
            v.wait_ge(s_v, 2)
            v.tensor_tensor(scale[:, :], c[:, 4:5], w.gamma[:, :], ALU.mult).then_inc(s_v, 1)
            v.wait_ge(s_v, 3)
            v.scalar_tensor_tensor(out=shift[:, :], in0=scale[:, :], scalar=c[:, 1:2], in1=w.beta[:, :],
                                   op0=ALU.mult, op1=ALU.add)

        @block.scalar
        def _(act):
            act.wait_ge(s_mean, 1)
            nc.scalar.activation(chip.acc2[0:D, 1, 0:N], x, ACT.Square, bias=c[:, 1:2],
                                 accum_out=c[:, 2:3]).then_inc(s_sq, 1)
            act.wait_ge(s_sq, 1)
            nc.scalar.activation(c[:, 3:4], c[:, 2:3], ACT.Sqrt, bias=c[:, 5:6], scale=1.0 / N).then_inc(s_sd, 1)


def batch_norm_rows(chip, scale, shift, out_rows):
    nc = chip.nc
    with ExitStack() as ctx:
        sb, ps, sem = chip.scope(ctx)
        xt = sb("xt", [D, 2, CH])
        stage = sb("stage", [P, 2, B, D])
        p_x = ps("p_x", [P, 2, CH])
        s_x = sem("s_x")
        s_turn = sem("s_turn")
        s_end = sem("s_end")
        s_out = [sem(f"s_out{i}") for i in (0, 1)]
        block = ctx.enter_context(nc.Block())

        @block.scalar
        def _(act):
            def body(c, k, pars):
                for i in pars:
                    act.wait_ge(s_end, c + 1)
                    nc.scalar.activation(xt[:, i, :], chip.acc2[0:D, 0, bass.ds((c + i) * CH, CH)], ACT.Relu,
                                         bias=shift[:, 0:1], scale=scale[:, 0:1]).then_inc(s_x, 1)

            by_pairs(act, body)

        @block.tensor
        def _(pe):
            def body(c, k, pars):
                for i in pars:
                    pe.wait_ge(s_x, c + i + 1)
                    gate(pe)
                    for b in range(B):
                        t = pe.transpose(p_x[:, i, b * D:(b + 1) * D], xt[:, i, b * P:(b + 1) * P],
                                         chip.ident[0:D, 0:D])
                    t.then_inc(s_turn, 1)

            by_pairs(pe, body)

        @block.vector
        def _(v):
            for i in (0, 1):
                v.memset(stage[0:1, i, 0, 0:1], 0.0).then_inc(s_out[i], 16)
            v.memset(stage[0:1, 0, 1, 0:1], 0.0).then_inc(s_end, 1)

            def body(c, k, pars):
                for i in pars:
                    v.wait_ge(s_turn, c + i + 1)
                    v.wait_ge(s_out[i], k * 16 + 16)
                    v.tensor_copy(stage[:, i, :, :],
                                  p_x[:, i, 0:B * D].rearrange("p (b f) -> p b f", b=B)).then_inc(s_end, 1)

            by_pairs(v, body)

        @block.sync
        def _(sp):
            def body(c, k, pars):
                for i in pars:
                    sp.wait_ge(s_end, c + i + 2)
                    sp.dma_start(rows_of(out_rows, c + i), stage[:, i]).then_inc(s_out[i], 16)

            by_pairs(sp, body)
            for i in (0, 1):
                sp.wait_ge(s_out[i], 16 + 16 * ((NCH + 1 - i) // 2))


def save_counts(chip, cnt_row):
    nc = chip.nc
    with ExitStack() as ctx:
        sb, ps, sem = chip.scope(ctx)
        s_cnt = sem("s_cnt")
        block = ctx.enter_context(nc.Block())

        @block.sync
        def _(sp):
            sp.dma_start(cnt_row.rearrange("(a n) -> a n", a=1), chip.acc[KC - 1:KC, :]).then_inc(s_cnt, 16)
            sp.wait_ge(s_cnt, 16)


def gnn(nc, x_pad, src_pad, dst_pad, ea_pad, ea_t, W1, b1, W2, b2, W3, b3, We, be, Wp, bp, Wo, bo, Wl, bl,
        bn_g, bn_b, out):
    chip = Chip(nc)
    flags = nc.dram_tensor("flags", [EP], BF16, kind="Internal").ap()
    cnt_row = nc.dram_tensor("cnt_row", [NP], F32, kind="Internal").ap()
    h1 = nc.dram_tensor("h1_rows", [NP, D], F32, kind="Internal").ap()
    h2 = nc.dram_tensor("h2_rows", [NP, D], F32, kind="Internal").ap()
    h3 = nc.dram_tensor("h3_rows", [NP, D], F32, kind="Internal").ap()
    x1 = nc.dram_tensor("x1_rows", [NP, D], F32, kind="Internal").ap()
    x2 = nc.dram_tensor("x2_rows", [NP, D], F32, kind="Internal").ap()
    x3 = nc.dram_tensor("x3_rows", [NP, D], F32, kind="Internal").ap()
    q_rows = nc.dram_tensor("q_rows", [NP, D], F32, kind="Internal").ap()
    with ExitStack() as ctx:
        sb, ps, sem = chip.scope(ctx)
        chip.ramp = sb("ramp", [P, P])
        chip.shifts = sb("shifts", [P, NP // P])
        chip.ident = sb("ident", [P, P])
        chip.dst = sb("dst", [P, NG + 1, G])
        chip.last = sb("last", [P, NG + 1, G])
        chip.regs = sb("regs", [1, 3, NG + 1], I32)
        prepare(chip, dst_pad, flags)
        with ExitStack() as l0:
            sb, ps, sem = chip.scope(l0)
            chip.acc = sb("acc", [P, NP])
            sum_pass(chip, x_pad, src_pad, ea_pad, True)
            conv_nodes(chip, x_pad, W1, b1, h1, True)
            sum_pass(chip, h1, src_pad, ea_pad, False)
            conv_nodes(chip, h1, W2, b2, h2, True)
            sum_pass(chip, h2, src_pad, ea_pad, False)
            conv_nodes(chip, h2, W3, b3, h3, False)
            save_counts(chip, cnt_row)
        residual_norm(chip, x_pad, h3, x1)
        with ExitStack() as l1:
            sb, ps, sem = chip.scope(l1)
            chip.acc2 = sb("acc2", [P, 2, NP])
            scale = sb("scale", [D, 1])
            shift = sb("shift", [D, 1])
            w = PnaWeights(sb)
            for layer, (x_rows, y_rows) in enumerate(((x1, x2), (x2, x3))):
                pna_weights(chip, w, layer, We, be, Wp, bp, Wo, bo, Wl, bl, bn_g, bn_b)
                source_table(chip, w, x_rows, q_rows)
                pna_pass(chip, w, q_rows, src_pad, ea_t, flags)
                pna_nodes(chip, w, x_rows, cnt_row)
                batch_norm_stats(chip, w, scale, shift)
                batch_norm_rows(chip, scale, shift, y_rows)
        residual_norm(chip, x1, x3, out)


_NAMES = ["L0_gnn_W1", "L0_gnn_b1", "L0_gnn_W2", "L0_gnn_b2", "L0_gnn_W3", "L0_gnn_b3",
          "L1_gnn_W_edge", "L1_gnn_b_edge", "L1_gnn_W_pre", "L1_gnn_b_pre", "L1_gnn_W_post",
          "L1_gnn_b_post", "L1_gnn_W_lin", "L1_gnn_b_lin", "L1_gnn_bn_gamma", "L1_gnn_bn_beta"]


def kernel(**inputs):
    import numpy as _np
    import concourse.bacc as _bacc
    from concourse import mybir as _mybir
    from concourse.bass_utils import run_bass_kernel_spmd as _run

    nc = _bacc.Bacc("TRN2", target_bir_lowering=False, num_devices=1)
    x = _np.asarray(inputs["x"])
    ea = _np.asarray(inputs["edge_attr_16"])
    src = _np.asarray(inputs["src"])
    dst = _np.asarray(inputs["dst"])
    arrays_in = {
        "x_pad": _np.concatenate([x, _np.zeros((NP - N, D), x.dtype)]),
        "src_pad": _np.concatenate([src, _np.zeros((EP - E,), src.dtype)]),
        "dst_pad": _np.concatenate([_np.full((1,), -1, dst.dtype), dst, _np.full((EP - E,), N, dst.dtype),
                                    _np.full((1,), N + 1, dst.dtype)]),
        "ea_pad": _np.concatenate([ea, _np.zeros((EP - E, FE), ea.dtype)]),
    }
    arrays_in["ea_t"] = _np.ascontiguousarray(arrays_in["ea_pad"].T)
    for name in _NAMES:
        arrays_in[name] = _np.ascontiguousarray(inputs[name])
    arrays, args = {}, []
    for name, a in arrays_in.items():
        arrays[f"in_{name}"] = a
        args.append(nc.dram_tensor(f"in_{name}", a.shape, _mybir.dt.from_np(a.dtype), kind="ExternalInput").ap())
    args.append(nc.dram_tensor("out_0", (NP, D), _mybir.dt.float32, kind="ExternalOutput").ap())
    gnn(nc, *args)
    r = _run(nc, [arrays], core_ids=[0])
    return r.results[0]["out_0"][:N]
```

```python
from contextlib import ExitStack

import numpy as np
import concourse.bass as bass
from concourse import mybir

F32 = mybir.dt.float32
I32 = mybir.dt.int32
I16 = mybir.dt.int16
BF16 = mybir.dt.bfloat16
ALU = mybir.AluOpType
ACT = mybir.ActivationFunctionType
AX_X = mybir.AxisListType.X

N, E, D, FE = 12500, 212500, 64, 16
P = 128
G = 8
H = 2
J = G // H
GE = G * P
SLOTS = 4
NG = -(-E // (GE * SLOTS)) * SLOTS
EP = NG * GE
CH = 512
NCH = -(-N // CH)
NP = NCH * CH
assert N + P <= NP
B = CH // P
BLOCKS = -(-N // P)
TURNS = NG // SLOTS
KC = D + FE + 1
RESET = -float(2.0 ** 127)
EPS_LN = 1e-5
EPS_STD = 1e-5
EPS_BN = 1e-5
AVG_LOG = float(np.log(17.0))
LAYERS = 2


def gate(eng):
    eng.nop(nofuse=True)


class Chip:

    def __init__(self, nc):
        self.nc = nc
        self.n = 0

    def scope(self, ctx):
        nc = self.nc
        self.n += 1
        tag = f"_{self.n}"
        sb = lambda name, shape, dt=F32: ctx.enter_context(nc.sbuf_tensor(name + tag, shape, dt))
        ps = lambda name, shape, dt=F32: ctx.enter_context(nc.psum_tensor(name + tag, shape, dt))
        sems = []

        def sem(name):
            sems.append(nc.alloc_semaphore(name + tag))
            return sems[-1]

        def close():
            if sems:
                nc.clear_and_free_semaphores(sems)
                nc.all_engine_barrier()

        ctx.callback(close)
        return sb, ps, sem


class PnaWeights:

    def __init__(self, sb):
        self.edge = sb("w_edge_feat", [FE, D])
        self.node = sb("w_node", [D + 1, 2 * D])
        self.source = sb("w_source", [D, D])
        self.post = sb("w_post", [P, 3, 3 * D])
        self.post_bias = sb("w_post_bias", [D, 1])
        self.gamma = sb("w_gamma", [D, 1])
        self.beta = sb("w_beta", [D, 1])


class WeightSteps:

    def __init__(self, sb, sem, shared, w, layer, weights):
        We, be, Wp, bp, Wo, bo, Wl, bl, bn_g, bn_b = (t[layer] for t in weights)
        self.w = w
        self.p_t, self.p_fold, self.p_e = shared
        name = lambda n: f"{n}{layer}"
        self.wp = sb(name("wp"), [D, 3 * D])
        self.wo = sb(name("wo"), [D, 18, D])
        self.wl = sb(name("wl"), [D, D])
        self.wl_t = sb(name("wl_t"), [D, D])
        self.we = sb(name("we"), [D, FE])
        self.be_c = sb(name("be_c"), [D + 1, 1])
        self.bo_c = sb(name("bo_c"), [D, 1])
        self.bl_c = sb(name("bl_c"), [D, 1])
        self.embed = sb(name("embed"), [D + 1, D])
        self.s_w = sem(name("s_w"))
        self.s_t = sem(name("s_t"))
        self.s_embed = sem(name("s_embed"))
        self.s_fold = sem(name("s_fold"))
        self.s_one = sem(name("s_one"))
        self.s_done = sem(name("s_done"))
        col = lambda t: t.rearrange("(f a) -> f a", a=1)
        wo, theirs = self.wo, Wo.rearrange("f (b c) -> f b c", c=D)
        self.loads = [(self.wp[:, :], Wp), (self.wl[:, :], Wl), (self.we[:, :], We), (self.be_c[0:D, :], col(be)),
                      (self.embed[D:, :], bp.rearrange("(a f) -> a f", a=1)), (self.bo_c[:, :], col(bo)),
                      (self.bl_c[:, :], col(bl)), (w.gamma[:, :], col(bn_g)), (w.beta[:, :], col(bn_b)),
                      (wo[:, 5, :], theirs[:, 0, :])]
        self.loads += [(wo[:, to:18:6, :], theirs[:, of:16:5, :]) for to, of in enumerate((1, 3, 2, 4, 5))]
        self.parts = [(k, m, P if m < 2 or k == 0 else D) for k in range(3) for m in range(3)]

    def folded(self, n, rows):
        return self.p_fold[rows, n // 8, n % 8, :]

    def load(self, eng):
        for to, of in self.loads:
            eng.dma_start(to, of).then_inc(self.s_w, 16)

    def tensor(self, pe, ident):
        p_t, p_e, wl_t, embed = self.p_t, self.p_e, self.wl_t, self.embed
        pe.wait_ge(self.s_w, 16 * len(self.loads))
        for n in range(3):
            pe.transpose(p_t[:, n, :], self.wp[:, n * D:(n + 1) * D], ident[0:D, 0:D])
        pe.transpose(p_t[:, 3, :], self.wl[:, :], ident[0:D, 0:D]).then_inc(self.s_t, 1)
        pe.wait_ge(self.s_embed, 1)
        pe.wait_ge(self.s_one, 2)
        for n, (k, m, rows) in enumerate(self.parts):
            at = self.wo[:, 6 * k + 2 * m:6 * k + 2 * m + rows // D, :].rearrange("f b c -> f (b c)")
            pe.matmul(self.folded(n, slice(0, rows)), at, wl_t[:, :], start=True, stop=True)
        pe.matmul(p_e[0:FE, 0:D], self.we[:, :], embed[0:D, :], start=True, stop=True)
        pe.matmul(p_e[0:1, D:2 * D], self.be_c[:, :], embed[:, :], start=True, stop=True)
        pe.matmul(p_e[0:D, 2 * D:2 * D + 1], wl_t[:, :], self.bo_c[:, :], start=True, stop=True)\
          .then_inc(self.s_fold, 1)

    def scalar(self, nc, act):
        w, p_t, p_e = self.w, self.p_t, self.p_e
        low, high = slice(0, D), slice(D, P)
        act.wait_ge(self.s_t, 1)
        nc.scalar.copy(self.wl_t[:, :], p_t[:, 3, :])
        nc.scalar.copy(self.embed[0:D, :], p_t[:, 2, :]).then_inc(self.s_embed, 1)
        nc.scalar.copy(w.node[0:D, 0:D], p_t[:, 0, :])
        nc.scalar.copy(w.node[0:D, D:], p_t[:, 0, :])
        nc.scalar.copy(w.source[:, :], p_t[:, 1, :])
        act.wait_ge(self.s_fold, 1)
        act.wait_ge(self.s_one, 2)
        for n, (k, m, rows) in enumerate(self.parts):
            to = lambda half: w.post[half, m, k * D:(k + 1) * D]
            if m == 1:
                nc.scalar.mul(to(low), self.folded(n, low), -1.0)
                nc.scalar.copy(to(high), self.folded(n, high))
            else:
                nc.scalar.copy(to(slice(0, rows)), self.folded(n, slice(0, rows)))
        nc.scalar.copy(w.edge[:, :], p_e[0:FE, 0:D])
        nc.scalar.copy(w.node[D:, 0:D], p_e[0:1, D:2 * D])
        nc.scalar.copy(w.node[D:, D:], p_e[0:1, D:2 * D])
        nc.scalar.activation(w.post_bias[:, :], p_e[0:D, 2 * D:2 * D + 1], ACT.Identity,
                             bias=self.bl_c[:, 0:1]).then_inc(self.s_done, 1)

    def vector(self, v):
        v.memset(self.be_c[D:, :], 1.0).then_inc(self.s_one, 1)
        v.memset(self.w.post[D:, 2, D:], 0.0).then_inc(self.s_one, 1)


def prepare(chip, dst_pad, flags, ws, weights):
    nc = chip.nc
    halves = [(t, min(P, NG - t * P)) for t in range(-(-NG // P))]
    with ExitStack() as ctx:
        sb, ps, sem = chip.scope(ctx)
        prev = sb("prev", [P, 2, GE], I32)
        cur = sb("cur", [P, 2, GE], I32)
        nxt = sb("nxt", [P, 2, GE], I32)
        first = sb("first", [P, 2])
        rel = sb("rel", [P, 2, GE])
        change = sb("change", [P, 2, GE])
        mark = sb("mark", [P, 2, GE])
        last = sb("last_row", [P, 2, GE])
        begin = sb("begin", [P, 2, GE])
        start = sb("start", [P, 2, GE], BF16)
        rows = sb("rows", [1, 2, NG], I32)
        span = sb("span", [1, 2, NG], I32)
        wf = sb("wf", [1, 6, NG + 1])
        p_table = ps("p_table", [P, 2, G, P])
        s_cur = sem("s_cur")
        s_nxt = sem("s_nxt")
        s_prev = sem("s_prev")
        s_rows = sem("s_rows")
        s_flags = sem("s_flags")
        s_v = sem("s_v")
        s_zero = sem("s_zero")
        s_ident = sem("s_ident")
        s_table = sem("s_table")
        s_begin = sem("s_begin")
        s_start = sem("s_start")
        s_turn = sem("s_turn")
        s_copy = sem("s_copy")
        shared = [ps("p_t", [D, 8, D]), ps("p_fold", [P, 2, 8, D]), ps("p_e", [P, CH])]
        steps = [WeightSteps(sb, sem, shared, w, layer, weights) for layer, w in enumerate(ws)]
        block = ctx.enter_context(nc.Block())
        line = lambda shift, t, n: (dst_pad[shift + t * P * GE:shift + (t * P + n) * GE]
                                    .rearrange("(g e) -> g e", e=GE))

        @block.sync
        def _(sp):
            heads = dst_pad[1:1 + EP].rearrange("(a g e) -> a g e", a=1, e=GE)
            for tile, shift, s in ((cur, 1, s_cur), (nxt, 2, s_nxt), (prev, 0, s_prev)):
                for t, n in halves:
                    sp.dma_start(tile[0:n, t, :], line(shift, t, n)).then_inc(s, 16)
            sp.dma_start(rows[:, 0, :], heads[:, :, 0], allow_slow_non_contiguous=True).then_inc(s_rows, 16)
            sp.dma_start(rows[:, 1, :], heads[:, :, GE - 1], allow_slow_non_contiguous=True).then_inc(s_rows, 16)
            steps[0].load(sp)
            sp.wait_ge(s_start, 2)
            for t, n in halves:
                sp.dma_start(flags[t * P * GE:(t * P + n) * GE].rearrange("(g e) -> g e", e=GE),
                             start[0:n, t, :]).then_inc(s_flags, 16)
            sp.wait_ge(s_flags, 32)

        @block.gpsimd
        def _(pool):
            pool.memset(chip.ident[:, :], 0.0).then_inc(s_zero, 1)
            pool.iota(chip.ramp[:, :], [[1, P]], base=0, channel_multiplier=0,
                      allow_small_or_imprecise_dtypes=True)
            pool.iota(chip.shifts[:, :], [[-P, NP // P]], base=0, channel_multiplier=0,
                      allow_small_or_imprecise_dtypes=True)
            pool.wait_ge(s_zero, 1)
            pool.affine_select(out=chip.ident[:, :], in_=chip.ident[:, :], compare_op=ALU.not_equal,
                               fill=1.0, base=0, pattern=[[-1, P]], channel_multiplier=1).then_inc(s_ident, 1)
            for step in steps[1:]:
                step.load(pool)

        @block.vector
        def _(v):
            done = [0]

            def then(ins, wait=True):
                done[0] += 1
                ins.then_inc(s_v, 1)
                if wait:
                    v.wait_ge(s_v, done[0])

            for step in steps:
                step.vector(v)
            v.memset(chip.last[:, 0, :], -1.0)
            v.wait_ge(s_cur, 32)
            for t, n in halves:
                then(v.tensor_copy(first[0:n, t:t + 1], cur[0:n, t, 0:1]), wait=t == 1)
            for t, n in halves:
                v.tensor_scalar(rel[0:n, t, :], cur[0:n, t, :], first[0:n, t:t + 1], None, ALU.subtract)\
                 .then_inc(s_table, 1)
            v.wait_ge(s_nxt, 32)
            for t, n in halves:
                then(v.tensor_tensor(change[0:n, t, :], cur[0:n, t, :], nxt[0:n, t, :], ALU.not_equal))
                v.wait_ge(s_table, t + 2)
                then(v.scalar_tensor_tensor(out=mark[0:n, t, :], in0=rel[0:n, t, :], scalar=1.0,
                                            in1=change[0:n, t, :], op0=ALU.add, op1=ALU.mult))
                v.tensor_scalar(last[0:n, t, :], mark[0:n, t, :], -1.0, None, ALU.add).then_inc(s_table, 1)
            v.wait_ge(s_prev, 32)
            for t, n in halves:
                v.tensor_tensor(begin[0:n, t, :], cur[0:n, t, :], prev[0:n, t, :], ALU.not_equal)\
                 .then_inc(s_begin, 1)
            v.wait_ge(s_rows, 32)
            v.memset(chip.blocks[:, 0:2], 0)
            ends = rows[:, 0, SLOTS::SLOTS]
            v.tensor_scalar(chip.blocks[:, 2:2 + ends.shape[-1]], ends, 7, None, ALU.arith_shift_right)
            v.memset(chip.blocks[:, 2 + ends.shape[-1]:], BLOCKS)
            then(v.tensor_tensor(span[:, 0, :], rows[:, 1, :], rows[:, 0, :], ALU.subtract))
            then(v.tensor_scalar(span[:, 1, :], span[:, 0, :], 7, None, ALU.arith_shift_right))
            v.memset(wf[:, 0, 0:1], 1.0)
            v.memset(wf[:, 5, 0:1], 0.0)
            v.tensor_copy(wf[:, 5, 1:], span[:, 1, :])
            v.tensor_scalar(wf[:, 0, 1:], span[:, 1, :], 1.0, None, ALU.add)
            v.memset(chip.regs[:, 2, 0:1], N)
            v.tensor_copy(chip.regs[:, 2, 1:], rows[:, 0, :])
            then(v.memset(wf[:, 1, :], 1.0))
            v.tensor_copy(chip.regs[:, 0, :], wf[:, 0, :])
            then(v.tensor_tensor_scan(wf[:, 2, :], wf[:, 1, :], wf[:, 5, :], 0.0, ALU.mult, ALU.add))
            then(v.tensor_tensor(wf[:, 3, :], wf[:, 2, :], wf[:, 5, :], ALU.subtract))
            v.tensor_copy(chip.regs[:, 1, :], wf[:, 3, :])

        turns = [(tile, t, n) for tile in (rel, last) for t, n in halves]

        @block.tensor
        def _(pe):
            pe.wait_ge(s_ident, 1)
            for x, (tile, t, n) in enumerate(turns):
                pe.wait_ge(s_table, x + 1)
                if x >= 2:
                    pe.wait_ge(s_copy, x - 1)
                for j in range(G):
                    at = (j // J) * CH + j % J
                    m = pe.transpose(p_table[:, x % 2, j, 0:n], tile[0:n, t, at:at + CH - J + 1:J],
                                     chip.ident[0:n, 0:n])
                m.then_inc(s_turn, 1)
            for x, step in enumerate(steps):
                if x:
                    pe.wait_ge(steps[x - 1].s_done, 1)
                step.tensor(pe, chip.ident)

        @block.scalar
        def _(act):
            for x, (tile, t, n) in enumerate(turns):
                to = chip.dst if tile is rel else chip.last
                act.wait_ge(s_turn, x + 1)
                nc.scalar.copy(to[:, 1 + t * P:1 + t * P + n, :],
                               p_table[:, x % 2, :, 0:n].rearrange("p j g -> p g j")).then_inc(s_copy, 1)
            act.wait_ge(s_begin, 2)
            for t, n in halves:
                nc.scalar.mul(start[0:n, t, :], begin[0:n, t, :], RESET).then_inc(s_start, 1)
            for step in steps:
                step.scalar(nc, act)


def edge_views(src_pad, g):
    return src_pad[bass.ds(g * GE, GE)].rearrange("(h p j) -> p h j", h=H, p=P)


def build_hot(chip, v, hot, table, entry, beyond=None):
    for j in range(G):
        column = table[:, bass.ds(entry, 1), j]
        if beyond is None:
            ins = v.tensor_scalar(hot[:, j, :], chip.ramp[:, :], column, None, ALU.is_equal)
        else:
            ins = v.tensor_scalar(hot[:, j, :], chip.ramp[:, :], column, chip.shifts[:, bass.ds(beyond, 1)],
                                  ALU.subtract, ALU.is_equal)
    return ins


def load_entry(chip, eng, row, entry, low, high):
    return eng.value_load(chip.regs[0:1, row, bass.ds(entry, 1)], min_val=low, max_val=high)


def further_windows(chip, eng, entry, body):
    windows = load_entry(chip, eng, 0, entry, 1, NP // P)
    with eng.If(windows > 1):
        before = load_entry(chip, eng, 1, entry, 0, NG * NP // P)
        with eng.Fori(1, windows) as n:
            body(n, eng.snap((before + n).with_bounds(min_val=1, max_val=NG * NP // P)))


def finished_blocks(chip, eng, k, body, ready=None):
    bound = lambda at: eng.value_load(chip.blocks[0:1, bass.ds(at, 1)], min_val=0, max_val=BLOCKS)
    low, high = bound(k + 1), bound(k + 2)
    with eng.If(high > low):
        if ready:
            ready()
        with eng.Fori(low, high) as c:
            body(c)


class DegreeSteps:

    def __init__(self, sb, sem, acc, rows):
        self.counts, self.rows = acc[KC - 1:KC, :], rows
        self.d = sb("degrees", [P, 8, NP // P])
        self.one = sb("one", [P, 1])
        self.s_cnt, self.s_in, self.s_max, self.s_log, self.s_rows, self.s_out = (
            sem(f"s_deg_{n}") for n in ("cnt", "in", "max", "log", "rows", "out"))

    def view(self, n):
        return self.rows[n].rearrange("(p r) -> p r", p=P)

    def scalar(self, nc, act):
        d = self.d
        act.dma_start(self.rows[0].rearrange("(a n) -> a n", a=1), self.counts).then_inc(self.s_cnt, 16)
        act.wait_ge(self.s_cnt, 16)
        act.dma_start(d[:, 0, :], self.view(0)).then_inc(self.s_in, 16)
        act.wait_ge(self.s_max, 2)
        nc.scalar.activation(d[:, 6, :], d[:, 5, :], ACT.Ln, bias=self.one[:, 0:1]).then_inc(self.s_log, 1)
        act.wait_ge(self.s_rows, 4)
        for n in range(1, 5):
            act.dma_start(self.view(n), d[:, n, :]).then_inc(self.s_out, 16)
        act.wait_ge(self.s_out, 64)

    def vector(self, v):
        d = self.d
        v.memset(self.one[:, :], 1.0).then_inc(self.s_max, 1)
        v.wait_ge(self.s_in, 16)
        v.tensor_scalar(d[:, 5, :], d[:, 0, :], 1.0, None, ALU.max).then_inc(self.s_max, 1)
        v.tensor_scalar(d[:, 2, :], d[:, 0, :], 1.0, None, ALU.min).then_inc(self.s_rows, 1)
        v.wait_ge(self.s_max, 2)
        v.reciprocal(d[:, 1, :], d[:, 5, :]).then_inc(self.s_rows, 1)
        v.wait_ge(self.s_log, 1)
        v.reciprocal(d[:, 7, :], d[:, 6, :]).then_inc(self.s_max, 1)
        v.tensor_scalar(d[:, 4, :], d[:, 6, :], 1.0 / AVG_LOG, None, ALU.mult).then_inc(self.s_rows, 1)
        v.wait_ge(self.s_max, 3)
        v.tensor_scalar(d[:, 3, :], d[:, 7, :], AVG_LOG, None, ALU.mult).then_inc(self.s_rows, 1)


def conv_pass(chip, table, src_pad, ea_pad, W, bias, out_rows, relu, first=False,
              degree_rows=None):
    nc = chip.nc
    acc = chip.acc
    M = KC if first else D
    with ExitStack() as ctx:
        sb, ps, sem = chip.scope(ctx)
        idx = sb("idx", [P, SLOTS, G], I32)
        data = sb("data", [P, SLOTS, G, KC])
        hot = sb("hot", [P, 2, G, P])
        part = ps("part", [P, 2, CH])
        part_x = ps("part_x", [P, CH])
        wa = sb("wa", [D, D])
        wsum = sb("wsum", [KC, D + 1])
        h_in = sb("h_in", [P, D])
        sums = sb("sums", [KC, P])
        h_t = sb("h_t", [D, P])
        part_s = sb("part_s", [P, D + 1])
        conv = sb("conv", [P, D])
        p_turn = ps("p_turn", [D, CH])
        p_sums = ps("p_sums", [P, CH])
        p_own = ps("p_own", [P, CH])
        s_sums = sem("s_sums")
        s_w = sem("s_w")
        s_pick = sem("s_pick")
        s_copy = sem("s_copy")
        s_h_turn = sem("s_h_turn")
        s_h_t = sem("s_h_t")
        s_conv = sem("s_conv")
        s_cnt = sem("s_cnt")
        s_x = sem("s_x")
        s_pre = sem("s_pre")
        s_h = sem("s_h")
        s_out = sem("s_out")
        scratch = sb("scratch", [1, 3])
        s_idx = [sem(f"s_idx{r}") for r in range(SLOTS)]
        s_ea = [sem(f"s_ea{r}") for r in range(SLOTS)]
        s_row = [sem(f"s_row{r}") for r in range(SLOTS)]
        s_ready = sem("s_ready")
        s_hot = sem("s_hot")
        s_part = sem("s_part")
        s_added = sem("s_added")
        s_hot_x = sem("s_hot_x")
        s_part_x = sem("s_part_x")
        s_added_x = sem("s_added_x")
        block = ctx.enter_context(nc.Block())

        degrees = DegreeSteps(sb, sem, acc, degree_rows) if degree_rows is not None else None
        h_row = lambda c: chip.h[:, bass.ds(c, 1), :].rearrange("p a f -> p (a f)")

        @block.sync
        def _(sp):
            def store(c):
                sp.wait_ge(s_h, c + 2)
                gate(sp)
                sp.dma_start(out_rows[bass.ds(c * P, P), :], h_row(c)).then_inc(s_out, 16)

            with sp.Fori(0, NG // SLOTS) as k:
                for r in range(SLOTS):
                    g = k * SLOTS + r
                    sp.wait_ge(s_hot, g + 1)
                    sp.dma_start(idx[:, r, :].rearrange("p (h j) -> p h j", h=H),
                                 edge_views(src_pad, g)).then_inc(s_idx[r], 16)
                    if first:
                        for h in range(H):
                            sp.dma_start(data[:, r, J * h:J * h + J, D:D + FE],
                                         ea_pad[bass.ds(g * GE + h * J * P, J * P), :]
                                         .rearrange("(p j) f -> p j f", p=P)).then_inc(s_ea[r], 16)
                if out_rows is not None:
                    finished_blocks(chip, sp, k - 1, store)
            if out_rows is not None:
                finished_blocks(chip, sp, TURNS - 1, store)
                sp.wait_ge(s_out, 16 * BLOCKS)

        @block.gpsimd
        def _(pool):
            with pool.Fori(0, NG // SLOTS) as k:
                for r in range(SLOTS):
                    pool.wait_ge(s_idx[r], k * 16 + 16)
                    gate(pool)
                    for j in range(G):
                        pool.indirect_dma_start(
                            out=data[:, r, j, 0:D], out_offset=None, in_=table[:, :],
                            in_offset=bass.IndirectOffsetOnAxis(ap=idx[:, r, j:j + 1], axis=0),
                        ).then_inc(s_row[r], 16)

        @block.scalar
        def _(act):
            act.dma_start(wa[:, :], W[0:D, :]).then_inc(s_w, 16)
            act.dma_start(wsum[0:D + FE, 0:D], W[D:, :]).then_inc(s_w, 16)
            act.dma_start(wsum[KC - 1:KC, 0:D], bias.rearrange("(a f) -> a f", a=1)).then_inc(s_w, 16)
            nc.scalar.copy(wsum[:, D:], chip.ident[0:KC, KC - 1:KC]).then_inc(s_pick, 1)
            if first:
                act.wait_ge(s_added, 2 * SLOTS)
                act.dma_start(chip.h[:, :, :], table.rearrange("(c p) f -> p c f", p=P))\
                   .then_inc(s_x, 16)
                act.wait_ge(s_x, 16)

            if degrees:
                degrees.scalar(nc, act)

            def stage(c):
                act.wait_ge(s_h, c + 1)
                nc.scalar.copy(h_in[:, :], h_row(c))
                nc.scalar.copy(sums[:, :], acc[0:KC, bass.ds(c * P, P)]).then_inc(s_copy, 1)
                act.wait_ge(s_h_turn, c + 1)
                nc.scalar.copy(h_t[:, :], p_turn[:, 0:P]).then_inc(s_h_t, 1)

            with act.Fori(0, TURNS) as k:
                def summed():
                    e = (k + 1) * SLOTS
                    total = (load_entry(chip, act, 0, e, 1, NP // P)
                             + load_entry(chip, act, 1, e, 0, NG * NP // P))
                    act.wait_ge(s_added, e + SLOTS)
                    act.wait_ge(s_added_x, act.snap(total.with_bounds(min_val=1, max_val=NG * NP // P)))

                finished_blocks(chip, act, k, stage, summed)

        @block.tensor
        def _(pe):
            def products(out, r):
                for j in range(G):
                    mm = pe.matmul(out[0:M, 0:P], data[:, r, j, 0:M], hot[:, r % 2, j, :],
                                   start=(j == 0), stop=(j == G - 1))
                return mm

            def convolve(c):
                pe.wait_ge(s_copy, c + 1)
                gate(pe)
                pe.transpose(p_turn[:, 0:P], h_in[:, :], chip.ident[:, :]).then_inc(s_h_turn, 1)
                pe.matmul(p_sums[:, 0:D + 1], sums[:, :], wsum[:, :], start=True, stop=True).then_inc(s_sums, 1)
                pe.wait_ge(s_h_t, c + 1)
                gate(pe)
                pe.matmul(p_own[:, 0:D], h_t[:, :], wa[:, :], start=True, stop=True).then_inc(s_conv, 1)

            pe.wait_ge(s_w, 48)
            pe.wait_ge(s_pick, 1)
            pe.wait_ge(s_ready, 1)
            with pe.Fori(0, NG // SLOTS) as k:
                for r in range(SLOTS):
                    g = k * SLOTS + r
                    pe.wait_ge(s_row[r], k * 16 * G + 16 * G)
                    if first:
                        pe.wait_ge(s_ea[r], k * 16 * H + 16 * H)
                    pe.wait_ge(s_hot, g + 3)
                    pe.wait_ge(s_added, g + SLOTS - 1)
                    gate(pe)
                    products(part[:, r % 2], r).then_inc(s_part, 1)

                    def more(n, x):
                        pe.wait_ge(s_hot_x, x)
                        pe.wait_ge(s_added_x, x)
                        gate(pe)
                        products(part_x, r).then_inc(s_part_x, 1)

                    further_windows(chip, pe, g + 1, more)

                finished_blocks(chip, pe, k, convolve)

        @block.vector
        def _(v):
            def add(base, n, sums):
                at = v.snap((base + n * P).with_bounds(min_val=0, max_val=NP - P))
                return v.tensor_tensor(acc[0:M, bass.ds(at, P)], acc[0:M, bass.ds(at, P)], sums[0:M, 0:P], ALU.add)

            def finish(k, r, g):
                base = load_entry(chip, v, 2, g + 1, 0, N)
                v.wait_ge(s_part, g + 1)
                v.wait_ge(s_added, g + SLOTS)
                add(base, 0, part[:, r % 2]).then_inc(s_added, 1)

                def more(n, x):
                    if_ready = g + SLOTS + 1
                    v.wait_ge(s_added, if_ready)
                    build_hot(chip, v, hot[:, r % 2], chip.dst, g + 1, n).then_inc(s_hot_x, 1)
                    v.wait_ge(s_part_x, x)
                    add(base, n, part_x).then_inc(s_added_x, 1)
                    v.wait_ge(s_added_x, x + 1)

                further_windows(chip, v, g + 1, more)

            v.memset(scratch[:, 1:2], 0.0).then_inc(s_hot, 2)
            for g in (0, 1):
                build_hot(chip, v, hot[:, g], chip.dst, g + 1).then_inc(s_hot, 1)
            v.memset(data[:, :, :, KC - 1:KC], 1.0).then_inc(s_ready, 1)
            v.memset(acc[0:M, :], 0.0).then_inc(s_added, SLOTS)
            v.memset(scratch[:, 0:1], 0.0).then_inc(s_added_x, 1)
            v.memset(scratch[:, 2:3], 0.0).then_inc(s_h, 1)
            if degrees:
                degrees.vector(v)
            last_k = NG // SLOTS - 1
            def body(k, r, ahead):
                g = k * SLOTS + r
                finish(k, r, g)
                if ahead:
                    build_hot(chip, v, hot[:, r % 2], chip.dst, g + 3).then_inc(s_hot, 1)

            def rows(c):
                v.wait_ge(s_sums, c + 1)
                v.tensor_copy(part_s[:, :], p_sums[:, 0:D + 1]).then_inc(s_cnt, 1)
                v.wait_ge(s_cnt, c + 1)
                v.wait_ge(s_conv, c + 1)
                cnt = part_s[:, D:D + 1]
                out = conv[:, :] if relu else h_row(c)
                ins = v.scalar_tensor_tensor(out=out, in0=p_own[:, 0:D], scalar=cnt, in1=part_s[:, 0:D],
                                             op0=ALU.mult, op1=ALU.add)
                if relu:
                    ins.then_inc(s_pre, 1)
                    v.wait_ge(s_pre, c + 1)
                    ins = v.tensor_scalar(h_row(c), conv[:, :], 0.0, None, ALU.max)
                ins.then_inc(s_h, 1)

            with v.Fori(0, last_k) as k:
                for r in range(SLOTS):
                    body(k, r, True)
                finished_blocks(chip, v, k, rows)
            for r in range(SLOTS):
                body(last_k, r, r < SLOTS - 2)
            finished_blocks(chip, v, last_k, rows)


def pipeline(eng, *stages):
    deep = max(lag for lag, _ in stages)
    start = deep + 2
    pairs = (NCH - start) // 2

    def turn(t):
        for lag, body in stages:
            if 0 <= t - lag < NCH:
                body(t - lag, (t - lag) % 2, (t - lag) // 2)

    for t in range(start):
        turn(t)
    with eng.Fori(0, pairs) as k:
        for t in (start, start + 1):
            for lag, body in stages:
                c = t - lag
                body(k * 2 + c, c % 2, k + c // 2)
    for t in range(start + 2 * pairs, NCH + deep):
        turn(t)


def reused(eng, sem, c):
    if not isinstance(c, int):
        eng.wait_ge(sem, c - 1)
    elif c >= 2:
        eng.wait_ge(sem, c - 1)


def stored(eng, sem, c, n):
    if not isinstance(c, int) or c >= 2:
        eng.wait_ge(sem, n * 16)


def spread(row, c, parts):
    return row[bass.ds(c * CH, CH)].rearrange("(a n) -> a n", a=1).broadcast_to([parts, CH])


def final_count(i):
    return 16 * ((NCH + 1 - i) // 2)


def rows_of(t, c):
    return t[bass.ds(c * CH, CH), :].rearrange("(b p) f -> p b f", p=P)


def residual_norm(chip, a, b_rows, out_rows, w=None, q_rows=None):
    nc = chip.nc
    PIECES = 5
    W = NP // P // PIECES
    with ExitStack() as ctx:
        sb, ps, sem = chip.scope(ctx)
        b = sb("b", [P, PIECES * W, D])
        sq = sb("sq", [P, 2, W, D])
        mean = sb("mean", [P, PIECES, W])
        var = sb("var", [P, PIECES, W])
        sd = sb("sd", [P, PIECES, W])
        rsd = sb("rsd", [P, PIECES, W])
        eps = sb("eps", [P, 1])
        x_in = sb("x_in", [P, 2, B, D])
        x_t = sb("x_t", [D, 2, CH])
        q_stage = sb("q_stage", [P, 2, B, D])
        p_x = ps("p_x", [D, 2, CH])
        p_q = ps("p_q", [P, 2, CH])
        s_in = sem("s_in")
        s_turn = sem("s_turn")
        s_xt = sem("s_xt")
        s_q = sem("s_q")
        s_stage = sem("s_stage")
        s_q_out = [sem(f"s_q_out{i}") for i in (0, 1)]
        s_a = [sem(f"s_a{n}") for n in range(PIECES)]
        s_v = sem("s_v")
        s_sd = sem("s_sd")
        s_center = sem("s_center")
        s_sq = sem("s_sq")
        s_rsd = sem("s_rsd")
        s_var = sem("s_var")
        s_norm = sem("s_norm")
        s_out = sem("s_out")
        block = ctx.enter_context(nc.Block())
        view = lambda t, n: t[n * W * P:(n + 1) * W * P, :].rearrange("(c p) f -> p c f", p=P)
        piece = lambda t, n: t[:, n * W:(n + 1) * W, :]

        @block.sync
        def _(sp):
            for n in range(PIECES):
                sp.dma_start(piece(b, n), view(b_rows, n)).then_inc(s_a[n], 16)
            for n in range(PIECES):
                sp.wait_ge(s_norm, n + 1)
                sp.dma_start(view(out_rows, n), piece(b, n)).then_inc(s_out, 16)
            if w:
                def store(c, i, n):
                    sp.wait_ge(s_stage, c + 1)
                    gate(sp)
                    sp.dma_start(rows_of(q_rows, c), q_stage[:, i]).then_inc(s_q_out[i], 16)

                pipeline(sp, (0, store))
                for i in (0, 1):
                    sp.wait_ge(s_q_out[i], final_count(i))
            sp.wait_ge(s_out, 16 * PIECES)

        @block.gpsimd
        def _(pool):
            def load(c, i, n):
                reused(pool, s_turn, c)
                gate(pool)
                pool.tensor_copy(x_in[:, i], b[:, bass.ds(c * B, B), :]).then_inc(s_in, 1)

            for m in range(PIECES):
                pool.wait_ge(s_rsd, m + 1)
                r3 = rsd[:, m, :].unsqueeze(2).broadcast_to([P, W, D])
                pool.tensor_tensor(piece(b, m), piece(a, m), r3, ALU.mult).then_inc(s_norm, 1)
            if w:
                pool.wait_ge(s_norm, PIECES)
                pipeline(pool, (0, load))

        @block.tensor
        def _(pe):
            def turn(c, i, n):
                pe.wait_ge(s_in, c + 1)
                reused(pe, s_xt, c)
                gate(pe)
                for m in range(B):
                    t = pe.transpose(p_x[:, i, m * P:(m + 1) * P], x_in[:, i, m, :], chip.ident[:, :])
                t.then_inc(s_turn, 1)

            def multiply(c, i, n):
                pe.wait_ge(s_xt, c + 1)
                reused(pe, s_stage, c)
                gate(pe)
                for m in range(B):
                    t = pe.matmul(p_q[:, i, m * D:(m + 1) * D], x_t[:, i, m * P:(m + 1) * P],
                                  w.source[:, :], start=True, stop=True)
                t.then_inc(s_q, 1)

            if w:
                pipeline(pe, (0, turn), (1, multiply))

        @block.scalar
        def _(act):
            for n in range(PIECES + 1):
                if n < PIECES:
                    act.wait_ge(s_center, n + 1)
                    if n >= 2:
                        act.wait_ge(s_var, n - 1)
                    nc.scalar.activation(sq[:, n % 2], piece(a, n), ACT.Square).then_inc(s_sq, 1)
                if n:
                    act.wait_ge(s_var, n)
                    nc.scalar.activation(sd[:, n - 1, :], var[:, n - 1, :], ACT.Sqrt, bias=eps[:, 0:1],
                                         scale=1.0 / D).then_inc(s_sd, 1)

            def copy_x(c, i, n):
                act.wait_ge(s_turn, c + 1)
                reused(act, s_q, c)
                nc.scalar.copy(x_t[:, i, :], p_x[:, i, :]).then_inc(s_xt, 1)

            def to_rows(c, i, n):
                act.wait_ge(s_q, c + 1)
                stored(act, s_q_out[i], c, n)
                nc.scalar.copy(q_stage[:, i, :, :],
                               p_q[:, i, 0:B * D].rearrange("p (b f) -> p b f", b=B)).then_inc(s_stage, 1)

            if w:
                pipeline(act, (0, copy_x), (2, to_rows))

        @block.vector
        def _(v):
            steps = [0]

            def then(ins):
                steps[0] += 1
                ins.then_inc(s_v, 1)
                v.wait_ge(s_v, steps[0])

            then(v.memset(eps[:, :], EPS_LN))

            def center(n):
                v.wait_ge(s_a[n], 16)
                x = piece(a, n)
                then(v.tensor_tensor(x, x, piece(b, n), ALU.add))
                then(v.tensor_reduce(mean[:, n, :], x, AX_X, ALU.add))
                then(v.tensor_scalar(mean[:, n, :], mean[:, n, :], 1.0 / D, None, ALU.mult))
                m3 = mean[:, n, :].unsqueeze(2).broadcast_to([P, W, D])
                v.tensor_tensor(x, x, m3, ALU.subtract).then_inc(s_center, 1)

            def variance(n):
                v.wait_ge(s_sq, n + 1)
                v.tensor_reduce(var[:, n, :], sq[:, n % 2], AX_X, ALU.add).then_inc(s_var, 1)

            def invert(n):
                v.wait_ge(s_sd, n + 1)
                v.reciprocal(rsd[:, n, :], sd[:, n, :]).then_inc(s_rsd, 1)

            for n in range(PIECES + 2):
                if n < PIECES:
                    center(n)
                if 0 <= n - 1 < PIECES:
                    variance(n - 1)
                if 0 <= n - 2:
                    invert(n - 2)


def pna_pass(chip, w, q_rows, src_pad, ea_t, flags):
    nc = chip.nc
    acc = chip.acc2
    with ExitStack() as ctx:
        sb, ps, sem = chip.scope(ctx)
        idx = sb("idx", [P, SLOTS, G], I32)
        data = sb("data", [P, SLOTS, G, D])
        feat = sb("feat", [FE, 2, GE])
        flag = sb("flag", [1, 2, GE], BF16)
        ones = sb("ones", [1, P], BF16)
        t3 = sb("t3", [P, SLOTS, G, 3, D])
        reset = sb("reset", [P, 2, GE], BF16)
        run = sb("run", [P, 2, GE])
        back = sb("back", [P, G, P])
        hot = sb("hot", [P, 2, 2, G, P])
        scratch = sb("scratch", [1, 8])
        p_feat = ps("p_feat", [P, CH])
        p_flag = ps("p_flag", [P, GE])
        p_turn = ps("p_turn", [P, GE])
        p_back = ps("p_back", [P, GE])
        part = ps("part", [P, 2, 2, P])
        s_idx = [sem(f"s_idx{r}") for r in range(SLOTS)]
        s_edge = [sem(f"s_edge{i}") for i in (0, 1)]
        s_row = [sem(f"s_row{r}") for r in range(SLOTS)]
        s_ready = sem("s_ready")
        s_feat = sem("s_feat")
        s_t = sem("s_t")
        s_flag = sem("s_flag")
        s_reset = sem("s_reset")
        s_split = sem("s_split")
        s_turn = sem("s_turn")
        s_run = sem("s_run")
        s_back = sem("s_back")
        s_bcopy = sem("s_bcopy")
        s_hot = sem("s_hot")
        s_part = sem("s_part")
        s_added = sem("s_added")
        s_hot_x = sem("s_hot_x")
        s_part_x = sem("s_part_x")
        s_added_x = sem("s_added_x")
        block = ctx.enter_context(nc.Block())
        last_k = NG // SLOTS - 1

        def turns(eng, body):
            with eng.Fori(0, last_k) as k:
                for r in range(SLOTS):
                    body(k, r, True)
            for r in range(SLOTS):
                body(last_k, r, r < SLOTS - 1)

        @block.sync
        def _(sp):
            with sp.Fori(0, NG // SLOTS) as k:
                for r in range(SLOTS):
                    g = k * SLOTS + r
                    sp.wait_ge(s_t, g + 1)
                    sp.dma_start(idx[:, r, :].rearrange("p (h j) -> p h j", h=H),
                                 edge_views(src_pad, g)).then_inc(s_idx[r], 16)
                    sp.wait_ge(s_flag, g + 1)
                    sp.dma_start(feat[:, r % 2, :], ea_t[:, bass.ds(g * GE, GE)]).then_inc(s_edge[r % 2], 16)
                    sp.dma_start(flag[:, r % 2, :], flags[bass.ds(g * GE, GE)].rearrange("(a e) -> a e", a=1))\
                      .then_inc(s_edge[r % 2], 16)

        @block.gpsimd
        def _(pool):
            with pool.Fori(0, NG // SLOTS) as k:
                for r in range(SLOTS):
                    pool.wait_ge(s_idx[r], k * 16 + 16)
                    gate(pool)
                    for j in range(G):
                        pool.indirect_dma_start(
                            out=data[:, r, j, :], out_offset=None, in_=q_rows[:, :],
                            in_offset=bass.IndirectOffsetOnAxis(ap=idx[:, r, j:j + 1], axis=0),
                        ).then_inc(s_row[r], 16)

        @block.tensor
        def _(pe):
            def front(k, r):
                g = k * SLOTS + r
                pe.wait_ge(s_edge[r % 2], k * (32 * SLOTS // 2) + 32 * (r // 2) + 32)
                pe.wait_ge(s_t, g + SLOTS)
                gate(pe)
                for j in range(G):
                    at = (j // J) * CH + j % J
                    m = pe.matmul(p_feat[:, j * D:(j + 1) * D], feat[:, r % 2, at:at + CH - J + 1:J],
                                  w.edge[:, :], start=True, stop=True)
                m.then_inc(s_feat, 1)
                pe.wait_ge(s_reset, g + 1)
                gate(pe)
                for h in range(H):
                    m = pe.matmul(p_flag[:, h * CH:(h + 1) * CH], ones[:, :], flag[:, r % 2, h * CH:(h + 1) * CH],
                                  start=True, stop=True)
                m.then_inc(s_flag, 1)

            def turn_back(e, par):
                pe.wait_ge(s_run, e + 1)
                pe.wait_ge(s_bcopy, e + 1)
                gate(pe)
                for j in range(G):
                    at = (j // J) * CH + j % J
                    b = pe.transpose(p_back[:, j * P:(j + 1) * P], run[:, par, at:at + CH - J + 1:J],
                                     chip.ident[:, :])
                b.then_inc(s_back, 1)

            def sums(x, slot, par):
                for j in range(G):
                    pe.matmul(part[:, x, 0, :], t3[:, slot, j, 1:3, :].rearrange("p b f -> p (b f)"),
                              hot[:, par, 0, j, :], start=(j == 0), stop=(j == G - 1))

            def maxima(x, par):
                for j in range(G):
                    m = pe.matmul(part[:, x, 1, :], back[:, j, :], hot[:, par, 1, j, :],
                                  start=(j == 0), stop=(j == G - 1))
                return m

            def sum_stage(e, slot, turn=None):
                par = slot % 2
                turn_back(e, par)
                pe.wait_ge(s_hot, e + 1)
                pe.wait_ge(s_added, e + 1)
                gate(pe)
                sums(0, slot, par)
                if turn:
                    turn()
                pe.wait_ge(s_bcopy, e + 2)
                gate(pe)
                maxima(0, par).then_inc(s_part, 1)

                def more(n, x):
                    pe.wait_ge(s_hot_x, x)
                    gate(pe)
                    sums(1, slot, par)
                    maxima(1, par).then_inc(s_part_x, 1)
                    pe.wait_ge(s_added_x, x + 1)
                    gate(pe)

                further_windows(chip, pe, e, more)

            def body(k, r, has_next):
                i = k * SLOTS + r
                if has_next:
                    front(k + (r + 1) // SLOTS, (r + 1) % SLOTS)

                def turn():
                    pe.wait_ge(s_split, i + 1)
                    gate(pe)
                    for j in range(G):
                        at = (j // J) * CH + j % J
                        m = pe.transpose(p_turn[:, at:at + CH - J + 1:J],
                                         t3[:, r, j, 0:2, :].rearrange("p b f -> p (b f)"), chip.ident[:, :])
                    m.then_inc(s_turn, 1)

                sum_stage(i, (r + SLOTS - 1) % SLOTS, turn)

            pe.wait_ge(s_ready, 1)
            front(0, 0)
            turns(pe, body)
            sum_stage(NG, SLOTS - 1)

        @block.scalar
        def _(act):
            def copy_flags(g, r):
                act.wait_ge(s_flag, g + 3)
                act.wait_ge(s_run, g)
                nc.scalar.copy(reset[:, r % 2, :], p_flag[:, :]).then_inc(s_reset, 1)

            def split(g, r):
                act.wait_ge(s_t, g + 1 + SLOTS)
                t = t3[:, r, :, 1, :]
                nc.scalar.mul(t3[:, r, :, 0, :], t, -1.0)
                nc.scalar.activation(t3[:, r, :, 2, :], t, ACT.Square).then_inc(s_split, 1)

            def copy_back(e):
                act.wait_ge(s_back, e + 1)
                nc.scalar.copy(back[:, :, :].rearrange("p j f -> p (j f)"), p_back[:, :]).then_inc(s_bcopy, 1)

            def body(k, r, has_next):
                i = k * SLOTS + r
                if has_next:
                    copy_flags(i + 1, r + 1)
                copy_back(i)
                if has_next:
                    split(i + 1, (r + 1) % SLOTS)

            act.wait_ge(s_flag, 3)
            nc.scalar.copy(reset[:, 0, :], p_flag[:, :]).then_inc(s_reset, 1)
            split(0, 0)
            turns(act, body)
            copy_back(NG)

        @block.vector
        def _(v):
            def make_t(k, r):
                g = k * SLOTS + r
                v.wait_ge(s_row[r], k * 16 * G + 16 * G)
                v.wait_ge(s_feat, g + 1)
                v.tensor_tensor(t3[:, r, :, 1, :], data[:, r, :, :],
                                p_feat[:, :].rearrange("p (j f) -> p j f", j=G), ALU.add).then_inc(s_t, 1)

            def add(base, n, x):
                at = v.snap((base + n * P).with_bounds(min_val=0, max_val=NP - P))
                return v.tensor_tensor(acc[:, :, bass.ds(at, P)], acc[:, :, bass.ds(at, P)], part[:, x], ALU.add)

            def finish(e, par):
                base = load_entry(chip, v, 2, e, 0, N)
                v.wait_ge(s_part, e + 1)
                v.wait_ge(s_added, e + 1)
                add(base, 0, 0).then_inc(s_added, 1)

                def more(n, x):
                    v.wait_ge(s_added, e + 2)
                    build_hot(chip, v, hot[:, par, 0], chip.dst, e, n)
                    build_hot(chip, v, hot[:, par, 1], chip.last, e, n).then_inc(s_hot_x, 1)
                    v.wait_ge(s_part_x, x)
                    add(base, n, 1).then_inc(s_added_x, 1)
                    v.wait_ge(s_added_x, x + 1)

                further_windows(chip, v, e, more)

            def body(k, r, has_next):
                i = k * SLOTS + r
                if has_next:
                    make_t(k + (r + 1) // SLOTS, (r + 1) % SLOTS)
                build_hot(chip, v, hot[:, r % 2, 0], chip.dst, i + 1)
                build_hot(chip, v, hot[:, r % 2, 1], chip.last, i + 1).then_inc(s_hot, 1)
                v.wait_ge(s_turn, i + 1)
                v.wait_ge(s_reset, i + 2)
                v.wait_ge(s_run, i + 1)
                v.tensor_tensor_scan(run[:, r % 2, :], reset[:, r % 2, :], p_turn[:, :],
                                     run[:, (r + 1) % 2, GE - 1:GE], ALU.add, ALU.max).then_inc(s_run, 1)
                finish(i, (r + 1) % 2)

            for n, (s, count) in enumerate(((s_t, SLOTS), (s_flag, 2), (s_reset, 1), (s_bcopy, 1), (s_added_x, 1))):
                v.memset(scratch[:, n:n + 1], 0.0).then_inc(s, count)
            v.memset(t3[:, SLOTS - 1], 0.0)
            v.memset(hot[:, 1], 0.0).then_inc(s_hot, 1)
            v.memset(ones[:, :], 1.0).then_inc(s_ready, 1)
            v.memset(run[:, 1, :], 0.0).then_inc(s_run, 1)
            v.memset(acc[:, :, :], 0.0).then_inc(s_added, 1)
            make_t(0, 0)
            turns(v, body)
            finish(NG, 1)


def pna_nodes(chip, w, x_rows, rows):
    nc = chip.nc
    acc = chip.acc2
    low, high = slice(0, D), slice(D, P)
    cnt_row, rden_row, has_row, att_row, amp_row = (rows[n] for n in range(5))
    with ExitStack() as ctx:
        sb, ps, sem = chip.scope(ctx)
        xin = sb("xin", [P, 2, B, D])
        xt = sb("xt", [D + 1, 2, CH])
        cnt = sb("cnt", [D, 2, CH])
        rden = sb("rden", [P, 2, CH])
        has = sb("has", [P, 2, CH])
        scales = sb("scales", [P, 2, CH])
        pn = sb("pn", [P, 2, CH])
        mom = sb("mom", [P, 2, CH])
        var = sb("var", [P, 2, CH])
        stat_a = sb("stat_a", [P, 2, CH])
        stat_b = sb("stat_b", [P, 2, CH])
        stat_c = sb("stat_c", [P, 2, CH])
        z = sb("z", [D, 2, CH])
        z_sum = sb("z_sum", [D, CH])
        eps = sb("eps", [P, 1])
        p_x = ps("p_x", [D, 2, CH])
        p_p = ps("p_p", [P, 2, CH])
        p_wide = ps("p_wide", [P, 2, CH])
        p_att = ps("p_att", [D, 2, CH])
        s_x = [sem(f"s_x{i}") for i in (0, 1)]
        s_rden = [sem(f"s_rden{i}") for i in (0, 1)]
        s_deg = [sem(f"s_deg{i}") for i in (0, 1)]
        s_sc = [sem(f"s_sc{i}") for i in (0, 1)]
        names = "turn xt p pn mom sq dv var sd xc hasp cp stats post zz zsum y eps".split()
        s = {name: sem("s_" + name) for name in names}
        block = ctx.enter_context(nc.Block())

        @block.sync
        def _(sp):
            def load(c, i, n):
                reused(sp, s["turn"], c)
                gate(sp)
                sp.dma_start(xin[:, i], rows_of(x_rows, c)).then_inc(s_x[i], 16)
                reused(sp, s["mom"], c)
                gate(sp)
                sp.dma_start(rden[:, i, :], spread(rden_row, c, P)).then_inc(s_rden[i], 16)

            def load_degrees(c, i, n):
                reused(sp, s["stats"], c)
                gate(sp)
                sp.dma_start(cnt[:, i, :], spread(cnt_row, c, D)).then_inc(s_deg[i], 16)
                sp.dma_start(has[:, i, :], spread(has_row, c, P)).then_inc(s_deg[i], 16)

            def load_scales(c, i, n):
                reused(sp, s["zz"], c)
                gate(sp)
                sp.dma_start(scales[low, i, :], spread(att_row, c, D)).then_inc(s_sc[i], 16)
                sp.dma_start(scales[high, i, :], spread(amp_row, c, D)).then_inc(s_sc[i], 16)

            pipeline(sp, (0, load), (1, load_degrees), (3, load_scales))

        @block.tensor
        def _(pe):
            def turn(c, i, n):
                pe.wait_ge(s_x[i], n * 16 + 16)
                reused(pe, s["xt"], c)
                gate(pe)
                for b in range(B):
                    t = pe.transpose(p_x[:, i, b * P:(b + 1) * P], xin[:, i, b, :], chip.ident[:, :])
                t.then_inc(s["turn"], 1)

            def node_part(c, i, n):
                pe.wait_ge(s["xt"], c + 1)
                reused(pe, s["pn"], c)
                gate(pe)
                pe.matmul(p_p[:, i, :], w.node[:, :], xt[:, i, :], start=True, stop=True).then_inc(s["p"], 1)

            def post(c, i, n):
                pe.wait_ge(s["stats"], c + 1)
                pe.wait_ge(s["sd"], c + 1)
                pe.wait_ge(s["xc"], c + 1)
                reused(pe, s["y"], c)
                gate(pe)
                for p_out, cols in ((p_wide, slice(0, P)), (p_att, slice(P, P + D))):
                    for m, stat in enumerate((stat_a, stat_b, stat_c)):
                        t = pe.matmul(p_out[:, i, :], w.post[:, m, cols], stat[:, i, :],
                                      start=(m == 0), stop=(m == 2))
                t.then_inc(s["post"], 1)

            pipeline(pe, (2, node_part), (1, turn), (4, post))

        @block.scalar
        def _(act):
            def node_part(c, i, n):
                act.wait_ge(s["p"], c + 1)
                reused(act, s["stats"], c)
                nc.scalar.copy(pn[:, i, :], p_p[:, i, :]).then_inc(s["pn"], 1)

            def features(c, i, n):
                act.wait_ge(s["turn"], c + 1)
                reused(act, s["xc"], c)
                reused(act, s["p"], c)
                nc.scalar.copy(xt[0:D, i, :], p_x[:, i, :]).then_inc(s["xt"], 1)

            def squares(c, i, n):
                act.wait_ge(s["mom"], c + 1)
                reused(act, s["sd"], c)
                nc.scalar.activation(var[high, i, :], mom[low, i, :], ACT.Square).then_inc(s["sq"], 1)

            def copy_x(c, i, n):
                act.wait_ge(s["xt"], c + 1)
                reused(act, s["post"], c)
                nc.scalar.copy(stat_c[high, i, :], xt[0:D, i, :]).then_inc(s["xc"], 1)

            def deviation(c, i, n):
                act.wait_ge(s["var"], c + 1)
                reused(act, s["post"], c)
                nc.scalar.activation(stat_b[high, i, :], var[high, i, :], ACT.Sqrt,
                                     bias=eps[high, 0:1]).then_inc(s["sd"], 1)

            act.wait_ge(s["eps"], 1)
            pipeline(act, (3, copy_x), (2, node_part), (1, features), (3, deviation), (2, squares))

        @block.gpsimd
        def _(pool):
            def scale_node_part(c, i, n):
                pool.wait_ge(s["pn"], c + 1)
                pool.wait_ge(s_deg[i], n * 32 + 32)
                reused(pool, s["post"], c)
                pool.tensor_tensor(has[:, i, :], has[:, i, :], pn[:, i, :], ALU.mult).then_inc(s["hasp"], 1)
                pool.tensor_tensor(stat_c[low, i, :], cnt[:, i, :], pn[low, i, :], ALU.mult).then_inc(s["cp"], 1)

            pipeline(pool, (3, scale_node_part))

        @block.vector
        def _(v):
            span = lambda c: bass.ds(c * CH, CH)

            def moments(c, i, n):
                v.wait_ge(s_rden[i], n * 16 + 16)
                reused(v, s["stats"], c)
                reused(v, s["sq"], c)
                v.tensor_tensor(mom[:, i, :], acc[:, 0, span(c)], rden[:, i, :], ALU.mult).then_inc(s["mom"], 1)

            def variance(c, i, n):
                v.wait_ge(s["sq"], c + 1)
                v.scalar_tensor_tensor(out=var[high, i, :], in0=var[high, i, :], scalar=-1.0,
                                       in1=mom[high, i, :], op0=ALU.mult, op1=ALU.add).then_inc(s["dv"], 1)
                v.wait_ge(s["dv"], c + 1)
                v.tensor_scalar(var[high, i, :], var[high, i, :], 0.0, None, ALU.max).then_inc(s["var"], 1)

            def stats(c, i, n):
                v.wait_ge(s["hasp"], c + 1)
                reused(v, s["post"], c)
                v.tensor_tensor(stat_a[low, i, :], has[low, i, :], mom[low, i, :], ALU.add)
                v.tensor_tensor(stat_a[high, i, :], has[high, i, :], acc[high, 1, span(c)], ALU.add)
                v.tensor_tensor(stat_b[low, i, :], acc[low, 1, span(c)], has[low, i, :], ALU.subtract)
                v.wait_ge(s["cp"], c + 1)
                v.tensor_tensor(stat_c[low, i, :], stat_c[low, i, :], acc[low, 0, span(c)], ALU.add)\
                 .then_inc(s["stats"], 1)

            def scale(c, i, n):
                v.wait_ge(s["post"], c + 1)
                v.wait_ge(s_sc[i], n * 32 + 32)
                if not isinstance(c, int) or c >= 1:
                    v.wait_ge(s["zsum"], c)
                v.tensor_tensor(z[:, 0, :], scales[high, i, :], p_wide[high, i, :], ALU.mult)
                v.tensor_tensor(z[:, 1, :], scales[low, i, :], p_att[:, i, :], ALU.mult).then_inc(s["zz"], 1)
                v.wait_ge(s["zz"], c + 1)
                if not isinstance(c, int) or c >= 1:
                    v.wait_ge(s["y"], c)
                v.tensor_tensor(z_sum[:, :], z[:, 0, :], z[:, 1, :], ALU.add).then_inc(s["zsum"], 1)
                v.wait_ge(s["zsum"], c + 1)
                v.wait_ge(s["stats"], c + 1)
                v.scalar_tensor_tensor(out=acc[low, 0, span(c)], in0=p_wide[low, i, :],
                                       scalar=w.post_bias[:, 0:1], in1=z_sum[:, :],
                                       op0=ALU.add, op1=ALU.add).then_inc(s["y"], 1)

            v.memset(xt[D:, :, :], 1.0)
            v.memset(eps[:, :], EPS_STD).then_inc(s["eps"], 1)
            pipeline(v, (5, scale), (3, variance), (3, stats), (1, moments))


def batch_norm(chip, w, out_rows=None, out_chip=None, next_w=None, q_rows=None):
    nc = chip.nc
    x = chip.acc2[0:D, 0, 0:N]
    HALF = N // 2
    with ExitStack() as ctx:
        sb, ps, sem = chip.scope(ctx)
        total = sb("total", [D, 2])
        c = sb("c", [D, 6])
        scale = sb("scale", [D, 1])
        shift = sb("shift", [D, 1])
        xt = sb("xt", [D, 2, CH])
        stage = sb("stage", [P, 2, B, D])
        q_stage = sb("q_stage", [P, 2, B, D])
        p_x = ps("p_x", [P, 2, CH])
        p_q = ps("p_q", [P, 2, CH])
        s_v = sem("s_v")
        s_half = sem("s_half")
        s_mean = sem("s_mean")
        s_sd = sem("s_sd")
        s_sq = sem("s_sq")
        s_scale = sem("s_scale")
        s_x = sem("s_x")
        s_turn = sem("s_turn")
        s_stage = sem("s_stage")
        s_q = sem("s_q")
        s_q_stage = sem("s_q_stage")
        s_out = [sem(f"s_out{i}") for i in (0, 1)]
        s_q_out = [sem(f"s_q_out{i}") for i in (0, 1)]
        block = ctx.enter_context(nc.Block())

        @block.scalar
        def _(act):
            nc.scalar.activation(chip.acc2[0:D, 1, HALF:N], x[:, HALF:], ACT.Identity,
                                 accum_out=total[:, 1:2]).then_inc(s_half, 1)
            act.wait_ge(s_half, 1)
            act.wait_ge(s_mean, 1)
            nc.scalar.activation(chip.acc2[0:D, 1, 0:N], x, ACT.Square, bias=c[:, 1:2],
                                 accum_out=c[:, 2:3]).then_inc(s_sq, 1)
            act.wait_ge(s_sq, 1)
            nc.scalar.activation(c[:, 3:4], c[:, 2:3], ACT.Sqrt, bias=c[:, 5:6], scale=1.0 / N).then_inc(s_sd, 1)

            def normalise(c, i, n):
                reused(act, s_q if next_w else s_turn, c)
                nc.scalar.activation(xt[:, i, :], chip.acc2[0:D, 0, bass.ds(c * CH, CH)], ACT.Relu,
                                     bias=shift[:, 0:1], scale=scale[:, 0:1]).then_inc(s_x, 1)

            def q_to_rows(c, i, n):
                act.wait_ge(s_q, c + 1)
                stored(act, s_q_out[i], c, n)
                nc.scalar.copy(q_stage[:, i, :, :],
                               p_q[:, i, 0:B * D].rearrange("p (b f) -> p b f", b=B)).then_inc(s_q_stage, 1)

            act.wait_ge(s_scale, 1)
            pipeline(act, (0, normalise), *([(2, q_to_rows)] if next_w else []))

        @block.tensor
        def _(pe):
            def turn_back(c, i, n):
                pe.wait_ge(s_x, c + 1)
                reused(pe, s_stage, c)
                gate(pe)
                for b in range(B):
                    t = pe.transpose(p_x[:, i, b * D:(b + 1) * D], xt[:, i, b * P:(b + 1) * P],
                                     chip.ident[0:D, 0:D])
                t.then_inc(s_turn, 1)
                if next_w:
                    reused(pe, s_q_stage, c)
                    gate(pe)
                    for b in range(B):
                        m = pe.matmul(p_q[:, i, b * D:(b + 1) * D], xt[:, i, b * P:(b + 1) * P],
                                      next_w.source[:, :], start=True, stop=True)
                    m.then_inc(s_q, 1)

            pipeline(pe, (1, turn_back))

        @block.vector
        def _(v):
            v.memset(c[:, 5:6], EPS_BN)
            v.tensor_reduce(total[:, 0:1], x[:, 0:HALF], AX_X, ALU.add).then_inc(s_v, 1)
            v.wait_ge(s_v, 1)
            v.wait_ge(s_half, 1)
            v.tensor_tensor(c[:, 0:1], total[:, 0:1], total[:, 1:2], ALU.add).then_inc(s_v, 1)
            v.wait_ge(s_v, 2)
            v.tensor_scalar(c[:, 1:2], c[:, 0:1], -1.0 / N, None, ALU.mult).then_inc(s_mean, 1)
            v.wait_ge(s_sd, 1)
            v.reciprocal(c[:, 4:5], c[:, 3:4]).then_inc(s_v, 1)
            v.wait_ge(s_v, 3)
            v.tensor_tensor(scale[:, :], c[:, 4:5], w.gamma[:, :], ALU.mult).then_inc(s_v, 1)
            v.wait_ge(s_v, 4)
            v.scalar_tensor_tensor(out=shift[:, :], in0=scale[:, :], scalar=c[:, 1:2], in1=w.beta[:, :],
                                   op0=ALU.mult, op1=ALU.add).then_inc(s_scale, 1)

            def to_rows(c, i, n):
                v.wait_ge(s_turn, c + 1)
                if out_chip is None:
                    stored(v, s_out[i], c, n)
                    to = stage[:, i, :, :]
                else:
                    gate(v)
                    to = out_chip[:, bass.ds(c * B, B), :]
                v.tensor_copy(to, p_x[:, i, 0:B * D].rearrange("p (b f) -> p b f", b=B)).then_inc(s_stage, 1)

            pipeline(v, (2, to_rows))

        @block.sync
        def _(sp):
            def store(c, i, n):
                if out_chip is None:
                    sp.wait_ge(s_stage, c + 1)
                    gate(sp)
                    sp.dma_start(rows_of(out_rows, c), stage[:, i]).then_inc(s_out[i], 16)
                if next_w:
                    sp.wait_ge(s_q_stage, c + 1)
                    gate(sp)
                    sp.dma_start(rows_of(q_rows, c), q_stage[:, i]).then_inc(s_q_out[i], 16)

            if out_chip is None:
                pipeline(sp, (3, store))
                for i in (0, 1):
                    sp.wait_ge(s_out[i], final_count(i))
                    if next_w:
                        sp.wait_ge(s_q_out[i], final_count(i))


def gnn(nc, x_pad, src_pad, dst_pad, ea_pad, ea_t, W1, b1, W2, b2, W3, b3, We, be, Wp, bp, Wo, bo, Wl, bl,
        bn_g, bn_b, out):
    chip = Chip(nc)
    flags = nc.dram_tensor("flags", [EP], BF16, kind="Internal").ap()
    rows = nc.dram_tensor("node_rows", [5, NP], F32, kind="Internal").ap()
    h1 = nc.dram_tensor("h1_rows", [BLOCKS * P, D], F32, kind="Internal").ap()
    h2 = nc.dram_tensor("h2_rows", [BLOCKS * P, D], F32, kind="Internal").ap()
    x1 = nc.dram_tensor("x1_rows", [NP, D], F32, kind="Internal").ap()
    x2 = nc.dram_tensor("x2_rows", [NP, D], F32, kind="Internal").ap()
    q_rows = nc.dram_tensor("q_rows", [NP, D], F32, kind="Internal").ap()
    with ExitStack() as ctx:
        sb, ps, sem = chip.scope(ctx)
        chip.ramp = sb("ramp", [P, P])
        chip.shifts = sb("shifts", [P, NP // P])
        chip.ident = sb("ident", [P, P])
        chip.dst = sb("dst", [P, NG + 1, G])
        chip.last = sb("last", [P, NG + 1, G])
        chip.regs = sb("regs", [1, 3, NG + 1], I32)
        chip.blocks = sb("blocks", [1, TURNS + 2], I32)
        ws = [PnaWeights(chip.scope(ctx)[0]) for _ in range(LAYERS)]
        prepare(chip, dst_pad, flags, ws, (We, be, Wp, bp, Wo, bo, Wl, bl, bn_g, bn_b))
        with ExitStack() as l0:
            sb, ps, sem = chip.scope(l0)
            chip.acc = sb("acc", [P, NP])
            chip.h = sb("h", [P, NP // P, D])
            conv_pass(chip, x_pad, src_pad, ea_pad, W1, b1, h1, True, first=True)
            conv_pass(chip, h1, src_pad, ea_pad, W2, b2, h2, True, degree_rows=rows)
            conv_pass(chip, h2, src_pad, ea_pad, W3, b3, None, False)
            residual_norm(chip, chip.h, x_pad, x1, ws[0], q_rows)
        with ExitStack() as l1:
            sb, ps, sem = chip.scope(l1)
            chip.acc2 = sb("acc2", [P, 2, NP])
            pna_pass(chip, ws[0], q_rows, src_pad, ea_t, flags)
            pna_nodes(chip, ws[0], x1, rows)
            batch_norm(chip, ws[0], out_rows=x2, next_w=ws[1], q_rows=q_rows)
            pna_pass(chip, ws[1], q_rows, src_pad, ea_t, flags)
            pna_nodes(chip, ws[1], x2, rows)
            x3 = sb("x3", [P, NP // P, D])
            batch_norm(chip, ws[1], out_chip=x3)
            residual_norm(chip, x3, x1, out)


_NAMES = ["L0_gnn_W1", "L0_gnn_b1", "L0_gnn_W2", "L0_gnn_b2", "L0_gnn_W3", "L0_gnn_b3",
          "L1_gnn_W_edge", "L1_gnn_b_edge", "L1_gnn_W_pre", "L1_gnn_b_pre", "L1_gnn_W_post",
          "L1_gnn_b_post", "L1_gnn_W_lin", "L1_gnn_b_lin", "L1_gnn_bn_gamma", "L1_gnn_bn_beta"]


def kernel(**inputs):
    import numpy as _np
    import concourse.bacc as _bacc
    from concourse import mybir as _mybir
    from concourse.bass_utils import run_bass_kernel_spmd as _run

    nc = _bacc.Bacc("TRN2", target_bir_lowering=False, num_devices=1)
    x = _np.asarray(inputs["x"])
    ea = _np.asarray(inputs["edge_attr_16"])
    src = _np.asarray(inputs["src"])
    dst = _np.asarray(inputs["dst"])
    arrays_in = {
        "x_pad": _np.concatenate([x, _np.zeros((NP - N, D), x.dtype)]),
        "src_pad": _np.concatenate([src, _np.zeros((EP - E,), src.dtype)]),
        "dst_pad": _np.concatenate([_np.full((1,), -1, dst.dtype), dst, _np.full((EP - E,), N, dst.dtype),
                                    _np.full((1,), N + 1, dst.dtype)]),
        "ea_pad": _np.concatenate([ea, _np.zeros((EP - E, FE), ea.dtype)]),
    }
    arrays_in["ea_t"] = _np.ascontiguousarray(arrays_in["ea_pad"].T)
    for name in _NAMES:
        arrays_in[name] = _np.ascontiguousarray(inputs[name])
    arrays, args = {}, []
    for name, a in arrays_in.items():
        arrays[f"in_{name}"] = a
        args.append(nc.dram_tensor(f"in_{name}", a.shape, _mybir.dt.from_np(a.dtype), kind="ExternalInput").ap())
    args.append(nc.dram_tensor("out_0", (NP, D), _mybir.dt.float32, kind="ExternalOutput").ap())
    gnn(nc, *args)
    r = _run(nc, [arrays], core_ids=[0])
    return r.results[0]["out_0"][:N]
```
